# Optimizing a Trainium2 kernel written in Bass

```python
import numpy as np
import jax
import jax.numpy as jnp

def _softmax(x, axis=-1):
    return jax.nn.softmax(x, axis=axis)

def _gelu(x):
    return jax.nn.gelu(x, approximate=True)

def _silu(x):
    return jax.nn.silu(x)

def _sigmoid(x):
    return jax.nn.sigmoid(x)

def _layernorm(x, axis=-1, eps=1e-05):
    m = jnp.mean(x, axis=axis, keepdims=True)
    v = jnp.var(x, axis=axis, keepdims=True)
    return (x - m) / jnp.sqrt(v + eps)

def _scatter_add(tgt, idx, src, axis=0):
    return tgt.at[idx].add(src)

def _segment_sum(src, seg, n):
    return jax.ops.segment_sum(src, seg, n)
kernel_name = 'mk_gnn_preln_d4_gnn_r64_de80da'

def setup_inputs(seed: int=0):
    np.random.seed(seed)
    _w = jnp.asarray

    def _rec_inputs():
        import jax
        import jax.numpy as jnp
        _gk = jax.random.key(seed)
        x = -0.0003713 + 1 * jax.random.normal(jax.random.fold_in(_gk, 1), (100000, 128), jnp.float32)
        src = jax.random.randint(jax.random.fold_in(_gk, 2), (50000,), 0, 100000, jnp.int32)
        dst = jax.random.randint(jax.random.fold_in(_gk, 3), (50000,), 0, 100000, jnp.int32)
        _o = jnp.argsort(dst, stable=True)
        src = src[_o]
        dst = dst[_o]
        edge_attr_20 = -9.88767e-05 + 0.999954 * jax.random.normal(jax.random.fold_in(_gk, 12), (50000, 20), jnp.float32)
        edge_weight = jax.random.uniform(jax.random.fold_in(_gk, 14), (50000,), jnp.float32, 0.0, 0.999998)
        return (x, src, dst, edge_attr_20, edge_weight)
    x, src, dst, edge_attr_20, edge_weight = _rec_inputs()

    def _L0_gnn_setup():
        import jax, jax.numpy as jnp
        import numpy as np
        N_NODES = 100000
        N_EDGES = 25000
        D_IN = 128
        HIDDEN = [128, 128]

        def _xavier(key, shape):
            fan_out, fan_in = shape
            a = np.sqrt(6.0 / (fan_in + fan_out)).astype(np.float32)
            return jax.random.uniform(key, shape, jnp.float32, -a, a)

        def _mean_aggregate(x, src, dst, n_nodes):
            summed = jax.ops.segment_sum(x[src], dst, num_segments=n_nodes)
            cnt = jax.ops.segment_sum(jnp.ones((src.shape[0],), x.dtype), dst, num_segments=n_nodes)
            return summed / jnp.maximum(cnt, 1.0)[:, None]
        key = jax.random.key(seed)
        ks = jax.random.split(key, 6)
        x = jax.random.normal(ks[0], (N_NODES, D_IN), jnp.float32)
        edge_index = jax.random.randint(ks[1], (2, N_EDGES), 0, N_NODES, dtype=jnp.int64)
        W_conv0 = _xavier(ks[2], (HIDDEN[0], D_IN))
        b_conv0 = jnp.zeros((HIDDEN[0],), jnp.float32)
        W_lin0 = _xavier(ks[3], (HIDDEN[0], D_IN))
        b_lin0 = jnp.zeros((HIDDEN[0],), jnp.float32)
        W_conv1 = _xavier(ks[4], (HIDDEN[1], HIDDEN[0]))
        b_conv1 = jnp.zeros((HIDDEN[1],), jnp.float32)
        W_lin1 = _xavier(ks[5], (HIDDEN[1], HIDDEN[0]))
        b_lin1 = jnp.zeros((HIDDEN[1],), jnp.float32)
        return {'x': x, 'edge_index': edge_index, 'W_conv0': W_conv0, 'b_conv0': b_conv0, 'W_lin0': W_lin0, 'b_lin0': b_lin0, 'W_conv1': W_conv1, 'b_conv1': b_conv1, 'W_lin1': W_lin1, 'b_lin1': b_lin1}
    _L0_gnn_all = _L0_gnn_setup()
    _L0_gnn_in = {k: v for k, v in _L0_gnn_all.items() if k in ('W_conv0', 'b_conv0', 'W_lin0', 'b_lin0', 'W_conv1', 'b_conv1', 'W_lin1', 'b_lin1')}
    del _L0_gnn_all

    def _L1_gnn_setup():
        import jax, jax.numpy as jnp
        import numpy as np
        LOG2 = 0.6931471805599453

        def shifted_softplus(x):
            return jax.nn.softplus(x) - LOG2
        N_ATOMS = 20000
        N_EDGES = 9375
        N_BASIS = 128
        N_RBF = 20
        N_FILT = 128
        key = jax.random.key(seed)
        ks = jax.random.split(key, 12)
        s = lambda k, sh, fan_in: jax.random.normal(k, sh, jnp.float32) / np.sqrt(fan_in)
        return {'x': jax.random.normal(ks[0], (N_ATOMS, N_BASIS), jnp.float32), 'f_ij': jax.random.normal(ks[1], (N_EDGES, N_RBF), jnp.float32), 'idx_i': jax.random.randint(ks[2], (N_EDGES,), 0, N_ATOMS), 'idx_j': jax.random.randint(ks[3], (N_EDGES,), 0, N_ATOMS), 'rcut_ij': jax.random.uniform(ks[4], (N_EDGES,), jnp.float32), 'W_in2f': s(ks[5], (N_FILT, N_BASIS), N_BASIS), 'b_in2f': jnp.zeros((N_FILT,), jnp.float32), 'W_f1': s(ks[6], (N_FILT, N_RBF), N_RBF), 'b_f1': jnp.zeros((N_FILT,), jnp.float32), 'W_f2': s(ks[7], (N_FILT, N_FILT), N_FILT), 'b_f2': jnp.zeros((N_FILT,), jnp.float32), 'W_o1': s(ks[8], (N_BASIS, N_FILT), N_FILT), 'b_o1': jnp.zeros((N_BASIS,), jnp.float32), 'W_o2': s(ks[9], (N_BASIS, N_BASIS), N_BASIS), 'b_o2': jnp.zeros((N_BASIS,), jnp.float32)}
    _L1_gnn_all = _L1_gnn_setup()
    _L1_gnn_in = {k: v for k, v in _L1_gnn_all.items() if k in ('W_in2f', 'b_in2f', 'W_f1', 'b_f1', 'W_f2', 'b_f2', 'W_o1', 'b_o1', 'W_o2', 'b_o2')}
    del _L1_gnn_all

    def _L2_gnn_setup():
        import jax, jax.numpy as jnp
        import numpy as np
        N_NODES = 100000
        N_EDGES = 10000
        DIM = 128
        key = jax.random.key(seed)
        k1, k2, k3, k4, k5 = jax.random.split(key, 5)
        x = jax.random.normal(k1, (N_NODES, DIM), dtype=jnp.float32)
        edge_index = jax.random.randint(k2, (2, N_EDGES), 0, N_NODES, dtype=jnp.int64)
        edge_weight = jax.random.uniform(k3, (N_EDGES,), dtype=jnp.float32)
        W = jax.random.normal(k4, (DIM, DIM), dtype=jnp.float32) * (1.0 / np.sqrt(DIM))
        b = jax.random.normal(k5, (DIM,), dtype=jnp.float32) * 0.01
        return {'x': x, 'edge_index': edge_index, 'edge_weight': edge_weight, 'W': W, 'b': b}
    _L2_gnn_all = _L2_gnn_setup()
    _L2_gnn_in = {k: v for k, v in _L2_gnn_all.items() if k in ('W', 'b')}
    del _L2_gnn_all

    def _L3_gnn_setup():
        import jax, jax.numpy as jnp
        import numpy as np
        N_NODES = 100000
        EMB_DIM = 128
        N_EDGES = 25000
        key = jax.random.key(seed)
        k1, k2 = jax.random.split(key)
        edge_index = jax.random.randint(k1, (2, N_EDGES), 0, N_NODES, dtype=jnp.int64 if jax.config.read('jax_enable_x64') else jnp.int32)
        embedding = jax.random.normal(k2, (N_NODES, EMB_DIM), dtype=jnp.float32)
        return {'edge_index': edge_index, 'embedding': embedding}
    _L3_gnn_all = _L3_gnn_setup()
    _L3_gnn_in = {k: v for k, v in _L3_gnn_all.items() if k in ()}
    del _L3_gnn_all
    return {'x': x, 'src': src, 'dst': dst, 'edge_attr_20': edge_attr_20, 'edge_weight': edge_weight, 'L0_gnn_W_conv0': _L0_gnn_in['W_conv0'], 'L0_gnn_b_conv0': _L0_gnn_in['b_conv0'], 'L0_gnn_W_lin0': _L0_gnn_in['W_lin0'], 'L0_gnn_b_lin0': _L0_gnn_in['b_lin0'], 'L0_gnn_W_conv1': _L0_gnn_in['W_conv1'], 'L0_gnn_b_conv1': _L0_gnn_in['b_conv1'], 'L0_gnn_W_lin1': _L0_gnn_in['W_lin1'], 'L0_gnn_b_lin1': _L0_gnn_in['b_lin1'], 'L1_gnn_W_in2f': _L1_gnn_in['W_in2f'], 'L1_gnn_b_in2f': _L1_gnn_in['b_in2f'], 'L1_gnn_W_f1': _L1_gnn_in['W_f1'], 'L1_gnn_b_f1': _L1_gnn_in['b_f1'], 'L1_gnn_W_f2': _L1_gnn_in['W_f2'], 'L1_gnn_b_f2': _L1_gnn_in['b_f2'], 'L1_gnn_W_o1': _L1_gnn_in['W_o1'], 'L1_gnn_b_o1': _L1_gnn_in['b_o1'], 'L1_gnn_W_o2': _L1_gnn_in['W_o2'], 'L1_gnn_b_o2': _L1_gnn_in['b_o2'], 'L2_gnn_W': _L2_gnn_in['W'], 'L2_gnn_b': _L2_gnn_in['b']}

def reference(x, src, dst, edge_attr_20, edge_weight, L0_gnn_W_conv0, L0_gnn_b_conv0, L0_gnn_W_lin0, L0_gnn_b_lin0, L0_gnn_W_conv1, L0_gnn_b_conv1, L0_gnn_W_lin1, L0_gnn_b_lin1, L1_gnn_W_in2f, L1_gnn_b_in2f, L1_gnn_W_f1, L1_gnn_b_f1, L1_gnn_W_f2, L1_gnn_b_f2, L1_gnn_W_o1, L1_gnn_b_o1, L1_gnn_W_o2, L1_gnn_b_o2, L2_gnn_W, L2_gnn_b):
    import jax
    import jax.numpy as jnp

    def _L0_gnn_ref(x, edge_index, W_conv0, b_conv0, W_lin0, b_lin0, W_conv1, b_conv1, W_lin1, b_lin1):
        import jax, jax.numpy as jnp
        import numpy as np
        N_NODES = 100000
        N_EDGES = 25000
        D_IN = 128
        HIDDEN = [128, 128]

        def _xavier(key, shape):
            fan_out, fan_in = shape
            a = np.sqrt(6.0 / (fan_in + fan_out)).astype(np.float32)
            return jax.random.uniform(key, shape, jnp.float32, -a, a)

        def _mean_aggregate(x, src, dst, n_nodes):
            summed = jax.ops.segment_sum(x[src], dst, num_segments=n_nodes)
            cnt = jax.ops.segment_sum(jnp.ones((src.shape[0],), x.dtype), dst, num_segments=n_nodes)
            return summed / jnp.maximum(cnt, 1.0)[:, None]
        src, dst = (edge_index[0], edge_index[1])
        n = x.shape[0]
        layers = [(W_conv0, b_conv0, W_lin0, b_lin0), (W_conv1, b_conv1, W_lin1, b_lin1)]
        n_convs = len(layers)
        for i, (Wc, bc, Wl, bl) in enumerate(layers):
            agg = _mean_aggregate(x, src, dst, n)
            h = jnp.einsum('nd,od->no', agg, Wc) + bc
            x = jnp.einsum('nd,od->no', x, Wl) + bl + h
            if i != n_convs - 1:
                x = jax.nn.relu(x)
        return x

    def _L1_gnn_ref(x, f_ij, idx_i, idx_j, rcut_ij, W_in2f, b_in2f, W_f1, b_f1, W_f2, b_f2, W_o1, b_o1, W_o2, b_o2):
        import jax, jax.numpy as jnp
        import numpy as np
        LOG2 = 0.6931471805599453

        def shifted_softplus(x):
            return jax.nn.softplus(x) - LOG2
        N_ATOMS = 20000
        N_EDGES = 9375
        N_BASIS = 128
        N_RBF = 20
        N_FILT = 128
        n_atoms = x.shape[0]
        h = x @ W_in2f.T + b_in2f
        Wij = shifted_softplus(f_ij @ W_f1.T + b_f1)
        Wij = Wij @ W_f2.T + b_f2
        Wij = Wij * rcut_ij[:, None]
        x_ij = h[idx_j] * Wij
        agg = jax.ops.segment_sum(x_ij, idx_i, num_segments=n_atoms)
        out = shifted_softplus(agg @ W_o1.T + b_o1)
        out = out @ W_o2.T + b_o2
        return out

    def _L2_gnn_ref(x, edge_index, edge_weight, W, b):
        import jax, jax.numpy as jnp
        import numpy as np
        N_NODES = 100000
        N_EDGES = 10000
        DIM = 128
        row, col = (edge_index[0], edge_index[1])
        msgs = edge_weight[:, None] * x[row]
        agg = jax.ops.segment_sum(msgs, col, num_segments=x.shape[0])
        return agg @ W.T + b

    def _L3_gnn_ref(edge_index, embedding):
        import jax, jax.numpy as jnp
        import numpy as np
        N_NODES = 100000
        EMB_DIM = 128
        N_EDGES = 25000
        N = embedding.shape[0]
        loop = jnp.arange(N, dtype=edge_index.dtype)
        row = jnp.concatenate([edge_index[0], loop])
        col = jnp.concatenate([edge_index[1], loop])
        deg = jax.ops.segment_sum(jnp.ones_like(row, dtype=embedding.dtype), row, num_segments=N)
        deg_inv_sqrt = jnp.where(deg > 0, jax.lax.rsqrt(jnp.maximum(deg, 1.0)), 0.0)
        norm = deg_inv_sqrt[row] * deg_inv_sqrt[col]
        msgs = norm[:, None] * embedding[row]
        out = jax.ops.segment_sum(msgs, col, num_segments=N)
        return out
    edge_index = jnp.stack([src, dst])
    h = jnp.maximum(_layernorm(x, axis=-1), 0.0)
    x = x + _L0_gnn_ref(h, edge_index, L0_gnn_W_conv0, L0_gnn_b_conv0, L0_gnn_W_lin0, L0_gnn_b_lin0, L0_gnn_W_conv1, L0_gnn_b_conv1, L0_gnn_W_lin1, L0_gnn_b_lin1)
    h = jnp.maximum(_layernorm(x, axis=-1), 0.0)
    x = x + _L1_gnn_ref(h, edge_attr_20, src, dst, edge_weight, L1_gnn_W_in2f, L1_gnn_b_in2f, L1_gnn_W_f1, L1_gnn_b_f1, L1_gnn_W_f2, L1_gnn_b_f2, L1_gnn_W_o1, L1_gnn_b_o1, L1_gnn_W_o2, L1_gnn_b_o2)
    h = jnp.maximum(_layernorm(x, axis=-1), 0.0)
    x = x + _L2_gnn_ref(h, edge_index, edge_weight, L2_gnn_W, L2_gnn_b)
    h = jnp.maximum(_layernorm(x, axis=-1), 0.0)
    x = x + _L3_gnn_ref(edge_index, h)
    return x

_drawn_inputs = setup_inputs


def setup_inputs(seed=0):
    import zlib

    import numpy as np

    out = dict(_drawn_inputs(seed))
    spreads = {'L0_gnn_b_conv0': (0.0, 0.1),
     'L0_gnn_b_lin0': (0.0, 0.1),
     'L0_gnn_b_conv1': (0.0, 0.1),
     'L0_gnn_b_lin1': (0.0, 0.1),
     'L1_gnn_b_in2f': (0.0, 0.76),
     'L1_gnn_b_f1': (0.0, 0.8),
     'L1_gnn_b_f2': (0.0, 0.604),
     'L1_gnn_b_o1': (0.0, 0.1),
     'L1_gnn_b_o2': (0.0, 0.1)}
    factors = {'L2_gnn_b': 6.43}
    for name, (base, spread) in spreads.items():
        noise = np.random.default_rng([zlib.crc32(name.encode()), seed]).standard_normal(out[name].shape)
        drawn = base * np.exp(spread * noise) if base else spread * noise
        out[name] = jnp.asarray(drawn.astype(out[name].dtype))
    for name, factor in factors.items():
        out[name] = (out[name] * factor).astype(out[name].dtype)
    return out
```

```python
from contextlib import ExitStack, contextmanager

import numpy as np

import concourse.bass as bass
from concourse import mybir

FP32, I32 = mybir.dt.float32, mybir.dt.int32
ALU, ACT, AX = mybir.AluOpType, mybir.ActivationFunctionType, mybir.AxisListType

P = 128
N, D = 100000, 128
E, R = 50000, 20
W = D + 4
AUX = D
J = 5
G = P * J
NG, NT = divmod(N, G)
EG, ET = divmod(E, G)
NTP, ETP = NT // J, ET // J
EPS = 1e-5
LOG2 = 0.6931471805599453


class Chain:

    def __init__(self, eng, sem, per_round):
        self.eng, self.sem, self.per_round, self.base, self.k = eng, sem, per_round, 0, 0

    def round(self, i):
        self.base, self.k = i * self.per_round, 0

    def __call__(self, ins):
        ins.then_inc(self.sem, 1)
        self.k += 1
        self.eng.wait_ge(self.sem, self.base + self.k)

    def end(self):
        assert self.k == self.per_round, (self.k, self.per_round)


def take(eng, sem, n):
    eng.wait_ge(sem, n)
    eng.nop().then_inc(sem, -n)


def moments(v, k, link):
    half = lambda n: k.stats[:, :, n]
    link(v.tensor_tensor(k.mean[:, :], half(1), half(4), ALU.add))
    link(v.tensor_tensor(k.gap[:, :], half(1), half(4), ALU.subtract))
    link(v.tensor_tensor(k.gap[:, :], k.gap[:, :], k.gap[:, :], ALU.mult))
    link(v.tensor_tensor(k.var[:, :], half(2), half(5), ALU.add))


def group_rows(ap, i, parts=P):
    return ap[bass.ds(i * G, parts * J), :].rearrange("(p j) w -> p j w", j=J)


class Kernel:
    def __init__(self, nc, ctx):
        self.nc, self.ctx = nc, ctx

    def sb(self, name, shape, dt=FP32):
        return self.ctx.enter_context(self.nc.sbuf_tensor(name, shape, dt))

    def ps(self, name, shape):
        return self.ctx.enter_context(self.nc.psum_tensor(name, shape, FP32))

    def sem(self, name):
        self.sems.append(self.pass_ctx.enter_context(self.nc.semaphore(name)))
        return self.sems[-1]

    def lasting_sem(self, name):
        return self.ctx.enter_context(self.nc.semaphore(name))

    @contextmanager
    def one_pass(self):
        self.sems = []
        with ExitStack() as self.pass_ctx:
            yield
            with self.nc.Block() as block:
                @block.gpsimd
                def _(pool):
                    for s in self.sems:
                        pool.sem_clear(s)


def load_constants(k, a):
    nc = k.nc
    mats = ["L0_gnn_W_conv0", "L0_gnn_W_lin0", "L0_gnn_W_conv1", "L0_gnn_W_lin1", "L1_gnn_W_in2f",
            "L1_gnn_W_f2", "L1_gnn_W_o1", "L1_gnn_W_o2", "L2_gnn_W"]
    rows = ["L0_gnn_b_conv0", "L0_gnn_b_lin0", "L0_gnn_b_conv1", "L0_gnn_b_lin1", "L1_gnn_b_in2f",
            "L1_gnn_b_f2", "L1_gnn_b_o1", "L1_gnn_b_o2", "L2_gnn_b"]
    k.ident, k.tri = k.sb("ident", [P, P]), k.sb("tri", [P, P])
    k.spare_i, k.spare = k.sb("spare_i", [P, 1], I32), k.sb("spare", [P, 1])
    k.eps, k.turn = k.sb("eps", [P, 1]), k.sb("turn", [P, 1])
    k.zeros = k.sb("zeros", [P, J, W])
    k.wt, k.bias = k.sb("wt", [P, len(mats), P]), k.sb("bias", [P, len(rows) + 2, D])
    k.raw = k.sb("raw", [P, len(mats), P])
    k.f1, k.f1_t = k.sb("f1", [P, R]), k.sb("f1_t", [R, P])
    k.f1_bias = k.sb("f1_bias", [P, 1])
    k.o1_bias = k.sb("o1_bias", [P, 1])
    s_const, s_load, s_pe, s_sum = k.sem("s_const"), k.sem("s_load"), k.sem("s_pe"), k.sem("s_sum")
    psw = k.ps_a
    k.W = {m: k.wt[:, n, :] for n, m in enumerate(mats)}
    k.B = {m: k.bias[:, n, :] for n, m in enumerate(rows)}
    k.B["L0_0"], k.B["L0_1"] = k.bias[:, len(rows), :], k.bias[:, len(rows) + 1, :]
    n_mats = len(mats)

    with nc.Block() as block:
        @block.sync
        def _(sp):
            for n, m in enumerate(mats):
                sp.dma_start(k.raw[:, n, :], a[m]).then_inc(s_load, 16)
            for n, m in enumerate(rows):
                sp.dma_start(k.bias[:, n, :], a[m].rearrange("(o n) -> o n", o=1).to_broadcast([P, D])).then_inc(s_load, 16)
            sp.dma_start(k.f1[:, :], a["L1_gnn_W_f1"]).then_inc(s_load, 16)
            sp.dma_start(k.f1_bias[:, :], a["L1_gnn_b_f1"].rearrange("(n o) -> n o", o=1)).then_inc(s_load, 16)
            sp.dma_start(k.o1_bias[:, :], a["L1_gnn_b_o1"].rearrange("(n o) -> n o", o=1)).then_inc(s_load, 16)

        @block.gpsimd
        def _(pool):
            pool.memset(k.ident[:, :], 0.0).then_inc(s_const, 1)
            pool.memset(k.tri[:, :], 1.0).then_inc(s_const, 1)
            pool.memset(k.eps[:, :], EPS)
            pool.memset(k.zeros[:, :, :], 0.0)
            pool.iota(k.spare_i[:, :], [[0, 1]], base=N, channel_multiplier=1).then_inc(s_const, 1)
            pool.wait_ge(s_const, 3)
            pool.affine_select(out=k.ident[:, :], in_=k.ident[:, :], compare_op=ALU.not_equal, fill=1.0,
                               base=0, pattern=[[-1, P]], channel_multiplier=1).then_inc(s_const, 1)
            pool.affine_select(out=k.tri[:, :], in_=k.tri[:, :], compare_op=ALU.is_gt, fill=0.0,
                               base=0, pattern=[[-1, P]], channel_multiplier=1).then_inc(s_const, 1)
            pool.tensor_copy(k.spare[:, :], k.spare_i[:, :]).then_inc(s_const, 1)

        @block.tensor
        def _(pe):
            pe.wait_ge(s_const, 6)
            pe.wait_ge(s_load, 16 * (len(mats) + len(rows) + 3))
            for n in range(n_mats):
                if n:
                    pe.wait_ge(s_sum, n)
                nc.tensor.transpose(psw[:, 0, :], k.raw[:, n, :], k.ident[:, :]).then_inc(s_pe, 1)
            pe.wait_ge(s_sum, n_mats)
            nc.tensor.transpose(psw[0:R, 0, :], k.f1[:, :], k.ident[:, :]).then_inc(s_pe, 1)

        @block.vector
        def _(dve):
            for n in range(n_mats):
                dve.wait_ge(s_pe, n + 1)
                nc.vector.tensor_copy(k.wt[:, n, :], psw[:, 0, :]).then_inc(s_sum, 1)
            dve.wait_ge(s_pe, n_mats + 1)
            nc.vector.tensor_copy(k.f1_t[:, :], psw[0:R, 0, :]).then_inc(s_sum, 1)
            dve.wait_ge(s_load, 16 * (len(mats) + len(rows) + 3))
            for n in (0, 1):
                nc.vector.tensor_tensor(k.B[f"L0_{n}"], k.B[f"L0_gnn_b_conv{n}"], k.B[f"L0_gnn_b_lin{n}"],
                                        ALU.add).then_inc(s_sum, 1)
            dve.wait_ge(s_sum, n_mats + 3)


def clear_tables(k, tables):
    s_cleared = k.sem("s_cleared")
    n = 0
    with k.nc.Block() as block:
        @block.sync
        def _(sp):
            with sp.Fori(0, NG) as i:
                for t in tables:
                    sp.dma_start(group_rows(t, i), k.zeros[:, :, :]).then_inc(s_cleared, 16)
            for t in tables:
                rest = N + P - NG * G
                sp.dma_start(t[NG * G:N + P, :].rearrange("(p j) w -> p j w", j=3), k.zeros[0:rest // 3, 0:3, :]).then_inc(s_cleared, 16)
            sp.wait_ge(s_cleared, 16 * len(tables) * (NG + 1))


def edge_pass(k, a, name, mode, table, sums, gather_by, add_by):
    nc = k.nc
    ln, filt, weighted, from_row = mode in ("h", "filter", "weight", "degree"), mode == "filter", mode == "weight", mode == "degree"
    width = D if mode == "h" else W
    s_idx, s_gidx, s_key, s_turn = (k.sem(f"{name}_{x}") for x in ("idx", "gidx", "key", "turn"))
    s_got, s_add = k.lasting_sem(f"{name}_got"), k.lasting_sem(f"{name}_add")
    s_chain, s_stat, s_std, s_norm = k.sem(f"{name}_chain"), k.sem(f"{name}_stat"), k.sem(f"{name}_std"), k.sem(f"{name}_norm")
    s_msg, s_sum, s_out, s_hid = k.sem(f"{name}_msg"), k.sem(f"{name}_sum"), k.sem(f"{name}_out"), k.sem(f"{name}_hid")
    s_act, s_tp, s_tpc, s_f1, s_ssp, s_fw = (k.sem(f"{name}_{x}") for x in ("act", "tp", "tpc", "f1", "ssp", "fw"))
    s_free = k.sem(f"{name}_free")
    s_preset, s_hid2 = k.sem(f"{name}_preset"), k.sem(f"{name}_hid2")
    loads = 2 + (weighted or filt) + filt
    gather_ap, key_ap = a[gather_by], a[add_by]
    sum_of = lambda j: k.ps_sum[:, j // 3, j % 3 * W:(j % 3 + 1) * W]

    def every_group(eng, body):
        with eng.Fori(0, EG) as i:
            body(i, False)
        body(EG, True)

    with nc.Block() as block:
        @block.sync
        def _(sp):
            def body(i, tail):
                parts = ETP if tail else P
                sp.wait_ge(s_free, i + 1)
                if tail:
                    sp.wait_ge(s_preset, 1)
                col = lambda ap: ap[bass.ds(i * G, parts * J)].rearrange("(p j) -> p j", j=J)
                sp.dma_start(k.gidx[0:parts, :], col(gather_ap)).then_inc(s_gidx, 16)
                sp.dma_start(k.kidx[0:parts, :], col(key_ap)).then_inc(s_idx, 16)
                sp.dma_start(k.krow[:, 0:parts * J], key_ap[bass.ds(i * G, parts * J)].rearrange("(o n) -> o n", o=1)
                             .to_broadcast([P, parts * J])).then_inc(s_idx, 16)
                if weighted or filt:
                    sp.dma_start(k.wcol[0:parts, :], col(a["edge_weight"])).then_inc(s_idx, 16)
                if filt:
                    sp.dma_start(k.rbf[0:parts, :, :], group_rows(a["edge_attr_20"], i, parts)).then_inc(s_idx, 16)
            sp.nop().then_inc(s_free, 1)
            every_group(sp, body)

        @block.gpsimd
        def _(pool):
            def body(i, tail):
                take(pool, s_gidx, 16)
                for j in range(J):
                    pool.indirect_dma_start(out=k.rows[:, j, 0:width], out_offset=None, in_=table,
                                            in_offset=bass.IndirectOffsetOnAxis(ap=k.gidx[:, j:j + 1], axis=0)).then_inc(s_got, 16)
                take(pool, s_key, 1)
                for j in range(J):
                    take(pool, s_out, 1)
                    pool.indirect_dma_start(out=sums, out_offset=bass.IndirectOffsetOnAxis(ap=k.sidx[:, j:j + 1], axis=0),
                                            in_=k.summed[:, j, :], in_offset=None, compute_op=ALU.add).then_inc(s_add, 16)
                    pool.wait_ge(s_add, 16 * (i * J + j + 1))
                    pool.tensor_tensor(k.turn[:, :], k.spare[:, :], k.spare[:, :], ALU.add).then_inc(s_turn, 1)
                    take(pool, s_turn, 1)
                pool.nop().then_inc(s_free, 1)
            every_group(pool, body)

        @block.vector
        def _(dve):
            link = Chain(dve, s_chain, 2 * J + 5 + J * (weighted or from_row) + (2 * J + 7) * ln + 5 * filt)
            v = nc.vector

            def body(i, tail):
                link.round(i)
                if tail:
                    dve.wait_ge(s_free, i + 1)
                    v.memset(k.krow[:, :], -1)
                    v.tensor_copy(k.kidx[:, :], k.spare_i[:, :].to_broadcast([P, J])).then_inc(s_preset, 1)
                    dve.wait_ge(s_preset, 1)
                dve.wait_ge(s_idx, 16 * loads * (i + 1))
                link(v.tensor_copy(k.kcol[:, :], k.kidx[:, :]))
                for j in range(J):
                    link(v.tensor_scalar(k.same[:, j, :], k.krow[:, j:G:J], k.kcol[:, j:j + 1], None, ALU.is_equal))
                for j in range(J):
                    link(v.tensor_tensor_reduce(out=k.junk[:, :], in0=k.same[:, j, :], in1=k.tri[:, :], scale=1.0, scalar=0.0,
                                                op0=ALU.mult, op1=ALU.add, accum_out=k.dup[:, j:j + 1]))
                link(v.tensor_scalar(k.dup[:, :], k.dup[:, :], 1.0, None, ALU.min))
                link(v.tensor_scalar(k.tgt[:, :], k.kcol[:, :], -1.0, k.spare[:, 0:1], ALU.mult, ALU.add))
                link(v.tensor_tensor(k.tgt[:, :], k.tgt[:, :], k.dup[:, :], ALU.mult))
                link(v.tensor_tensor(k.tgt[:, :], k.tgt[:, :], k.kcol[:, :], ALU.add))
                v.tensor_copy(k.sidx[:, :], k.tgt[:, :]).then_inc(s_key, 1)
                dve.wait_ge(s_got, 16 * J * (i + 1))
                if from_row:
                    wsrc = k.rows[:, :, AUX]
                elif weighted:
                    wsrc = k.wcol[:, :]
                if weighted or from_row:
                    for j in range(J):
                        link(v.tensor_scalar(k.same[:, j, :], k.same[:, j, :], wsrc[:, j:j + 1], None, ALU.mult))
                if not ln:
                    v.tensor_copy(k.msg[:, :, :], k.rows[:, :, :]).then_inc(s_msg, 1)
                else:
                    for j in range(J):
                        link(v.bn_stats(k.stats[:, j, :], k.rows[:, j, 0:D]))
                    moments(v, k, link)
                    v.scalar_tensor_tensor(k.var[:, :], k.gap[:, :], D / 4, k.var[:, :], ALU.mult, ALU.add).then_inc(s_stat, 1)
                    dve.wait_ge(s_std, i + 1)
                    link(v.reciprocal(k.rstd[:, :], k.std[:, :]))
                    link(v.scalar_tensor_tensor(k.mean[:, :], k.mean[:, :], -0.5, k.rstd[:, :], ALU.mult, ALU.mult))
                    for j in range(J):
                        link(v.tensor_scalar(k.rows[:, j, 0:D], k.rows[:, j, 0:D], k.rstd[:, j:j + 1], k.mean[:, j:j + 1], ALU.mult, ALU.add))
                if ln:
                    link(v.memset(k.msg[:, :, D:W], 1.0))
                if ln and not filt:
                    v.tensor_scalar(k.msg[:, :, 0:D], k.rows[:, :, 0:D], 0.0, None, ALU.max).then_inc(s_msg, 1)
                if filt:
                    v.tensor_scalar(k.rows[:, :, 0:D], k.rows[:, :, 0:D], 0.0, None, ALU.max).then_inc(s_norm, 1)
                    dve.wait_ge(s_tp, i + 1)
                    link(v.tensor_copy(k.h_t[:, :, :], k.ps_a[:, 0:J, :]))
                    v.tensor_copy(k.rbf_t[:, :, :], k.ps_b[0:R, 0:J, :]).then_inc(s_tpc, 1)
                    dve.wait_ge(s_f1, i + 1)
                    v.tensor_scalar(k.z[:, :, :], k.ps_a[:, 0:J, :], k.f1_bias[:, 0:1], None, ALU.add).then_inc(s_hid, 1)
                    dve.wait_ge(s_act, i + 1)
                    link(v.tensor_scalar(k.z[:, :, :], k.z[:, :, :], 0.0, -LOG2, ALU.max, ALU.add))
                    v.tensor_tensor(k.z[:, :, :], k.z[:, :, :], k.az[:, :, :], ALU.add).then_inc(s_ssp, 1)
                    dve.wait_ge(s_fw, i + 1)
                    link(v.tensor_tensor(k.fw[:, :, :], k.ps_c[:, 0:J, :], k.B["L1_gnn_b_f2"].unsqueeze(1).to_broadcast([P, J, D]), ALU.add))
                    link(v.tensor_tensor(k.fw[:, :, :], k.fw[:, :, :], k.wcol[:, :].unsqueeze(2).to_broadcast([P, J, D]), ALU.mult))
                    link(v.tensor_tensor(k.hf[:, :, :], k.ps_b[:, 0:J, :], k.B["L1_gnn_b_in2f"].unsqueeze(1).to_broadcast([P, J, D]), ALU.add))
                    v.tensor_tensor(k.msg[:, :, 0:D], k.hf[:, :, :], k.fw[:, :, :], ALU.mult).then_inc(s_msg, 1)
                dve.wait_ge(s_sum, i + 1)
                for j in range(J):
                    v.tensor_copy(k.summed[:, j, :], sum_of(j)).then_inc(s_out, 1)
                link.end()
            every_group(dve, body)

        @block.scalar
        def _(act):
            s = nc.scalar

            def body(i, tail):
                if ln:
                    act.wait_ge(s_stat, i + 1)
                    if filt:
                        s.activation(k.lnv[:, :], k.var[:, :], ACT.Ln, bias=k.eps[:, 0:1], scale=1.0 / D).then_inc(s_hid2, 1)
                        act.wait_ge(s_hid2, 3 * i + 1)
                        s.activation(k.std[:, :], k.lnv[:, :], ACT.Exp, scale=0.5).then_inc(s_std, 1)
                    else:
                        s.activation(k.std[:, :], k.var[:, :], ACT.Sqrt, bias=k.eps[:, 0:1], scale=1.0 / D).then_inc(s_std, 1)
                if filt:
                    act.wait_ge(s_hid, i + 1)
                    s.activation(k.az[:, :, :], k.z[:, :, :], ACT.Abs).then_inc(s_hid2, 1)
                    act.wait_ge(s_hid2, 3 * i + 2)
                    s.activation(k.az[:, :, :], k.az[:, :, :], ACT.Exp, scale=-1.0).then_inc(s_hid2, 1)
                    act.wait_ge(s_hid2, 3 * i + 3)
                    s.activation(k.az[:, :, :], k.az[:, :, :], ACT.Ln, bias=1.0).then_inc(s_act, 1)
            if ln:
                every_group(act, body)

        @block.tensor
        def _(pe):
            t = nc.tensor

            def body(i, tail):
                if filt:
                    pe.wait_ge(s_norm, i + 1)
                    pe.wait_ge(s_idx, 16 * loads * (i + 1))
                    for j in range(J):
                        t.transpose(k.ps_a[:, j, :], k.rows[:, j, 0:D], k.ident[:, :])
                        last = t.transpose(k.ps_b[0:R, j, :], k.rbf[:, j, :], k.ident[:, :])
                    last.then_inc(s_tp, 1)
                    pe.wait_ge(s_tpc, i + 1)
                    for j in range(J):
                        last = t.matmul(k.ps_a[:, j, :], k.f1_t[:, :], k.rbf_t[:, j, :], start=True, stop=True)
                    last.then_inc(s_f1, 1)
                    for j in range(J):
                        t.matmul(k.ps_b[:, j, :], k.h_t[:, j, :], k.W["L1_gnn_W_in2f"], start=True, stop=True)
                    pe.wait_ge(s_ssp, i + 1)
                    for j in range(J):
                        last = t.matmul(k.ps_c[:, j, :], k.z[:, j, :], k.W["L1_gnn_W_f2"], start=True, stop=True)
                    last.then_inc(s_fw, 1)
                pe.wait_ge(s_msg, i + 1)
                for j in range(J):
                    last = t.matmul(sum_of(j), k.same[:, j, :], k.msg[:, j, :], start=True, stop=True)
                last.then_inc(s_sum, 1)
            every_group(pe, body)


def node_pass(k, a, name, kind, table, out, sums=None, residual=None):
    nc = k.nc
    s_in, s_st = k.sem(f"{name}_in"), k.sem(f"{name}_st")
    s_chain, s_stat, s_std = k.sem(f"{name}_chain"), k.sem(f"{name}_stat"), k.sem(f"{name}_std")
    s_op, s_tp, s_tc, s_mm, s_done = (k.sem(f"{name}_{x}") for x in ("op", "tp", "tc", "mm", "done"))
    s_z, s_a, s_az = k.sem(f"{name}_z"), k.sem(f"{name}_a"), k.sem(f"{name}_az")
    ln = kind in ("first", "last")
    width = D if kind == "first" else W
    loads = 2 + (residual is not None)
    out_w = D if kind == "last" else W

    def every_group(eng, body):
        with eng.Fori(0, NG) as i:
            body(i, P)
        body(NG, NTP)

    with nc.Block() as block:
        @block.sync
        def _(sp):
            def body(i, parts):
                sp.wait_ge(s_done, i + 1)
                sp.dma_start(k.rows[0:parts, :, 0:width], group_rows(table, i, parts)).then_inc(s_in, 16)
                sp.dma_start(k.summed[0:parts, :, :], group_rows(sums, i, parts)).then_inc(s_in, 16)
                if residual is not None:
                    sp.dma_start(k.res[0:parts, :, :], group_rows(residual, i, parts)).then_inc(s_in, 16)
                sp.wait_ge(s_done, i + 2)
                sp.dma_start(group_rows(out, i, parts), k.msg[0:parts, :, 0:out_w]).then_inc(s_st, 16)
            sp.nop().then_inc(s_done, 1)
            sp.nop().then_inc(s_st, 16)
            every_group(sp, body)
            sp.wait_ge(s_st, 16 * (NG + 2))

        @block.vector
        def _(dve):
            v = nc.vector
            link = Chain(dve, s_chain, {"first": 2 * J + 5 + 3 + 4, "mid": 4, "filter": 6, "linear": 3, "last": 2 * J + 6 + 4}[kind])

            def body(i, parts):
                link.round(i)
                dve.wait_ge(s_in, 16 * loads * (i + 1))
                dve.wait_ge(s_st, 16 * (i + 1))
                x, agg, o = k.rows[:, :, 0:D], k.summed[:, :, 0:D], k.msg[:, :, 0:D]
                each = lambda ap: ap.unsqueeze(2).to_broadcast([P, J, D])
                over = lambda ap: ap.unsqueeze(1).to_broadcast([P, J, D])
                if ln:
                    for j in range(J):
                        link(v.bn_stats(k.stats[:, j, :], k.rows[:, j, 0:D]))
                    moments(v, k, link)
                    v.scalar_tensor_tensor(k.var[:, :], k.gap[:, :], D / 4, k.var[:, :], ALU.mult, ALU.add).then_inc(s_stat, 1)
                    dve.wait_ge(s_std, i + 1)
                    link(v.reciprocal(k.rstd[:, :], k.std[:, :]))
                    link(v.scalar_tensor_tensor(k.mean[:, :], k.mean[:, :], -0.5, k.rstd[:, :], ALU.mult, ALU.mult))
                    for j in range(J):
                        link(v.tensor_scalar(k.z[:, j, :], k.rows[:, j, 0:D], k.rstd[:, j:j + 1], k.mean[:, j:j + 1], ALU.mult, ALU.add))
                    link(v.tensor_scalar(k.z[:, :, :], k.z[:, :, :], 0.0, None, ALU.max))
                if kind in ("first", "mid"):
                    link(v.tensor_scalar(k.dup[:, :], k.summed[:, :, AUX], 1.0, None, ALU.max))
                    link(v.reciprocal(k.dup[:, :], k.dup[:, :]))
                    v.tensor_tensor(k.fw[:, :, :], agg, each(k.dup[:, :]), ALU.mult).then_inc(s_op, 1)
                if kind in ("first", "mid", "filter", "linear"):
                    dve.wait_ge(s_tp, i + 1)
                    if kind in ("first", "mid"):
                        link(v.tensor_copy(k.h_t[:, :, :], k.ps_a[:, 0:J, :]))
                    v.tensor_copy(k.az[:, :, :], k.ps_b[:, 0:J, :]).then_inc(s_tc, 1)
                if kind == "filter":
                    dve.wait_ge(s_z, i + 1)
                    v.tensor_scalar(k.z[:, :, :], k.ps_a[:, 0:J, :], k.o1_bias[:, 0:1], None, ALU.add).then_inc(s_a, 1)
                    link(v.tensor_scalar(k.dup[:, :], k.summed[:, :, AUX], 1.0, 1.0, ALU.add, ALU.max))
                    link(v.reciprocal(k.dup[:, :], k.dup[:, :]))
                    v.tensor_copy(k.mean[:, :], k.dup[:, :]).then_inc(s_stat, 1)
                    dve.wait_ge(s_az, i + 1)
                    link(v.tensor_scalar(k.z[:, :, :], k.z[:, :, :], 0.0, -LOG2, ALU.max, ALU.add))
                    v.tensor_tensor(k.z[:, :, :], k.z[:, :, :], k.fw[:, :, :], ALU.add).then_inc(s_op, 1)
                    link(v.tensor_copy(k.msg[:, :, AUX], k.std[:, :]))
                if kind != "last":
                    dve.wait_ge(s_mm, i + 1)
                    bias = {"first": k.B["L0_0"], "mid": k.B["L0_1"], "filter": k.B["L1_gnn_b_o2"], "linear": k.B["L2_gnn_b"]}[kind]
                    link(v.tensor_tensor(o, k.ps_c[:, 0:J, :], over(bias), ALU.add))
                if kind == "first":
                    link(v.memset(k.msg[:, :, D:W], 1.0))
                    v.tensor_scalar(o, o, 0.0, None, ALU.max).then_inc(s_done, 1)
                elif kind == "mid":
                    v.tensor_tensor(o, o, k.res[:, :, :], ALU.add).then_inc(s_done, 1)
                elif kind == "filter":
                    link(v.tensor_tensor(o, o, x, ALU.add))
                    v.memset(k.msg[:, :, D + 1:W], 0.0).then_inc(s_done, 1)
                elif kind == "linear":
                    link(v.tensor_copy(k.msg[:, :, D:W], k.rows[:, :, D:W]))
                    link(v.tensor_tensor(o, o, x, ALU.add))
                    v.tensor_copy(k.dup[:, :], k.rows[:, :, AUX]).then_inc(s_done, 1)
                else:
                    inv_root = k.rows[:, :, AUX]
                    link(v.tensor_tensor(k.z[:, :, :], k.z[:, :, :], each(inv_root), ALU.mult))
                    link(v.tensor_tensor(k.z[:, :, :], k.z[:, :, :], agg, ALU.add))
                    link(v.tensor_tensor(k.z[:, :, :], k.z[:, :, :], each(inv_root), ALU.mult))
                    v.tensor_tensor(o, k.z[:, :, :], x, ALU.add).then_inc(s_done, 1)
                link.end()
            every_group(dve, body)

        @block.scalar
        def _(act):
            s = nc.scalar

            def body(i, parts):
                if ln:
                    act.wait_ge(s_stat, i + 1)
                    s.activation(k.std[:, :], k.var[:, :], ACT.Sqrt, bias=k.eps[:, 0:1], scale=1.0 / D).then_inc(s_std, 1)
                if kind == "filter":
                    act.wait_ge(s_a, i + 1)
                    s.activation(k.fw[:, :, :], k.z[:, :, :], ACT.Abs).then_inc(s_std, 1)
                    act.wait_ge(s_std, 4 * i + 1)
                    s.activation(k.fw[:, :, :], k.fw[:, :, :], ACT.Exp, scale=-1.0).then_inc(s_std, 1)
                    act.wait_ge(s_std, 4 * i + 2)
                    s.activation(k.fw[:, :, :], k.fw[:, :, :], ACT.Ln, bias=1.0).then_inc(s_std, 1)
                    act.wait_ge(s_stat, i + 1)
                    s.activation(k.lnv[:, :], k.mean[:, :], ACT.Ln).then_inc(s_std, 1)
                    act.wait_ge(s_std, 4 * i + 4)
                    s.activation(k.std[:, :], k.lnv[:, :], ACT.Exp, scale=0.5).then_inc(s_az, 1)
            if ln or kind == "filter":
                every_group(act, body)

        @block.tensor
        def _(pe):
            t = nc.tensor

            def body(i, parts):
                src = k.fw if kind in ("first", "mid") else k.summed
                if kind in ("first", "mid"):
                    pe.wait_ge(s_op, i + 1)
                else:
                    pe.wait_ge(s_in, 16 * loads * (i + 1))
                pe.wait_ge(s_done, i + 1)
                for j in range(J):
                    if kind in ("first", "mid"):
                        t.transpose(k.ps_a[:, j, :], (k.z if kind == "first" else k.rows)[:, j, 0:D], k.ident[:, :])
                    last = t.transpose(k.ps_b[:, j, :], src[:, j, 0:D], k.ident[:, :])
                last.then_inc(s_tp, 1)
                pe.wait_ge(s_tc, i + 1)
                for j in range(J):
                    if kind in ("first", "mid"):
                        n = "01"[kind == "mid"]
                        t.matmul(k.ps_c[:, j, :], k.h_t[:, j, :], k.W[f"L0_gnn_W_lin{n}"], start=True, stop=False)
                        last = t.matmul(k.ps_c[:, j, :], k.az[:, j, :], k.W[f"L0_gnn_W_conv{n}"], start=False, stop=True)
                    elif kind == "filter":
                        last = t.matmul(k.ps_a[:, j, :], k.W["L1_gnn_W_o1"], k.az[:, j, :], start=True, stop=True)
                    else:
                        last = t.matmul(k.ps_c[:, j, :], k.az[:, j, :], k.W["L2_gnn_W"], start=True, stop=True)
                if kind == "filter":
                    last.then_inc(s_z, 1)
                    pe.wait_ge(s_op, i + 1)
                    for j in range(J):
                        last = t.matmul(k.ps_c[:, j, :], k.z[:, j, :], k.W["L1_gnn_W_o2"], start=True, stop=True)
                last.then_inc(s_mm, 1)
            if kind != "last":
                every_group(pe, body)


def build(nc, **a):
    with ExitStack() as ctx:
        k = Kernel(nc, ctx)
        dram = lambda name, rows=N + P: nc.dram_tensor(name, [rows, W], FP32, kind="Internal").ap()
        tables = [dram(f"table{n}", N) for n in range(4)]
        sums = [dram(f"sums{n}") for n in range(5)]
        k.ps_a, k.ps_b, k.ps_c = (k.ps(f"ps_{c}", [P, 8, P]) for c in "abc")
        k.ps_sum = k.ps("ps_sum", [P, 2, 512])
        k.gidx, k.kidx, k.sidx = (k.sb(x, [P, J], I32) for x in ("gidx", "kidx", "sidx"))
        k.krow = k.sb("krow", [P, G], I32)
        k.rbf, k.rbf_t = k.sb("rbf", [P, J, R]), k.sb("rbf_t", [R, J, P])
        k.wcol, k.kcol, k.dup, k.tgt = (k.sb(x, [P, J]) for x in ("wcol", "kcol", "dup", "tgt"))
        k.mean, k.gap, k.var = (k.sb(x, [P, J]) for x in ("mean", "gap", "var"))
        k.std, k.rstd, k.lnv = (k.sb(x, [P, J]) for x in ("std", "rstd", "lnv"))
        k.stats = k.sb("stats", [P, J, 6])
        k.same, k.junk = k.sb("same", [P, J, P]), k.sb("junk", [P, P])
        k.rows, k.msg, k.summed = (k.sb(x, [P, J, W]) for x in ("rows", "msg", "summed"))
        k.h_t, k.z, k.az, k.fw, k.hf, k.res = (k.sb(x, [P, J, D]) for x in ("h_t", "z", "az", "fw", "hf", "res"))
        x = a["x"]
        with k.one_pass():
            load_constants(k, a)
        with k.one_pass():
            clear_tables(k, sums)
        with k.one_pass():
            edge_pass(k, a, "e0", "h", x, sums[0], "src", "dst")
        with k.one_pass():
            node_pass(k, a, "n0", "first", x, tables[0], sums[0])
        with k.one_pass():
            edge_pass(k, a, "e1", "plain", tables[0], sums[1], "src", "dst")
        with k.one_pass():
            node_pass(k, a, "n1", "mid", tables[0], tables[1], sums[1], x)
        with k.one_pass():
            edge_pass(k, a, "e2", "filter", tables[1], sums[2], "dst", "src")
        with k.one_pass():
            node_pass(k, a, "n2", "filter", tables[1], tables[2], sums[2])
        with k.one_pass():
            edge_pass(k, a, "e3", "weight", tables[2], sums[3], "src", "dst")
        with k.one_pass():
            node_pass(k, a, "n3", "linear", tables[2], tables[3], sums[3])
        with k.one_pass():
            edge_pass(k, a, "e4", "degree", tables[3], sums[4], "src", "dst")
        with k.one_pass():
            node_pass(k, a, "n4", "last", tables[3], a["out"], sums[4])


INPUTS = ["x", "src", "dst", "edge_attr_20", "edge_weight",
          "L0_gnn_W_conv0", "L0_gnn_b_conv0", "L0_gnn_W_lin0", "L0_gnn_b_lin0",
          "L0_gnn_W_conv1", "L0_gnn_b_conv1", "L0_gnn_W_lin1", "L0_gnn_b_lin1",
          "L1_gnn_W_in2f", "L1_gnn_b_in2f", "L1_gnn_W_f1", "L1_gnn_b_f1", "L1_gnn_W_f2", "L1_gnn_b_f2",
          "L1_gnn_W_o1", "L1_gnn_b_o1", "L1_gnn_W_o2", "L1_gnn_b_o2", "L2_gnn_W", "L2_gnn_b"]


def kernel(**inputs):
    import concourse.bacc as bacc
    from concourse.bass_utils import run_bass_kernel_spmd

    nc = bacc.Bacc("TRN2", target_bir_lowering=False, num_devices=1)
    arrays, aps = {}, {}
    for name in INPUTS:
        arrays[name] = np.ascontiguousarray(inputs[name])
        aps[name] = nc.dram_tensor(name, arrays[name].shape, mybir.dt.from_np(arrays[name].dtype),
                                   kind="ExternalInput").ap()
    aps["out"] = nc.dram_tensor("out", [N, D], FP32, kind="ExternalOutput").ap()
    build(nc, **aps)
    return run_bass_kernel_spmd(nc, [arrays], core_ids=[0]).results[0]["out"]
```

```python
from contextlib import ExitStack, contextmanager

import numpy as np

import concourse.bass as bass
from concourse import mybir

FP32, I32, BF16, F16 = mybir.dt.float32, mybir.dt.int32, mybir.dt.bfloat16, mybir.dt.float16
ALU, ACT, AX = mybir.AluOpType, mybir.ActivationFunctionType, mybir.AxisListType

P = 128
N, D = 100000, 128
E, R = 50000, 20
W = D + 4
AUX = D
SPARES = 2 * P
J = 5
G = P * J
NG, NT = divmod(N, G)
EG, ET = divmod(E, G)
NTP, ETP = NT // J, ET // J
EPS = 1e-5
LOG2 = 0.6931471805599453

T = 4
STEPS = -(-N // (T * P))
B = 2
TILES, BLOCKS = STEPS * T, STEPS * B
LEAD = 6
AHEAD = 8
WINDOW = B * LEAD
RING = 64
FULL, LAST = divmod(E, P)
assert STEPS % 4 == 0 and AHEAD % 4 == 0 and AHEAD >= LEAD + 2 and BLOCKS > FULL and RING >= 4 * WINDOW


class Chain:

    def __init__(self, eng, sem, per_round=None):
        self.eng, self.sem, self.per_round, self.base, self.k = eng, sem, per_round, 0, 0

    def round(self, i):
        self.base, self.k = i * self.per_round, 0

    def __call__(self, ins):
        ins.then_inc(self.sem, 1)
        self.k += 1
        self.eng.wait_ge(self.sem, self.base + self.k)

    def end(self):
        assert self.k == self.per_round, (self.k, self.per_round)


def take(eng, sem, n):
    eng.wait_ge(sem, n)
    eng.nop().then_inc(sem, -n)


def moments(v, k, link):
    half = lambda n: k.stats[:, :, n]
    link(v.tensor_tensor(k.mean[:, :], half(1), half(4), ALU.add))
    link(v.tensor_tensor(k.gap[:, :], half(1), half(4), ALU.subtract))
    link(v.tensor_tensor(k.gap[:, :], k.gap[:, :], k.gap[:, :], ALU.mult))
    link(v.tensor_tensor(k.var[:, :], half(2), half(5), ALU.add))


def group_rows(ap, i, parts=P):
    return ap[bass.ds(i * G, parts * J), :].rearrange("(p j) w -> p j w", j=J)


class Kernel:
    def __init__(self, nc, ctx):
        self.nc, self.ctx, self.owned = nc, ctx, 0

    def sb(self, name, shape, dt=FP32):
        return self.ctx.enter_context(self.nc.sbuf_tensor(name, shape, dt))

    def ps(self, name, shape):
        return self.ctx.enter_context(self.nc.psum_tensor(name, shape, FP32))

    def sem(self, name):
        self.sems.append(self.pass_ctx.enter_context(self.nc.semaphore(name)))
        return self.sems[-1]

    def own(self, name, shape, dt=FP32):
        self.owned += 1
        return self.pass_ctx.enter_context(self.nc.sbuf_tensor(f"{name}_{self.owned}", shape, dt))

    def only(self, path):
        def part(program):
            def guarded(eng):
                if path is None:
                    return program(eng)
                at = ("sorted", "general").index(path)
                with eng.If(eng.value_load(self.paths[0:1, at:at + 1], min_val=0, max_val=1)):
                    program(eng)
            return guarded
        return part

    def lasting_sem(self, name):
        return self.ctx.enter_context(self.nc.semaphore(name))

    @contextmanager
    def one_pass(self):
        self.sems = []
        with ExitStack() as self.pass_ctx:
            yield
            with self.nc.Block() as block:
                @block.gpsimd
                def _(pool):
                    for s in self.sems:
                        pool.sem_clear(s)


def load_constants(k, a):
    nc = k.nc
    mats = ["L0_gnn_W_conv0", "L0_gnn_W_lin0", "L0_gnn_W_conv1", "L0_gnn_W_lin1", "L1_gnn_W_in2f",
            "L1_gnn_W_f2", "L1_gnn_W_o1", "L1_gnn_W_o2", "L2_gnn_W"]
    rows = ["L0_gnn_b_conv0", "L0_gnn_b_lin0", "L0_gnn_b_conv1", "L0_gnn_b_lin1", "L1_gnn_b_in2f",
            "L1_gnn_b_f2", "L1_gnn_b_o1", "L1_gnn_b_o2", "L2_gnn_b"]
    k.ident, k.tri = k.sb("ident", [P, P]), k.sb("tri", [P, P])
    k.spare_i, k.spare = k.sb("spare_i", [P, 1], I32), k.sb("spare", [P, 1])
    k.eps, k.turn = k.sb("eps", [P, 1]), k.sb("turn", [P, 1])
    k.zeros = k.sb("zeros", [P, J, W])
    k.wt, k.bias = k.sb("wt", [P, len(mats), P]), k.sb("bias", [P, len(rows) + 2, D])
    k.f1, k.f1_t = k.sb("f1", [P, R]), k.sb("f1_t", [R, P])
    k.f1_bias = k.sb("f1_bias", [P, 1])
    k.o1_bias = k.sb("o1_bias", [P, 1])
    k.raw = k.own("raw", [P, len(mats), P])
    s_const, s_load, s_pe, s_sum = k.sem("s_const"), k.sem("s_load"), k.sem("s_pe"), k.sem("s_sum")
    psw = k.ps_a
    k.W = {m: k.wt[:, n, :] for n, m in enumerate(mats)}
    k.B = {m: k.bias[:, n, :] for n, m in enumerate(rows)}
    k.B["L0_0"], k.B["L0_1"] = k.bias[:, len(rows), :], k.bias[:, len(rows) + 1, :]
    n_mats = len(mats)

    with nc.Block() as block:
        @block.sync
        def _(sp):
            for n, m in enumerate(mats):
                sp.dma_start(k.raw[:, n, :], a[m]).then_inc(s_load, 16)
            for n, m in enumerate(rows):
                sp.dma_start(k.bias[:, n, :], a[m].rearrange("(o n) -> o n", o=1).to_broadcast([P, D])).then_inc(s_load, 16)
            sp.dma_start(k.f1[:, :], a["L1_gnn_W_f1"]).then_inc(s_load, 16)
            sp.dma_start(k.f1_bias[:, :], a["L1_gnn_b_f1"].rearrange("(n o) -> n o", o=1)).then_inc(s_load, 16)
            sp.dma_start(k.o1_bias[:, :], a["L1_gnn_b_o1"].rearrange("(n o) -> n o", o=1)).then_inc(s_load, 16)

        @block.gpsimd
        def _(pool):
            pool.memset(k.ident[:, :], 0.0).then_inc(s_const, 1)
            pool.memset(k.tri[:, :], 1.0).then_inc(s_const, 1)
            pool.memset(k.eps[:, :], EPS)
            pool.memset(k.zeros[:, :, :], 0.0)
            pool.iota(k.spare_i[:, :], [[0, 1]], base=N, channel_multiplier=1).then_inc(s_const, 1)
            pool.wait_ge(s_const, 3)
            pool.affine_select(out=k.ident[:, :], in_=k.ident[:, :], compare_op=ALU.not_equal, fill=1.0,
                               base=0, pattern=[[-1, P]], channel_multiplier=1).then_inc(s_const, 1)
            pool.affine_select(out=k.tri[:, :], in_=k.tri[:, :], compare_op=ALU.is_gt, fill=0.0,
                               base=0, pattern=[[-1, P]], channel_multiplier=1).then_inc(s_const, 1)
            pool.tensor_copy(k.spare[:, :], k.spare_i[:, :]).then_inc(s_const, 1)

        @block.tensor
        def _(pe):
            pe.wait_ge(s_const, 6)
            pe.wait_ge(s_load, 16 * (len(mats) + len(rows) + 3))
            for n in range(n_mats):
                if n:
                    pe.wait_ge(s_sum, n)
                nc.tensor.transpose(psw[:, 0, :], k.raw[:, n, :], k.ident[:, :]).then_inc(s_pe, 1)
            pe.wait_ge(s_sum, n_mats)
            nc.tensor.transpose(psw[0:R, 0, :], k.f1[:, :], k.ident[:, :]).then_inc(s_pe, 1)

        @block.vector
        def _(dve):
            for n in range(n_mats):
                dve.wait_ge(s_pe, n + 1)
                nc.vector.tensor_copy(k.wt[:, n, :], psw[:, 0, :]).then_inc(s_sum, 1)
            dve.wait_ge(s_pe, n_mats + 1)
            nc.vector.tensor_copy(k.f1_t[:, :], psw[0:R, 0, :]).then_inc(s_sum, 1)
            dve.wait_ge(s_load, 16 * (len(mats) + len(rows) + 3))
            for n in (0, 1):
                nc.vector.tensor_tensor(k.B[f"L0_{n}"], k.B[f"L0_gnn_b_conv{n}"], k.B[f"L0_gnn_b_lin{n}"],
                                        ALU.add).then_inc(s_sum, 1)
            dve.wait_ge(s_sum, n_mats + 3)


def clear_tables(k, tables, path):
    s_cleared = k.sem("s_cleared")
    n = 0
    with k.nc.Block() as block:
        @block.sync
        @k.only(path)
        def _(sp):
            with sp.Fori(0, NG) as i:
                for t in tables:
                    sp.dma_start(group_rows(t, i), k.zeros[:, :, :]).then_inc(s_cleared, 16)
            for t in tables:
                rest = N + SPARES - NG * G
                sp.dma_start(t[NG * G:N + SPARES, :].rearrange("(p j) w -> p j w", j=4), k.zeros[0:rest // 4, 0:4, :]).then_inc(s_cleared, 16)
            sp.wait_ge(s_cleared, 16 * len(tables) * (NG + 1))


def general_buffers(k):
    sb = k.own
    k.gidx, k.kidx, k.sidx = (sb(x, [P, J], I32) for x in ("gidx", "kidx", "sidx"))
    k.krow = sb("krow", [P, G], I32)
    k.rbf, k.rbf_t = sb("rbf", [P, J, R]), sb("rbf_t", [R, J, P])
    k.wcol, k.kcol, k.dup, k.tgt = (sb(x, [P, J]) for x in ("wcol", "kcol", "dup", "tgt"))
    k.mean, k.gap, k.var = (sb(x, [P, J]) for x in ("mean", "gap", "var"))
    k.std, k.rstd, k.lnv = (sb(x, [P, J]) for x in ("std", "rstd", "lnv"))
    k.stats = sb("stats", [P, J, 6])
    k.same, k.junk = sb("same", [P, J, P]), sb("junk", [P, P])
    k.rows, k.msg, k.summed = (sb(x, [P, J, W]) for x in ("rows", "msg", "summed"))
    k.h_t, k.z, k.az, k.fw, k.hf, k.res = (sb(x, [P, J, D]) for x in ("h_t", "z", "az", "fw", "hf", "res"))


def sorted_buffers(k):
    sb = k.own
    k.numbers = sb("numbers", [P, 4, B], I32)
    k.stage, k.plain = sb("stage", [P, 4, B, W]), sb("plain", [P, 2, B, D])
    k.ring = sb("ring", [P, RING * D])
    k.plain_t = sb("plain_t", [P, 2, B, D])
    k.x, k.res4, k.y = sb("node_x", [P, 4, T, W]), sb("res4", [P, 4, T, W]), sb("y", [P, 4, T, W])
    k.h, k.h_t2 = (sb(x, [P, 2, T, D]) for x in ("h", "h_t2"))
    k.select = sb("select", [P, 2, T * B, P])
    k.estats, k.nstats = sb("estats", [P, 2, B, 6]), sb("nstats", [P, 2, T, 6])
    k.emv, k.nmv = sb("emv", [P, 2, B, 2]), sb("nmv", [P, 2, T, 2])
    k.estd, k.erstd, k.eshift = (sb(x, [P, 2, B]) for x in ("estd", "erstd", "eshift"))
    k.nstd, k.nrstd, k.nshift = (sb(x, [P, 2, T]) for x in ("nstd", "nrstd", "nshift"))
    k.idle, k.idle3 = sb("idle", [P, 4]), sb("idle3", [P, 1])


def edge_pass(k, a, name, path, mode, table, sums, gather_by, add_by):
    nc = k.nc
    general_buffers(k)
    ln, filt, weighted, from_row = mode in ("h", "filter", "weight", "degree"), mode == "filter", mode == "weight", mode == "degree"
    width = table.shape[1]
    s_idx, s_gidx, s_key, s_turn = (k.sem(f"{name}_{x}") for x in ("idx", "gidx", "key", "turn"))
    s_got, s_add = k.lasting_sem(f"{name}_got"), k.lasting_sem(f"{name}_add")
    s_chain, s_stat, s_std, s_norm = k.sem(f"{name}_chain"), k.sem(f"{name}_stat"), k.sem(f"{name}_std"), k.sem(f"{name}_norm")
    s_msg, s_sum, s_out, s_hid = k.sem(f"{name}_msg"), k.sem(f"{name}_sum"), k.sem(f"{name}_out"), k.sem(f"{name}_hid")
    s_act, s_tp, s_tpc, s_f1, s_ssp, s_fw = (k.sem(f"{name}_{x}") for x in ("act", "tp", "tpc", "f1", "ssp", "fw"))
    s_free = k.sem(f"{name}_free")
    s_preset, s_hid2 = k.sem(f"{name}_preset"), k.sem(f"{name}_hid2")
    loads = 2 + (weighted or filt) + filt
    gather_ap, key_ap = a[gather_by], a[add_by]
    sum_of = lambda j: k.ps_sum[:, j // 3, j % 3 * W:(j % 3 + 1) * W]

    def every_group(eng, body):
        with eng.Fori(0, EG) as i:
            body(i, False)
        body(EG, True)

    with nc.Block() as block:
        @block.sync
        @k.only(path)
        def _(sp):
            def body(i, tail):
                parts = ETP if tail else P
                sp.wait_ge(s_free, i + 1)
                if tail:
                    sp.wait_ge(s_preset, 1)
                col = lambda ap: ap[bass.ds(i * G, parts * J)].rearrange("(p j) -> p j", j=J)
                sp.dma_start(k.gidx[0:parts, :], col(gather_ap)).then_inc(s_gidx, 16)
                sp.dma_start(k.kidx[0:parts, :], col(key_ap)).then_inc(s_idx, 16)
                sp.dma_start(k.krow[:, 0:parts * J], key_ap[bass.ds(i * G, parts * J)].rearrange("(o n) -> o n", o=1)
                             .to_broadcast([P, parts * J])).then_inc(s_idx, 16)
                if weighted or filt:
                    sp.dma_start(k.wcol[0:parts, :], col(a["edge_weight"])).then_inc(s_idx, 16)
                if filt:
                    sp.dma_start(k.rbf[0:parts, :, :], group_rows(a["edge_attr_20"], i, parts)).then_inc(s_idx, 16)
            sp.nop().then_inc(s_free, 1)
            every_group(sp, body)

        @block.gpsimd
        @k.only(path)
        def _(pool):
            def body(i, tail):
                take(pool, s_gidx, 16)
                for j in range(J):
                    pool.indirect_dma_start(out=k.rows[:, j, 0:width], out_offset=None, in_=table,
                                            in_offset=bass.IndirectOffsetOnAxis(ap=k.gidx[:, j:j + 1], axis=0)).then_inc(s_got, 16)
                take(pool, s_key, 1)
                for j in range(J):
                    take(pool, s_out, 1)
                    pool.indirect_dma_start(out=sums, out_offset=bass.IndirectOffsetOnAxis(ap=k.sidx[:, j:j + 1], axis=0),
                                            in_=k.summed[:, j, :], in_offset=None, compute_op=ALU.add).then_inc(s_add, 16)
                    pool.wait_ge(s_add, 16 * (i * J + j + 1))
                    pool.tensor_tensor(k.turn[:, :], k.spare[:, :], k.spare[:, :], ALU.add).then_inc(s_turn, 1)
                    take(pool, s_turn, 1)
                pool.nop().then_inc(s_free, 1)
            every_group(pool, body)

        @block.vector
        @k.only(path)
        def _(dve):
            link = Chain(dve, s_chain, 2 * J + 5 + J * (weighted or from_row) + ((2 * J + 7) if ln else 1) + 5 * filt)
            v = nc.vector

            def body(i, tail):
                link.round(i)
                if tail:
                    dve.wait_ge(s_free, i + 1)
                    v.memset(k.krow[:, :], -1)
                    v.tensor_copy(k.kidx[:, :], k.spare_i[:, :].to_broadcast([P, J])).then_inc(s_preset, 1)
                    dve.wait_ge(s_preset, 1)
                dve.wait_ge(s_idx, 16 * loads * (i + 1))
                link(v.tensor_copy(k.kcol[:, :], k.kidx[:, :]))
                for j in range(J):
                    link(v.tensor_scalar(k.same[:, j, :], k.krow[:, j:G:J], k.kcol[:, j:j + 1], None, ALU.is_equal))
                for j in range(J):
                    link(v.tensor_tensor_reduce(out=k.junk[:, :], in0=k.same[:, j, :], in1=k.tri[:, :], scale=1.0, scalar=0.0,
                                                op0=ALU.mult, op1=ALU.add, accum_out=k.dup[:, j:j + 1]))
                link(v.tensor_scalar(k.dup[:, :], k.dup[:, :], 1.0, None, ALU.min))
                link(v.tensor_scalar(k.tgt[:, :], k.kcol[:, :], -1.0, k.spare[:, 0:1], ALU.mult, ALU.add))
                link(v.tensor_tensor(k.tgt[:, :], k.tgt[:, :], k.dup[:, :], ALU.mult))
                link(v.tensor_tensor(k.tgt[:, :], k.tgt[:, :], k.kcol[:, :], ALU.add))
                v.tensor_copy(k.sidx[:, :], k.tgt[:, :]).then_inc(s_key, 1)
                dve.wait_ge(s_got, 16 * J * (i + 1))
                if from_row:
                    wsrc = k.rows[:, :, AUX]
                elif weighted:
                    wsrc = k.wcol[:, :]
                if weighted or from_row:
                    for j in range(J):
                        link(v.tensor_scalar(k.same[:, j, :], k.same[:, j, :], wsrc[:, j:j + 1], None, ALU.mult))
                if not ln:
                    link(v.memset(k.msg[:, :, D:W], 1.0))
                    v.tensor_copy(k.msg[:, :, 0:D], k.rows[:, :, 0:D]).then_inc(s_msg, 1)
                else:
                    for j in range(J):
                        link(v.bn_stats(k.stats[:, j, :], k.rows[:, j, 0:D]))
                    moments(v, k, link)
                    v.scalar_tensor_tensor(k.var[:, :], k.gap[:, :], D / 4, k.var[:, :], ALU.mult, ALU.add).then_inc(s_stat, 1)
                    dve.wait_ge(s_std, i + 1)
                    link(v.reciprocal(k.rstd[:, :], k.std[:, :]))
                    link(v.scalar_tensor_tensor(k.mean[:, :], k.mean[:, :], -0.5, k.rstd[:, :], ALU.mult, ALU.mult))
                    for j in range(J):
                        link(v.tensor_scalar(k.rows[:, j, 0:D], k.rows[:, j, 0:D], k.rstd[:, j:j + 1], k.mean[:, j:j + 1], ALU.mult, ALU.add))
                if ln:
                    link(v.memset(k.msg[:, :, D:W], 1.0))
                if ln and not filt:
                    v.tensor_scalar(k.msg[:, :, 0:D], k.rows[:, :, 0:D], 0.0, None, ALU.max).then_inc(s_msg, 1)
                if filt:
                    v.tensor_scalar(k.rows[:, :, 0:D], k.rows[:, :, 0:D], 0.0, None, ALU.max).then_inc(s_norm, 1)
                    dve.wait_ge(s_tp, i + 1)
                    link(v.tensor_copy(k.h_t[:, :, :], k.ps_a[:, 0:J, :]))
                    v.tensor_copy(k.rbf_t[:, :, :], k.ps_b[0:R, 0:J, :]).then_inc(s_tpc, 1)
                    dve.wait_ge(s_f1, i + 1)
                    v.tensor_scalar(k.z[:, :, :], k.ps_a[:, 0:J, :], k.f1_bias[:, 0:1], None, ALU.add).then_inc(s_hid, 1)
                    dve.wait_ge(s_act, i + 1)
                    link(v.tensor_scalar(k.z[:, :, :], k.z[:, :, :], 0.0, -LOG2, ALU.max, ALU.add))
                    v.tensor_tensor(k.z[:, :, :], k.z[:, :, :], k.az[:, :, :], ALU.add).then_inc(s_ssp, 1)
                    dve.wait_ge(s_fw, i + 1)
                    link(v.tensor_tensor(k.fw[:, :, :], k.ps_c[:, 0:J, :], k.B["L1_gnn_b_f2"].unsqueeze(1).to_broadcast([P, J, D]), ALU.add))
                    link(v.tensor_tensor(k.fw[:, :, :], k.fw[:, :, :], k.wcol[:, :].unsqueeze(2).to_broadcast([P, J, D]), ALU.mult))
                    link(v.tensor_tensor(k.hf[:, :, :], k.ps_b[:, 0:J, :], k.B["L1_gnn_b_in2f"].unsqueeze(1).to_broadcast([P, J, D]), ALU.add))
                    v.tensor_tensor(k.msg[:, :, 0:D], k.hf[:, :, :], k.fw[:, :, :], ALU.mult).then_inc(s_msg, 1)
                dve.wait_ge(s_sum, i + 1)
                for j in range(J):
                    v.tensor_copy(k.summed[:, j, :], sum_of(j)).then_inc(s_out, 1)
                link.end()
            every_group(dve, body)

        @block.scalar
        @k.only(path)
        def _(act):
            s = nc.scalar

            def body(i, tail):
                if ln:
                    act.wait_ge(s_stat, i + 1)
                    if filt:
                        s.activation(k.lnv[:, :], k.var[:, :], ACT.Ln, bias=k.eps[:, 0:1], scale=1.0 / D).then_inc(s_hid2, 1)
                        act.wait_ge(s_hid2, 3 * i + 1)
                        s.activation(k.std[:, :], k.lnv[:, :], ACT.Exp, scale=0.5).then_inc(s_std, 1)
                    else:
                        s.activation(k.std[:, :], k.var[:, :], ACT.Sqrt, bias=k.eps[:, 0:1], scale=1.0 / D).then_inc(s_std, 1)
                if filt:
                    act.wait_ge(s_hid, i + 1)
                    s.activation(k.az[:, :, :], k.z[:, :, :], ACT.Abs).then_inc(s_hid2, 1)
                    act.wait_ge(s_hid2, 3 * i + 2)
                    s.activation(k.az[:, :, :], k.az[:, :, :], ACT.Exp, scale=-1.0).then_inc(s_hid2, 1)
                    act.wait_ge(s_hid2, 3 * i + 3)
                    s.activation(k.az[:, :, :], k.az[:, :, :], ACT.Ln, bias=1.0).then_inc(s_act, 1)
            if ln:
                every_group(act, body)

        @block.tensor
        @k.only(path)
        def _(pe):
            t = nc.tensor

            def body(i, tail):
                if filt:
                    pe.wait_ge(s_norm, i + 1)
                    pe.wait_ge(s_idx, 16 * loads * (i + 1))
                    for j in range(J):
                        t.transpose(k.ps_a[:, j, :], k.rows[:, j, 0:D], k.ident[:, :])
                        last = t.transpose(k.ps_b[0:R, j, :], k.rbf[:, j, :], k.ident[:, :])
                    last.then_inc(s_tp, 1)
                    pe.wait_ge(s_tpc, i + 1)
                    for j in range(J):
                        last = t.matmul(k.ps_a[:, j, :], k.f1_t[:, :], k.rbf_t[:, j, :], start=True, stop=True)
                    last.then_inc(s_f1, 1)
                    for j in range(J):
                        t.matmul(k.ps_b[:, j, :], k.h_t[:, j, :], k.W["L1_gnn_W_in2f"], start=True, stop=True)
                    pe.wait_ge(s_ssp, i + 1)
                    for j in range(J):
                        last = t.matmul(k.ps_c[:, j, :], k.z[:, j, :], k.W["L1_gnn_W_f2"], start=True, stop=True)
                    last.then_inc(s_fw, 1)
                pe.wait_ge(s_msg, i + 1)
                for j in range(J):
                    last = t.matmul(sum_of(j), k.same[:, j, :], k.msg[:, j, :], start=True, stop=True)
                last.then_inc(s_sum, 1)
            every_group(pe, body)


def node_pass(k, a, name, path, kind, table, out, sums, residual=None):
    nc = k.nc
    general_buffers(k)
    s_in, s_st = k.sem(f"{name}_in"), k.sem(f"{name}_st")
    s_chain, s_stat, s_std = k.sem(f"{name}_chain"), k.sem(f"{name}_stat"), k.sem(f"{name}_std")
    s_op, s_tp, s_tc, s_mm, s_done = (k.sem(f"{name}_{x}") for x in ("op", "tp", "tc", "mm", "done"))
    s_z, s_a, s_az = k.sem(f"{name}_z"), k.sem(f"{name}_a"), k.sem(f"{name}_az")
    ln = kind in ("first", "last")
    width = table.shape[1]
    loads = 2 + (residual is not None)
    out_w = out.shape[1]

    def every_group(eng, body):
        with eng.Fori(0, NG) as i:
            body(i, P)
        body(NG, NTP)

    with nc.Block() as block:
        @block.sync
        @k.only(path)
        def _(sp):
            def body(i, parts):
                sp.wait_ge(s_done, i + 1)
                sp.dma_start(k.rows[0:parts, :, 0:width], group_rows(table, i, parts)).then_inc(s_in, 16)
                sp.dma_start(k.summed[0:parts, :, :], group_rows(sums, i, parts)).then_inc(s_in, 16)
                if residual is not None:
                    sp.dma_start(k.res[0:parts, :, :], group_rows(residual, i, parts)).then_inc(s_in, 16)
                sp.wait_ge(s_done, i + 2)
                sp.dma_start(group_rows(out, i, parts), k.msg[0:parts, :, 0:out_w]).then_inc(s_st, 16)
            sp.nop().then_inc(s_done, 1)
            sp.nop().then_inc(s_st, 16)
            every_group(sp, body)
            sp.wait_ge(s_st, 16 * (NG + 2))

        @block.vector
        @k.only(path)
        def _(dve):
            v = nc.vector
            link = Chain(dve, s_chain, {"first": 2 * J + 5 + 3 + 3, "mid": 4, "filter": 6, "linear": 3, "last": 2 * J + 6 + 4}[kind])

            def body(i, parts):
                link.round(i)
                dve.wait_ge(s_in, 16 * loads * (i + 1))
                dve.wait_ge(s_st, 16 * (i + 1))
                x, agg, o = k.rows[:, :, 0:D], k.summed[:, :, 0:D], k.msg[:, :, 0:D]
                each = lambda ap: ap.unsqueeze(2).to_broadcast([P, J, D])
                over = lambda ap: ap.unsqueeze(1).to_broadcast([P, J, D])
                if ln:
                    for j in range(J):
                        link(v.bn_stats(k.stats[:, j, :], k.rows[:, j, 0:D]))
                    moments(v, k, link)
                    v.scalar_tensor_tensor(k.var[:, :], k.gap[:, :], D / 4, k.var[:, :], ALU.mult, ALU.add).then_inc(s_stat, 1)
                    dve.wait_ge(s_std, i + 1)
                    link(v.reciprocal(k.rstd[:, :], k.std[:, :]))
                    link(v.scalar_tensor_tensor(k.mean[:, :], k.mean[:, :], -0.5, k.rstd[:, :], ALU.mult, ALU.mult))
                    for j in range(J):
                        link(v.tensor_scalar(k.z[:, j, :], k.rows[:, j, 0:D], k.rstd[:, j:j + 1], k.mean[:, j:j + 1], ALU.mult, ALU.add))
                    link(v.tensor_scalar(k.z[:, :, :], k.z[:, :, :], 0.0, None, ALU.max))
                if kind in ("first", "mid"):
                    link(v.tensor_scalar(k.dup[:, :], k.summed[:, :, AUX], 1.0, None, ALU.max))
                    link(v.reciprocal(k.dup[:, :], k.dup[:, :]))
                    v.tensor_tensor(k.fw[:, :, :], agg, each(k.dup[:, :]), ALU.mult).then_inc(s_op, 1)
                if kind in ("first", "mid", "filter", "linear"):
                    dve.wait_ge(s_tp, i + 1)
                    if kind in ("first", "mid"):
                        link(v.tensor_copy(k.h_t[:, :, :], k.ps_a[:, 0:J, :]))
                    v.tensor_copy(k.az[:, :, :], k.ps_b[:, 0:J, :]).then_inc(s_tc, 1)
                if kind == "filter":
                    dve.wait_ge(s_z, i + 1)
                    v.tensor_scalar(k.z[:, :, :], k.ps_a[:, 0:J, :], k.o1_bias[:, 0:1], None, ALU.add).then_inc(s_a, 1)
                    link(v.tensor_scalar(k.dup[:, :], k.summed[:, :, AUX], 1.0, 1.0, ALU.add, ALU.max))
                    link(v.reciprocal(k.dup[:, :], k.dup[:, :]))
                    v.tensor_copy(k.mean[:, :], k.dup[:, :]).then_inc(s_stat, 1)
                    dve.wait_ge(s_az, i + 1)
                    link(v.tensor_scalar(k.z[:, :, :], k.z[:, :, :], 0.0, -LOG2, ALU.max, ALU.add))
                    v.tensor_tensor(k.z[:, :, :], k.z[:, :, :], k.fw[:, :, :], ALU.add).then_inc(s_op, 1)
                    link(v.tensor_copy(k.msg[:, :, AUX], k.std[:, :]))
                if kind != "last":
                    dve.wait_ge(s_mm, i + 1)
                    bias = {"first": k.B["L0_0"], "mid": k.B["L0_1"], "filter": k.B["L1_gnn_b_o2"], "linear": k.B["L2_gnn_b"]}[kind]
                    link(v.tensor_tensor(o, k.ps_c[:, 0:J, :], over(bias), ALU.add))
                if kind == "first":
                    v.tensor_scalar(o, o, 0.0, None, ALU.max).then_inc(s_done, 1)
                elif kind == "mid":
                    v.tensor_tensor(o, o, k.res[:, :, :], ALU.add).then_inc(s_done, 1)
                elif kind == "filter":
                    link(v.tensor_tensor(o, o, x, ALU.add))
                    v.memset(k.msg[:, :, D + 1:W], 0.0).then_inc(s_done, 1)
                elif kind == "linear":
                    link(v.tensor_copy(k.msg[:, :, D:W], k.rows[:, :, D:W]))
                    link(v.tensor_tensor(o, o, x, ALU.add))
                    v.tensor_copy(k.dup[:, :], k.rows[:, :, AUX]).then_inc(s_done, 1)
                else:
                    inv_root = k.rows[:, :, AUX]
                    link(v.tensor_tensor(k.z[:, :, :], k.z[:, :, :], each(inv_root), ALU.mult))
                    link(v.tensor_tensor(k.z[:, :, :], k.z[:, :, :], agg, ALU.add))
                    link(v.tensor_tensor(k.z[:, :, :], k.z[:, :, :], each(inv_root), ALU.mult))
                    v.tensor_tensor(o, k.z[:, :, :], x, ALU.add).then_inc(s_done, 1)
                link.end()
            every_group(dve, body)

        @block.scalar
        @k.only(path)
        def _(act):
            s = nc.scalar

            def body(i, parts):
                if ln:
                    act.wait_ge(s_stat, i + 1)
                    s.activation(k.std[:, :], k.var[:, :], ACT.Sqrt, bias=k.eps[:, 0:1], scale=1.0 / D).then_inc(s_std, 1)
                if kind == "filter":
                    act.wait_ge(s_a, i + 1)
                    s.activation(k.fw[:, :, :], k.z[:, :, :], ACT.Abs).then_inc(s_std, 1)
                    act.wait_ge(s_std, 4 * i + 1)
                    s.activation(k.fw[:, :, :], k.fw[:, :, :], ACT.Exp, scale=-1.0).then_inc(s_std, 1)
                    act.wait_ge(s_std, 4 * i + 2)
                    s.activation(k.fw[:, :, :], k.fw[:, :, :], ACT.Ln, bias=1.0).then_inc(s_std, 1)
                    act.wait_ge(s_stat, i + 1)
                    s.activation(k.lnv[:, :], k.mean[:, :], ACT.Ln).then_inc(s_std, 1)
                    act.wait_ge(s_std, 4 * i + 4)
                    s.activation(k.std[:, :], k.lnv[:, :], ACT.Exp, scale=0.5).then_inc(s_az, 1)
            if ln or kind == "filter":
                every_group(act, body)

        @block.tensor
        @k.only(path)
        def _(pe):
            t = nc.tensor

            def body(i, parts):
                src = k.fw if kind in ("first", "mid") else k.summed
                if kind in ("first", "mid"):
                    pe.wait_ge(s_op, i + 1)
                else:
                    pe.wait_ge(s_in, 16 * loads * (i + 1))
                pe.wait_ge(s_done, i + 1)
                for j in range(J):
                    if kind in ("first", "mid"):
                        t.transpose(k.ps_a[:, j, :], (k.z if kind == "first" else k.rows)[:, j, 0:D], k.ident[:, :])
                    last = t.transpose(k.ps_b[:, j, :], src[:, j, 0:D], k.ident[:, :])
                last.then_inc(s_tp, 1)
                pe.wait_ge(s_tc, i + 1)
                for j in range(J):
                    if kind in ("first", "mid"):
                        n = "01"[kind == "mid"]
                        t.matmul(k.ps_c[:, j, :], k.h_t[:, j, :], k.W[f"L0_gnn_W_lin{n}"], start=True, stop=False)
                        last = t.matmul(k.ps_c[:, j, :], k.az[:, j, :], k.W[f"L0_gnn_W_conv{n}"], start=False, stop=True)
                    elif kind == "filter":
                        last = t.matmul(k.ps_a[:, j, :], k.W["L1_gnn_W_o1"], k.az[:, j, :], start=True, stop=True)
                    else:
                        last = t.matmul(k.ps_c[:, j, :], k.az[:, j, :], k.W["L2_gnn_W"], start=True, stop=True)
                if kind == "filter":
                    last.then_inc(s_z, 1)
                    pe.wait_ge(s_op, i + 1)
                    for j in range(J):
                        last = t.matmul(k.ps_c[:, j, :], k.z[:, j, :], k.W["L1_gnn_W_o2"], start=True, stop=True)
                last.then_inc(s_mm, 1)
            if kind != "last":
                every_group(pe, body)


def filter_edges(k, a, name, table, sums):
    nc = k.nc
    PAIR, pairs = 2 * P, -(-E // (2 * P))
    sb = k.own
    sidx = sb("sidx", [P, 2, 2], I32)
    numbers = sb("numbers", [P, 2, 2], I32)
    krow = sb("krow", [P, 2, PAIR], I32)
    rbf = sb("rbf", [P, 2, 2, R])
    rbf_t, h_t = sb("rbf_t", [R, 2, PAIR]), sb("h_t", [P, 2, PAIR])
    rows = sb("rows", [P, 2, 2, D])
    h, hf, z, soft, ssp, fw = (sb(x, [P, 2, 2, D]) for x in ("h", "hf", "z", "soft", "ssp", "fw"))
    same = sb("same", [P, 2, 2, PAIR])
    msg, summed = sb("msg", [P, 2, 2, W]), sb("summed", [P, 2, 2, W])
    stats, mv = sb("stats", [P, 2, 2, 6]), sb("mv", [P, 2, 2, 2])
    lnv, rstd, shift = (sb(x, [P, 2, 2]) for x in ("lnv", "rstd", "shift"))
    dup, tgt, spares = (sb(x, [P, 2]) for x in ("dup", "tgt", "spares"))
    junk, idle = sb("junk", [P, PAIR]), sb("idle", [P, 2])
    earlier = sb("earlier", [P, 2, PAIR])
    s_got = [k.lasting_sem(f"{name}_got{s}") for s in range(2)]
    s_add = k.lasting_sem(f"{name}_add")
    s_krow, s_rbf = [k.sem(f"{name}_krow{s}") for s in range(2)], [k.sem(f"{name}_rbf{s}") for s in range(2)]
    (s_free, s_numbers, s_chain, s_var, s_rstd, s_scale, s_h, s_turned, s_turned_sb, s_first, s_z, s_hf, s_lnz, s_act,
     s_ssp, s_second, s_fw, s_keys, s_msg, s_sums, s_summed, s_link, s_preset, s_filled, s_added, s_soft, s_copied) = (
        k.sem(f"{name}_{x}") for x in (
            "free", "numbers", "chain", "var", "rstd", "scale", "h", "turned", "turned_sb", "first", "z", "hf", "lnz", "act",
            "ssp", "second", "fw", "keys", "msg", "sums", "summed", "link", "preset", "filled", "added", "soft", "copied"))

    def pair(tile, s):
        return tile[:, s % 2, :, :]

    def bank(ps, s, at, n=PAIR):
        return ps[:, :, :].rearrange("p a b -> p (a b)")[:, 512 * (s % 2) + at:512 * (s % 2) + at + n]

    def uses(i, s, n):
        return (i - s % 2) * (8 * n) + 16 * n

    def known(i, least):
        return not isinstance(i, int) or i >= least

    def live(i):
        return not isinstance(i, int) or 0 <= i < pairs

    def every_round(eng, stages):
        def one(i, s):
            for n, stage in stages:
                if live(i - n):
                    stage(i - n, (s - n) % 2)
        for i in range(6):
            one(i, i % 2)
        with eng.Fori(3, pairs // 2 - 1) as u:
            for s in range(2):
                one(2 * u + s, s)
        for i in range(pairs - 2, pairs + 5):
            one(i, i % 2)

    with nc.Block() as block:
        @block.sync
        def _(sp):
            def radial(i, s):
                if known(i, 2):
                    sp.wait_ge(s_turned, i - 1)
                if isinstance(i, int) and i == pairs - 1:
                    lo = i * PAIR
                    sp.dma_start(rbf[0:E - lo, s, 0, :], a["edge_attr_20"][lo:E, :]).then_inc(s_rbf[s], 16)
                else:
                    sp.dma_start(pair(rbf, s), a["edge_attr_20"][bass.ds(i * PAIR, PAIR), :].rearrange("(q p) r -> p q r", p=P)).then_inc(s_rbf[s], 16)

            def keys(i, s):
                if known(i, 2):
                    sp.wait_ge(s_keys, i - 1)
                if isinstance(i, int) and i == pairs - 1:
                    sp.wait_ge(s_preset, 1)
                    lo = i * PAIR
                    sp.dma_start(krow[:, s, 0:E - lo], a["src"][lo:E].rearrange("(o n) -> o n", o=1).to_broadcast([P, E - lo])).then_inc(s_krow[s], 16)
                else:
                    sp.dma_start(krow[:, s, :], a["src"][bass.ds(i * PAIR, PAIR)].rearrange("(o n) -> o n", o=1).to_broadcast([P, PAIR])).then_inc(s_krow[s], 16)
            every_round(sp, ((0, radial), (2, keys)))

        @block.gpsimd
        def _(pool):
            pool.nop().then_inc(s_free, 2)

            def gather(i, s):
                take(pool, s_free, 1)
                pool.tensor_copy(numbers[:, s, :], k.dst_col[:, bass.ds(i * 2, 2)]).then_inc(s_numbers, 1)
                take(pool, s_numbers, 1)
                for q in range(2):
                    pool.indirect_dma_start(out=rows[:, s, q, :], out_offset=None, in_=table,
                                            in_offset=bass.IndirectOffsetOnAxis(ap=numbers[:, s, q:q + 1], axis=0)).then_inc(s_got[s], 16)

            def scatter(i, s):
                take(pool, s_summed, 1)
                for q in range(2):
                    pool.indirect_dma_start(out=sums, out_offset=bass.IndirectOffsetOnAxis(ap=sidx[:, s, q:q + 1], axis=0),
                                            in_=summed[:, s, q, :], in_offset=None, compute_op=ALU.add).then_inc(s_add, 16)

            def added(i, s):
                pool.wait_ge(s_add, 32 * (i + 1))
                pool.tensor_tensor(idle[:, 0:1], k.spare[:, :], k.spare[:, :], ALU.add).then_inc(s_added, 1)
                take(pool, s_added, 1)

            every_round(pool, ((5, scatter), (0, gather), (5, added)))

        @block.vector
        def _(dve):
            v = nc.vector
            link = Chain(dve, s_chain, 2)
            klink = Chain(dve, s_link, 8)

            def normalise(i, s):
                link.round(i)
                dve.wait_ge(s_got[s], uses(i, s, 2))
                v.tensor_tensor(idle[:, 1:2], k.spare[:, :], k.spare[:, :], ALU.add)
                for q in range(2):
                    v.bn_stats(stats[:, s, q, :], rows[:, s, q, :]).then_inc(s_chain, 1)
                link.k += 2
                dve.wait_ge(s_chain, link.base + link.k)
                v.tensor_tensor(idle[:, 1:2], k.spare[:, :], k.spare[:, :], ALU.add)
                v.bn_aggr(mv[:, s, 0, :], stats[:, s, 0, :])
                v.bn_aggr(mv[:, s, 1, :], stats[:, s, 1, :]).then_inc(s_var, 1)
                dve.wait_ge(s_rstd, i + 1)
                v.scalar_tensor_tensor(shift[:, s, :], mv[:, s, :, 0], -1.0, rstd[:, s, :], ALU.mult, ALU.mult).then_inc(s_scale, 1)
                link.end()

            def hidden(i, s):
                dve.wait_ge(s_first, i + 1)
                v.tensor_scalar(pair(z, s), bank(k.ps_b, s, 0).rearrange("p (q n) -> p q n", q=2), k.f1_bias[:, 0:1], 0.0, ALU.add, ALU.max).then_inc(s_z, 1)
                v.tensor_tensor(pair(hf, s), bank(k.ps_b, s, PAIR).rearrange("p (q n) -> p q n", q=2),
                                k.B["L1_gnn_b_in2f"].unsqueeze(1).to_broadcast([P, 2, D]), ALU.add).then_inc(s_hf, 1)

            def hidden_end(i, s):
                dve.wait_ge(s_act, i + 1)
                dve.wait_ge(s_z, i + 1)
                v.scalar_tensor_tensor(pair(ssp, s), pair(z, s), -LOG2, pair(soft, s), ALU.add, ALU.add).then_inc(s_ssp, 1)

            def keys(i, s):
                if isinstance(i, int) and i == pairs - 1:
                    v.memset(krow[:, s, :], -1).then_inc(s_preset, 1)
                klink.round(i)
                dve.wait_ge(s_krow[s], uses(i, s, 1))
                if known(i, 2):
                    dve.wait_ge(s_sums, i - 1)
                for q in range(2):
                    v.tensor_scalar(same[:, s, q, :], krow[:, s, :], k.add_col[:, bass.ds(i * 2 + q, 1)], None, ALU.is_equal).then_inc(s_link, 1)
                klink.k += 2
                dve.wait_ge(s_link, klink.base + klink.k)
                for q in range(2):
                    klink(v.tensor_tensor_reduce(out=junk[:, :], in0=same[:, s, q, :], in1=earlier[:, q, :], scale=1.0, scalar=0.0,
                                                 op0=ALU.mult, op1=ALU.add, accum_out=dup[:, q:q + 1]))
                key = k.add_col[:, bass.ds(i * 2, 2)]
                klink(v.tensor_scalar(dup[:, :], dup[:, :], 1.0, None, ALU.min))
                klink(v.tensor_tensor(tgt[:, :], spares[:, :], key, ALU.subtract))
                klink(v.tensor_tensor(tgt[:, :], tgt[:, :], dup[:, :], ALU.mult))
                klink(v.tensor_tensor(tgt[:, :], tgt[:, :], key, ALU.add))
                if known(i, 2):
                    dve.wait_ge(s_add, 32 * (i - 1))
                v.tensor_copy(sidx[:, s, :], tgt[:, :]).then_inc(s_keys, 1)
                klink.end()

            def messages(i, s):
                dve.wait_ge(s_second, i + 1)
                v.tensor_tensor(pair(fw, s), bank(k.ps_c, s, 0).rearrange("p (q n) -> p q n", q=2),
                                k.B["L1_gnn_b_f2"].unsqueeze(1).to_broadcast([P, 2, D]), ALU.add).then_inc(s_fw, 1)
                dve.wait_ge(s_fw, i + 1)
                for q in range(2):
                    made = v.scalar_tensor_tensor(msg[:, s, q, 0:D], fw[:, s, q, :], k.weight_col[:, bass.ds(i * 2 + q, 1)], hf[:, s, q, :], ALU.mult, ALU.mult)
                made.then_inc(s_msg, 1)

            v.memset(msg[:, :, :, D:W], 1.0)
            v.memset(earlier[:, 0, P:PAIR], 0.0)
            for q in range(2):
                v.tensor_scalar(spares[:, q:q + 1], k.spare[:, :], float(q * P), None, ALU.add)
            v.memset(earlier[:, 1, 0:P], 1.0)
            v.tensor_copy(earlier[:, 0, 0:P], k.tri[:, :]).then_inc(s_filled, 1)
            v.tensor_copy(earlier[:, 1, P:PAIR], k.tri[:, :]).then_inc(s_filled, 1)
            dve.wait_ge(s_filled, 2)

            every_round(dve, ((3, keys), (3, messages), (2, hidden), (0, normalise), (2, hidden_end)))

        @block.scalar
        def _(act):
            sc = nc.scalar

            def normalise(i, s):
                act.wait_ge(s_var, i + 1)
                sc.activation(lnv[:, s, :], mv[:, s, :, 1], ACT.Ln, bias=k.eps[:, 0:1]).then_inc(s_lnz, 1)
                act.wait_ge(s_lnz, i + 1)
                sc.activation(rstd[:, s, :], lnv[:, s, :], ACT.Exp, scale=-0.5).then_inc(s_rstd, 1)
                act.wait_ge(s_scale, i + 1)
                act.wait_ge(s_rstd, i + 1)
                if known(i, 2):
                    act.wait_ge(s_turned, i - 1)
                for q in range(2):
                    made = sc.activation(h[:, s, q, :], rows[:, s, q, :], ACT.Relu, bias=shift[:, s, q:q + 1], scale=rstd[:, s, q:q + 1])
                made.then_inc(s_h, 1)

            def turned(i, s):
                act.wait_ge(s_turned, i + 1)
                act.nop().then_inc(s_free, 1)
                if known(i, 2):
                    act.wait_ge(s_first, i - 1)
                sc.activation(rbf_t[:, s, :], bank(k.ps_a, s, PAIR)[0:R, :], ACT.Copy)
                sc.activation(h_t[:, s, :], bank(k.ps_a, s, 0), ACT.Copy).then_inc(s_turned_sb, 1)

            def soften(i, s):
                act.wait_ge(s_first, i + 1)
                act.wait_ge(s_z, i + 1)
                act.wait_ge(s_hf, i + 1)
                if known(i, 2):
                    act.wait_ge(s_ssp, i - 1)
                what = soft[:, s, :, :].rearrange("p q n -> p (q n)")
                sc.activation(what, bank(k.ps_b, s, 0), ACT.Abs, bias=k.f1_bias[:, 0:1]).then_inc(s_soft, 1)
                act.wait_ge(s_soft, 3 * i + 1)
                sc.activation(what, what, ACT.Exp, scale=-1.0).then_inc(s_soft, 1)
                act.wait_ge(s_soft, 3 * i + 2)
                sc.activation(what, what, ACT.Ln, bias=1.0).then_inc(s_act, 1)
                act.nop().then_inc(s_soft, 1)

            def copy_sums(i, s):
                act.wait_ge(s_sums, i + 1)
                act.wait_ge(s_keys, i + 1)
                if known(i, 2):
                    act.wait_ge(s_add, 32 * (i - 1))
                sc.activation(summed[:, s, :, :], k.ps_sum[:, s, 0:2 * W].rearrange("p (q w) -> p q w", q=2), ACT.Copy).then_inc(s_copied, 1)
                act.wait_ge(s_copied, i + 1)
                act.nop().then_inc(s_summed, 1)

            sc.preload_act_table_set("natural_log_exp_and_others")
            every_round(act, ((4, copy_sums), (2, soften), (1, turned), (0, normalise)))

        @block.tensor
        def _(pe):
            t = nc.tensor

            def turn(i, s):
                pe.wait_ge(s_h, i + 1)
                pe.wait_ge(s_rbf[s], uses(i, s, 1))
                if known(i, 2):
                    pe.wait_ge(s_turned_sb, i - 1)
                for q in range(2):
                    t.transpose(bank(k.ps_a, s, q * P, P), h[:, s, q, :], k.ident[:, :])
                    last = t.transpose(bank(k.ps_a, s, PAIR + q * P, P)[0:R, :], rbf[:, s, q, :], k.ident[:, :])
                last.then_inc(s_turned, 1)

            def first(i, s):
                pe.wait_ge(s_turned_sb, i + 1)
                if known(i, 2):
                    pe.wait_ge(s_act, i - 1)
                    pe.wait_ge(s_hf, i - 1)
                t.matmul(bank(k.ps_b, s, 0), k.f1_t[:, :], rbf_t[:, s, :], start=True, stop=True)
                for q in range(2):
                    last = t.matmul(bank(k.ps_b, s, PAIR + q * P, P), h_t[:, s, q * P:(q + 1) * P], k.W["L1_gnn_W_in2f"], start=True, stop=True)
                last.then_inc(s_first, 1)

            def second(i, s):
                pe.wait_ge(s_ssp, i + 1)
                if known(i, 2):
                    pe.wait_ge(s_fw, i - 1)
                for q in range(2):
                    last = t.matmul(bank(k.ps_c, s, q * P, P), ssp[:, s, q, :], k.W["L1_gnn_W_f2"], start=True, stop=True)
                last.then_inc(s_second, 1)

            def sum_equal(i, s):
                pe.wait_ge(s_msg, i + 1)
                pe.wait_ge(s_keys, i + 1)
                if known(i, 2):
                    pe.wait_ge(s_copied, i - 1)
                for q in range(2):
                    for c in range(2):
                        last = t.matmul(k.ps_sum[:, s, q * W:(q + 1) * W], same[:, s, c, q * P:(q + 1) * P], msg[:, s, c, :], start=(c == 0), stop=(c == 1))
                last.then_inc(s_sums, 1)

            every_round(pe, ((3, sum_equal), (1, first), (0, turn), (2, second)))


def filter_nodes(k, a, name, table, sums, out):
    nc = k.nc
    sb = k.own
    agg, x, y = sb("agg", [P, 4, T, W]), sb("x", [P, 4, T, D]), sb("y", [P, 2, T, W])
    agg_t, z, soft, ssp = (sb(n, [P, 2, T, P]) for n in ("agg_t", "z", "soft", "ssp"))
    degree, lnd = sb("degree", [P, 2, T]), sb("lnd", [P, 2, T])
    s_agg, s_x = [k.sem(f"{name}_agg{s}") for s in range(4)], [k.sem(f"{name}_x{s}") for s in range(4)]
    s_stored = [k.sem(f"{name}_stored{s}") for s in range(2)]
    (s_turned, s_agg_t, s_first, s_z, s_soft, s_act, s_ssp, s_second, s_biased, s_out, s_degree, s_lnd, s_root, s_pad) = (
        k.sem(f"{name}_{n}") for n in (
            "turned", "agg_t", "first", "z", "soft", "act", "ssp", "second", "biased", "out", "degree", "lnd", "root", "pad"))
    rest = N - (STEPS - 1) * T * P

    def bank(ps, s):
        return ps[:, T * (s % 2):T * (s % 2) + T, :]

    def flat(tile):
        return tile.rearrange("p t n -> p (t n)")

    def known(i, least):
        return not isinstance(i, int) or i >= least

    def live(i):
        return not isinstance(i, int) or 0 <= i < STEPS

    def uses(i, s, slots):
        return (i - s % slots) * (16 // slots) + 16 + (16 if isinstance(i, int) and i == STEPS - 1 else 0)

    def every_round(eng, stages):
        def one(i, s):
            for n, stage in stages:
                if live(i - n):
                    stage(i - n, (s - n) % 4)
        for i in range(8):
            one(i, i % 4)
        with eng.Fori(2, STEPS // 4 - 1) as u:
            for s in range(4):
                one(4 * u + s, s)
        for i in range(STEPS - 4, STEPS + 6):
            one(i, i % 4)

    def move(sp, tile, s, rows, i, sem, width, store=False):
        if isinstance(i, int) and i == STEPS - 1:
            lo = i * T * P
            parts = [(tile[:, s, 0, 0:width], rows[lo:lo + P, 0:width]), (tile[0:rest - P, s, 1, 0:width], rows[lo + P:N, 0:width])]
        else:
            parts = [(tile[:, s, :, 0:width], rows[bass.ds(i * T * P, T * P), 0:width].rearrange("(t p) w -> p t w", p=P))]
        for on_chip, dram in parts:
            sp.dma_start(*((dram, on_chip) if store else (on_chip, dram))).then_inc(sem, 16)

    with nc.Block() as block:
        @block.sync
        def _(sp):
            def load_sums(i, s):
                if known(i, 4):
                    sp.wait_ge(s_turned, i - 3)
                    sp.wait_ge(s_degree, i - 3)
                move(sp, agg, s, sums, i, s_agg[s], W)

            def load_x(i, s):
                if known(i, 4):
                    sp.wait_ge(s_out, i - 3)
                move(sp, x, s, table, i, s_x[s], D)

            def store(i, s):
                sp.wait_ge(s_out, i + 1)
                sp.wait_ge(s_root, i + 1)
                move(sp, y, s % 2, out, i, s_stored[s % 2], W, store=True)

            every_round(sp, ((0, load_sums), (2, load_x), (6, store)))
            sp.wait_ge(s_stored[0], 16 * (STEPS // 2))
            sp.wait_ge(s_stored[1], 16 * (STEPS // 2 + 1))

        @block.gpsimd
        def _(pool):
            def add_bias(i, s):
                take(pool, s_x[s], 32 if isinstance(i, int) and i == STEPS - 1 else 16)
                pool.tensor_tensor(x[:, s, :, :], x[:, s, :, :], k.B["L1_gnn_b_o2"].unsqueeze(1).to_broadcast([P, T, D]), ALU.add).then_inc(s_biased, 1)
            every_round(pool, ((0, add_bias),))

        @block.vector
        def _(dve):
            v = nc.vector

            def count(i, s):
                dve.wait_ge(s_agg[s], uses(i, s, 4))
                if known(i, 2):
                    dve.wait_ge(s_lnd, i - 1)
                v.tensor_scalar(degree[:, s % 2, :], agg[:, s, :, AUX], 1.0, 1.0, ALU.add, ALU.max).then_inc(s_degree, 1)

            def positive(i, s):
                dve.wait_ge(s_first, i + 1)
                v.tensor_scalar(flat(z[:, s % 2, :, :]), flat(bank(k.ps_b, s)), k.o1_bias[:, 0:1], 0.0, ALU.add, ALU.max).then_inc(s_z, 1)

            def soften(i, s):
                dve.wait_ge(s_act, i + 1)
                dve.wait_ge(s_z, i + 1)
                if known(i, 2):
                    dve.wait_ge(s_second, i - 1)
                v.scalar_tensor_tensor(ssp[:, s % 2, :, :], z[:, s % 2, :, :], -LOG2, soft[:, s % 2, :, :], ALU.add, ALU.add).then_inc(s_ssp, 1)

            def finish(i, s):
                dve.wait_ge(s_second, i + 1)
                dve.wait_ge(s_biased, i + 1)
                if known(i, 2):
                    dve.wait_ge(s_stored[s % 2], uses(i - 2, s, 2))
                v.tensor_tensor(y[:, s % 2, :, 0:D], bank(k.ps_c, s), x[:, s, :, :], ALU.add).then_inc(s_out, 1)

            v.memset(y[:, :, :, D:W], 0.0).then_inc(s_pad, 1)
            dve.wait_ge(s_pad, 1)
            every_round(dve, ((2, positive), (3, finish), (0, count), (2, soften)))

        @block.scalar
        def _(act):
            sc = nc.scalar

            def copy_sums(i, s):
                act.wait_ge(s_turned, i + 1)
                if known(i, 2):
                    act.wait_ge(s_first, i - 1)
                sc.activation(agg_t[:, s % 2, :, :], bank(k.ps_a, s), ACT.Copy).then_inc(s_agg_t, 1)

            def soften(i, s):
                what = flat(soft[:, s % 2, :, :])
                act.wait_ge(s_first, i + 1)
                act.wait_ge(s_z, i + 1)
                if known(i, 2):
                    act.wait_ge(s_ssp, i - 1)
                sc.activation(what, flat(bank(k.ps_b, s)), ACT.Abs, bias=k.o1_bias[:, 0:1]).then_inc(s_soft, 1)
                act.wait_ge(s_soft, 2 * i + 1)
                sc.activation(what, what, ACT.Exp, scale=-1.0).then_inc(s_soft, 1)
                act.wait_ge(s_soft, 2 * i + 2)
                sc.activation(what, what, ACT.Ln, bias=1.0).then_inc(s_act, 1)

            def log_degree(i, s):
                act.wait_ge(s_degree, i + 1)
                if known(i, 2):
                    act.wait_ge(s_root, i - 1)
                sc.activation(lnd[:, s % 2, :], degree[:, s % 2, :], ACT.Ln).then_inc(s_lnd, 1)

            def root(i, s):
                act.wait_ge(s_pad, 1)
                act.wait_ge(s_lnd, i + 1)
                if known(i, 2):
                    act.wait_ge(s_stored[s % 2], uses(i - 2, s, 2))
                sc.activation(y[:, s % 2, :, AUX], lnd[:, s % 2, :], ACT.Exp, scale=-0.5).then_inc(s_root, 1)
            sc.preload_act_table_set("natural_log_exp_and_others")
            every_round(act, ((1, copy_sums), (2, soften), (3, root), (1, log_degree)))

        @block.tensor
        def _(pe):
            t = nc.tensor

            def turn(i, s):
                pe.wait_ge(s_agg[s], uses(i, s, 4))
                if known(i, 2):
                    pe.wait_ge(s_agg_t, i - 1)
                for j in range(T):
                    last = t.transpose(bank(k.ps_a, s)[:, j, :], agg[:, s, j, 0:D], k.ident[:, :])
                last.then_inc(s_turned, 1)

            def first(i, s):
                pe.wait_ge(s_agg_t, i + 1)
                if known(i, 2):
                    pe.wait_ge(s_act, i - 1)
                t.matmul(flat(bank(k.ps_b, s)), k.W["L1_gnn_W_o1"], flat(agg_t[:, s % 2, :, :]), start=True, stop=True).then_inc(s_first, 1)

            def second(i, s):
                pe.wait_ge(s_ssp, i + 1)
                if known(i, 2):
                    pe.wait_ge(s_out, i - 1)
                for j in range(T):
                    last = t.matmul(bank(k.ps_c, s)[:, j, :], ssp[:, s % 2, j, :], k.W["L1_gnn_W_o2"], start=True, stop=True)
                last.then_inc(s_second, 1)
            every_round(pe, ((3, second), (1, first), (0, turn)))


def plan_pass(k, a):
    nc = k.nc
    s_load, s_set, s_rows, s_tp, s_col = (k.sem(f"plan_{x}") for x in ("load", "set", "rows", "tp", "col"))
    s_hot, s_hist, s_link, s_tot, s_first, s_place = (k.sem(f"plan_{x}") for x in ("hot", "hist", "link", "tot", "first", "place"))
    C = -(-BLOCKS // P)
    psa, psb = k.ps_a[:, :, :].rearrange("p a b -> p (a b)"), k.ps_b[:, :, :].rearrange("p a b -> p (a b)")
    halves = [(0, 512), (512, TILES)]
    names = ["dst", "src", "edge_weight"]
    if True:
        sb = k.own
        raw = sb("key_rows", [P, C, P], I32)
        nxt = sb("next_rows", [P, C, P], I32)
        srow = sb("src_rows", [P, C, P], I32)
        arow, arow_f = sb("add_rows", [P, C, P], I32), sb("arow_f", [P, C, P])
        wrow = sb("weight_rows", [P, C, P])
        rows_f, srow_f, late = sb("rows_f", [P, C, P]), sb("srow_f", [P, C, P]), sb("late", [P, C, P])
        key_col = sb("key_col", [P, C * P], I32)
        hi_i, lo_i = sb("hi_i", [P, C * P], I32), sb("lo_i", [P, C * P], I32)
        hi, lo = sb("hi", [P, C * P]), sb("lo", [P, C * P])
        tile_i, tile_no = sb("tile_i", [P, TILES], I32), sb("tile_no", [P, TILES])
        tile_h, lane_h = sb("tile_h", [P, TILES], F16), sb("lane_h", [P, P], F16)
        hot_hi, hot_lo = sb("hot_hi", [P, 2, TILES], BF16), sb("hot_lo", [P, 2, P], BF16)
        start, b0i, b0, lasti, last = sb("start", [P, TILES + 1]), sb("b0i", [P, TILES], I32), sb("b0", [P, TILES]), sb("lasti", [P, TILES], I32), sb("last", [P, TILES])
        base_i, base, bad = sb("base_i", [P, TILES], I32), sb("base", [P, TILES]), sb("bad", [P, TILES])
        ones, total, junk = sb("ones", [P, P]), sb("total", [P, 4]), sb("plan_junk", [P, TILES])
        part_i, part = sb("part_i", [P, C], I32), sb("part", [P, C])
        at_block = sb("at_block", [P, C, B, TILES])
        slot_i = sb("slot_i", [P, TILES], I32)

        with nc.Block() as block:
            @block.sync
            def _(sp):
                sp.wait_ge(s_set, 5)
                full = FULL // P
                for tile, ap in ((raw, a["dst"]), (srow, a["src"]), (wrow, a["edge_weight"]), (arow, a["src"]), (nxt, a["dst"][1:E])):
                    rest = ap.shape[0] - FULL * P
                    sp.dma_start(tile[:, 0:full, :], ap[0:full * P * P].rearrange("(c b e) -> b c e", b=P, e=P)).then_inc(s_load, 16)
                    sp.dma_start(tile[0:FULL - full * P, full, :], ap[full * P * P:FULL * P].rearrange("(b e) -> b e", e=P)).then_inc(s_load, 16)
                    sp.dma_start(tile[FULL - full * P:FULL - full * P + 1, full, 0:rest],
                                 ap[FULL * P:FULL * P + rest].rearrange("(o n) -> o n", o=1)).then_inc(s_load, 16)

            @block.gpsimd
            def _(pool):
                pool.memset(raw[:, :, :], -1).then_inc(s_set, 1)
                pool.memset(srow[:, :, :], 0).then_inc(s_set, 1)
                pool.memset(wrow[:, :, :], 0.0).then_inc(s_set, 1)
                pool.memset(nxt[:, :, :], N).then_inc(s_set, 1)
                pool.iota(arow[:, :, :], [[0, C], [1, P]], base=N, channel_multiplier=0).then_inc(s_set, 1)
                pool.memset(ones[:, :], 1.0)
                pool.iota(tile_i[:, :], [[1, TILES]], base=0, channel_multiplier=0).then_inc(s_rows, 1)
                pool.iota(k.lane_i[:, :], [[1, P]], base=0, channel_multiplier=0).then_inc(s_rows, 1)
                pool.iota(part_i[:, :], [[P, C]], base=0, channel_multiplier=1).then_inc(s_rows, 1)

            @block.vector
            def _(dve):
                v = nc.vector
                link = Chain(dve, s_link, None)
                dve.wait_ge(s_rows, 3)
                link(v.tensor_copy(tile_no[:, :], tile_i[:, :]))
                link(v.tensor_copy(tile_h[:, :], tile_no[:, :]))
                link(v.tensor_copy(k.lane[:, :], k.lane_i[:, :]))
                link(v.tensor_copy(lane_h[:, :], k.lane[:, :]))
                link(v.tensor_copy(part[:, :], part_i[:, :]))
                link(v.tensor_scalar(base_i[:, :], tile_i[:, :], 2, 1, ALU.logical_shift_right, ALU.logical_shift_left))
                link(v.tensor_copy(base[:, :], base_i[:, :]))
                dve.wait_ge(s_load, 16 * 15)
                link(v.tensor_copy(rows_f[:, :, :], raw[:, :, :]))
                link(v.tensor_copy(srow_f[:, :, :], srow[:, :, :]))
                link(v.tensor_copy(arow_f[:, :, :], arow[:, :, :]))
                link(v.tensor_copy(late[:, :, :], nxt[:, :, :]))
                v.tensor_tensor(late[:, :, :], late[:, :, :], rows_f[:, :, :], ALU.is_lt).then_inc(s_col, 1)
                dve.wait_ge(s_col, 1)
                link(v.tensor_reduce(total[:, 0:1], late[:, :, :].rearrange("p c e -> p (c e)"), op=ALU.add, axis=AX.X))
                for n, tile in enumerate((key_col, k.src_col, k.weight_col, k.add_col)):
                    dve.wait_ge(s_tp, n + 1)
                    v.tensor_copy(tile[:, :], psa[:, 0:C * P]).then_inc(s_col, 1)
                    dve.wait_ge(s_col, n + 2)
                link(v.tensor_scalar(k.add_col[:, BLOCKS - 1:BLOCKS], k.spare[:, :], float(P), None, ALU.add))
                link(v.tensor_scalar(k.dst_col[:, :], key_col[:, :], 0, None, ALU.max))
                link(v.tensor_scalar(hi_i[:, :], key_col[:, :], 7, None, ALU.arith_shift_right))
                link(v.tensor_scalar(lo_i[:, :], key_col[:, :], P - 1, None, ALU.bitwise_and))
                link(v.tensor_copy(hi[:, :], hi_i[:, :]))
                link(v.tensor_copy(lo[:, :], lo_i[:, :]))

                def hot(b, s):
                    v.tensor_scalar(hot_hi[:, s, :], tile_h[:, :], hi[:, bass.ds(b, 1)], None, ALU.is_equal)
                    v.tensor_scalar(hot_lo[:, s, :], lane_h[:, :], lo[:, bass.ds(b, 1)], None, ALU.is_equal).then_inc(s_hot, 1)
                hot(0, 0)
                hot(1, 1)
                with dve.Fori(1, BLOCKS // 2) as u:
                    for s in range(2):
                        dve.wait_ge(s_hist, 2 * u + s - 1)
                        hot(2 * u + s, s)
                dve.wait_ge(s_hist, BLOCKS)
                link(v.tensor_copy(k.degree[:, :], psb[:, 0:TILES]))
                link(v.tensor_scalar(k.count[:, :], k.degree[:, :], 1.0, None, ALU.max))
                v.reciprocal(k.inverse[:, :], k.count[:, :]).then_inc(s_tot, 1)
                dve.wait_ge(s_first, 1)
                link(v.memset(start[:, 0:1], 0.0))
                link(v.memset(junk[:, :], 0.0))
                link(v.tensor_tensor_scan(start[:, 1:TILES + 1], psa[:, 0:TILES], junk[:, :], 0.0, ALU.add, ALU.add))
                link(v.tensor_copy(b0i[:, :], start[:, 0:TILES]))
                link(v.tensor_scalar(b0i[:, :], b0i[:, :], 7, None, ALU.arith_shift_right))
                link(v.tensor_copy(b0[:, :], b0i[:, :]))
                link(v.tensor_scalar(last[:, :], start[:, 1:TILES + 1], -1.0, None, ALU.add))
                link(v.tensor_copy(lasti[:, :], last[:, :]))
                link(v.tensor_scalar(lasti[:, :], lasti[:, :], 7, None, ALU.arith_shift_right))
                link(v.tensor_copy(last[:, :], lasti[:, :]))
                link(v.tensor_tensor(last[:, :], last[:, :], b0[:, :], ALU.subtract))
                link(v.tensor_scalar(bad[:, :], last[:, :], 1.0, None, ALU.is_gt))
                link(v.tensor_reduce(total[:, 1:2], bad[:, :], op=ALU.add, axis=AX.X))
                link(v.tensor_tensor(last[:, :], b0[:, :], base[:, :], ALU.subtract))
                link(v.tensor_scalar(bad[:, :], last[:, :], float(-WINDOW), None, ALU.is_lt))
                link(v.tensor_reduce(total[:, 2:3], bad[:, :], op=ALU.add, axis=AX.X))
                link(v.tensor_scalar(bad[:, :], last[:, :], float(WINDOW - 2), None, ALU.is_gt))
                link(v.tensor_reduce(total[:, 3:4], bad[:, :], op=ALU.add, axis=AX.X))
                for q in range(B):
                    link(v.tensor_scalar(last[:, :], b0[:, :], float(q), None, ALU.add))
                    link(v.tensor_copy(slot_i[:, :], last[:, :]))
                    link(v.tensor_scalar(slot_i[:, :], slot_i[:, :], RING - 1, 7, ALU.bitwise_and, ALU.logical_shift_left))
                    link(v.tensor_copy(k.slots[:, :].rearrange("o (t q) -> o t q", q=B)[:, :, q], slot_i[0:1, :]))
                for c in range(C):
                    for q in range(B):
                        link(v.tensor_scalar(at_block[:, c, q, :], b0[:, :], part[:, c:c + 1], float(q), ALU.subtract, ALU.add))
                        link(v.tensor_scalar(at_block[:, c, q, :], at_block[:, c, q, :], 0.0, None, ALU.is_equal))
                link(v.tensor_scalar(base[:, :], tile_no[:, :], float(P), None, ALU.mult))
                v.memset(junk[:, 0:1], 0.0).then_inc(s_tot, 1)
                for q, ps in enumerate((psa, psb)):
                    dve.wait_ge(s_place, q + 1)
                    link(v.tensor_tensor(k.place[:, :].rearrange("p (t q) -> p t q", q=B)[:, :, q], ps[:, 0:TILES], base[:, :], ALU.subtract))
                dve.wait_ge(s_place, 3)
                link(v.tensor_reduce(total[:, 0:1], k.ps_c[:, 0, 0:4], op=ALU.add, axis=AX.X))
                link(v.tensor_scalar(total[:, 0:1], total[:, 0:1], 0.0, None, ALU.is_gt))
                link(v.tensor_copy(k.paths[:, 1:2], total[0:1, 0:1]))
                link(v.tensor_scalar(total[:, 0:1], total[:, 0:1], -1.0, 1.0, ALU.mult, ALU.add))
                link(v.tensor_copy(k.paths[:, 0:1], total[0:1, 0:1]))

            @block.tensor
            def _(pe):
                t = nc.tensor
                pe.wait_ge(s_set, 4)
                for n, tile in enumerate((rows_f, srow_f, wrow, arow_f)):
                    pe.wait_ge(s_col, n + 1)
                    for c in range(C):
                        turned = t.transpose(psa[:, c * P:(c + 1) * P], tile[:, c, :], k.ident[:, :])
                    turned.then_inc(s_tp, 1)

                def count(b, s, start=False, stop=False):
                    pe.wait_ge(s_hot, b + 1)
                    for m, n in halves:
                        counted = t.matmul(psb[:, m:n], hot_lo[:, s, :], hot_hi[:, s, m:n], start=start, stop=stop)
                    counted.then_inc(s_hist, 1)
                count(0, 0, True)
                count(1, 1)
                with pe.Fori(1, BLOCKS // 2 - 1) as u:
                    for s in range(2):
                        count(2 * u + s, s)
                count(BLOCKS - 2, 0)
                count(BLOCKS - 1, 1, stop=True)
                pe.wait_ge(s_tot, 1)
                for m, n in halves:
                    summed = t.matmul(psa[:, m:n], ones[:, :], k.degree[:, m:n], start=True, stop=True)
                summed.then_inc(s_first, 1)
                pe.wait_ge(s_tot, 2)
                for q, ps in enumerate((psa, psb)):
                    for m, n in halves:
                        for c in range(C):
                            placed = t.matmul(ps[:, m:n], rows_f[:, c, :], at_block[:, c, q, m:n], start=(c == 0), stop=(c == C - 1))
                    placed.then_inc(s_place, 1)
                t.matmul(k.ps_c[:, 0, 0:4], ones[:, :], total[:, :], start=True, stop=True).then_inc(s_place, 1)


def sorted_pass(k, a, name, kind, table, out):
    nc = k.nc
    sorted_buffers(k)
    ring_w = B * D
    sum_lag = 3 if kind in ("first", "mid") else 2
    norm_edges, norm_nodes, weighted = kind != "mid", kind in ("first", "last"), kind == "linear"
    two_products, edge_product = kind in ("first", "mid"), kind != "last"
    residual = {"mid": a["x"], "last": table}.get(kind)
    in_w, out_w = table.shape[1], out.shape[1]
    s_x = [k.sem(f"{name}_x{s}") for s in range(4)]
    s_res = [k.sem(f"{name}_res{s}") for s in range(4)]
    s_got = [k.lasting_sem(f"{name}_got{s}") for s in range(4)]
    s_stored = [k.sem(f"{name}_stored{s}") for s in range(4)]
    (s_stage, s_numbers, s_elink, s_evar, s_estd, s_escale, s_relu, s_eturned, s_plain_t, s_eproduct, s_edges,
     s_nlink, s_nvar, s_nstd, s_nscale, s_h, s_select, s_turned, s_h_t, s_product, s_pre, s_out, s_elink2, s_nlink2) = (
        k.sem(f"{name}_{x}") for x in (
            "stage", "numbers", "edge_link", "edge_var", "edge_std", "edge_scale", "relu", "edge_turned", "plain_t",
            "edge_product", "edges", "node_link", "node_var", "node_std", "node_scale", "h", "select", "turned", "h_t",
            "product", "pre", "out", "edge_link2", "node_link2"))
    weight = {"first": "L0_gnn_W_conv0", "mid": "L0_gnn_W_conv1", "linear": "L2_gnn_W", "last": None}[kind]
    own_weight = {"first": "L0_gnn_W_lin0", "mid": "L0_gnn_W_lin1"}.get(kind)
    bias = {"first": k.B["L0_0"], "mid": k.B["L0_1"], "linear": k.B["L2_gnn_b"], "last": None}[kind]
    rest = N - (STEPS - 1) * T * P

    def bank(ps, s):
        return ps[:, T * (s % 2):T * (s % 2) + T, :]

    def in_ring(e, q, n):
        return bass.ds(e % (RING // B) * ring_w + q * D, n * D)

    def uses(i, s, slots, n):
        return (i - s % slots) * (16 * n // slots) + 16 * n

    def uses_last(i, s):
        return uses(i, s, 4, 1) + (16 if isinstance(i, int) and i == STEPS - 1 else 0)

    def known(i, least):
        return not isinstance(i, int) or i >= least

    def live(e):
        return not isinstance(e, int) or 0 <= e < STEPS

    def every_round(eng, edge_stages, node_stages):
        def one(r, s):
            for n, stage in node_stages:
                if live(r - AHEAD - n):
                    stage(r - AHEAD - n, (s - n) % 4)
            for n, stage in edge_stages:
                if live(r - n):
                    stage(r - n, (s - n) % 4)
        for r in range(16):
            one(r, r % 4)
        with eng.Fori(4, STEPS // 4) as u:
            for s in range(4):
                one(4 * u + s, s)
        for r in range(STEPS, STEPS + AHEAD + 7):
            one(r, r % 4)

    with nc.Block() as block:
        @block.sync
        @k.only("sorted")
        def _(sp):
            def move(tile, s, rows, i, sem, width, store=False):
                if isinstance(i, int) and i == STEPS - 1:
                    lo = i * T * P
                    parts = [(tile[:, s, 0, 0:width], rows[lo:lo + P, 0:width]), (tile[0:rest - P, s, 1, 0:width], rows[lo + P:N, 0:width])]
                else:
                    parts = [(tile[:, s, :, 0:width], rows[bass.ds(i * T * P, T * P), 0:width].rearrange("(t p) w -> p t w", p=P))]
                for on_chip, dram in parts:
                    sp.dma_start(*((dram, on_chip) if store else (on_chip, dram))).then_inc(sem, 16)

            def load_x(i, s):
                if known(i, 4):
                    sp.wait_ge(s_out if kind == "linear" else s_h, i - 3)
                move(k.x, s, table, i, s_x[s], in_w)

            def load_residual(i, s):
                if known(i, 4):
                    sp.wait_ge(s_out, i - 3)
                move(k.res4, s, residual, i, s_res[s], residual.shape[1])

            def store(i, s):
                sp.wait_ge(s_out, i + 1)
                move(k.y, s, out, i, s_stored[s], out_w, store=True)

            stages = [(5, store), (0 if kind == "linear" else -3, load_x)]
            if residual is not None:
                stages.append((0, load_residual))
            every_round(sp, (), stages)
            for s in range(4):
                sp.wait_ge(s_stored[s], uses((STEPS - 4) + s, s, 4, 1) + 16 * (s == 3))

        @block.gpsimd
        @k.only("sorted")
        def _(pool):
            pool.nop().then_inc(s_stage, 4)

            def gather(e, s):
                take(pool, s_stage, 1)
                pool.tensor_copy(k.numbers[:, s, :], k.src_col[:, bass.ds(e * B, B)]).then_inc(s_numbers, 1)
                take(pool, s_numbers, 1)
                for q in range(B):
                    pool.indirect_dma_start(out=k.stage[:, s, q, 0:in_w], out_offset=None, in_=table,
                                            in_offset=bass.IndirectOffsetOnAxis(ap=k.numbers[:, s, q:q + 1], axis=0)).then_inc(s_got[s], 16)
            with pool.Fori(0, STEPS // 4) as u:
                for s in range(4):
                    gather(4 * u + s, s)

        @block.vector
        @k.only("sorted")
        def _(dve):
            v = nc.vector
            elink, elink2 = Chain(dve, s_elink, B), Chain(dve, s_elink2, 1 + (kind == "last"))
            nlink, nlink2 = Chain(dve, s_nlink, T), Chain(dve, s_nlink2, 2)

            def spread(link, rows, n, stats, mv, sem, column):
                for j in range(n):
                    v.bn_stats(stats[:, j, :], rows[:, j, 0:D]).then_inc(link.sem, 1)
                link.k += n
                dve.wait_ge(link.sem, link.base + link.k)
                v.tensor_tensor(k.idle[:, column:column + 1], k.lane[:, 0:1], k.lane[:, 0:1], ALU.add)
                for j in range(n):
                    aggregated = v.bn_aggr(mv[:, j, :], stats[:, j, :])
                aggregated.then_inc(sem, 1)

            def edge_stats(e, s):
                o = s % 2
                elink.round(e)
                dve.wait_ge(s_got[s], uses(e, s, 4, B))
                v.tensor_tensor(k.idle[:, 0:1], k.lane[:, 0:1], k.lane[:, 0:1], ALU.add)
                spread(elink, k.stage[:, s, :, :], B, k.estats[:, o, :, :], k.emv[:, o, :, :], s_evar, 1)

            def edge_scale(e, s):
                o = s % 2
                elink2.round(e)
                dve.wait_ge(s_estd, e + 1)
                elink2(v.reciprocal(k.erstd[:, o, :], k.estd[:, o, :]))
                if kind == "last":
                    elink2(v.tensor_tensor(k.erstd[:, o, :], k.erstd[:, o, :], k.stage[:, s, :, AUX], ALU.mult))
                v.scalar_tensor_tensor(k.eshift[:, o, :], k.emv[:, o, :, 0], -1.0, k.erstd[:, o, :], ALU.mult, ALU.mult).then_inc(s_escale, 1)
                elink2.end()

            def select(i, s):
                if known(i, 2):
                    dve.wait_ge(s_product, i - 1)
                v.tensor_tensor(k.select[:, s % 2, :, :], k.lane[:, :].unsqueeze(1).to_broadcast([P, T * B, P]),
                                k.place[:, bass.ds(i * T * B, T * B)].unsqueeze(2).to_broadcast([P, T * B, P]),
                                ALU.is_equal).then_inc(s_select, 1)

            def node_stats(i, s):
                dve.wait_ge(s_x[s], uses_last(i, s))
                v.tensor_tensor(k.idle[:, 2:3], k.lane[:, 0:1], k.lane[:, 0:1], ALU.add)
                nlink.round(i)
                spread(nlink, k.x[:, s, :, :], T, k.nstats[:, s % 2, :, :], k.nmv[:, s % 2, :, :], s_nvar, 3)

            def node_scale(i, s):
                o = s % 2
                nlink2.round(i)
                dve.wait_ge(s_nstd, i + 1)
                nlink2(v.reciprocal(k.nrstd[:, o, :], k.nstd[:, o, :]))
                factor = k.x[:, s, :, AUX] if kind == "last" else k.count[:, bass.ds(i * T, T)]
                nlink2(v.tensor_tensor(k.nrstd[:, o, :], k.nrstd[:, o, :], factor, ALU.mult))
                v.scalar_tensor_tensor(k.nshift[:, o, :], k.nmv[:, o, :, 0], -1.0, k.nrstd[:, o, :], ALU.mult, ALU.mult).then_inc(s_nscale, 1)
                nlink2.end()

            def finish(i, s):
                y, rows = k.y[:, s, :, :], bank(k.ps_c, s)
                dve.wait_ge(s_product, i + 1)
                if known(i, 4):
                    dve.wait_ge(s_stored[s], uses(i - 4, s, 4, 1))
                if two_products:
                    for j in range(T):
                        pre = v.scalar_tensor_tensor(y[:, j, 0:D], rows[:, j, :], k.inverse[:, bass.ds(i * T + j, 1)], bias, ALU.mult, ALU.add)
                    pre.then_inc(s_pre, 1)
                if residual is not None:
                    dve.wait_ge(s_res[s], uses_last(i, s))
                if kind == "mid":
                    dve.wait_ge(s_pre, i + 1)
                    v.tensor_tensor(y[:, :, 0:D], y[:, :, 0:D], k.res4[:, s, :, 0:D], ALU.add).then_inc(s_out, 1)
                if kind == "linear":
                    dve.wait_ge(s_x[s], uses_last(i, s))
                    v.tensor_copy(y[:, :, D:W], k.x[:, s, :, D:W])
                    v.tensor_tensor(y[:, :, 0:D], rows, bias.unsqueeze(1).to_broadcast([P, T, D]), ALU.add).then_inc(s_pre, 1)
                    dve.wait_ge(s_pre, i + 1)
                    v.tensor_tensor(y[:, :, 0:D], y[:, :, 0:D], k.x[:, s, :, 0:D], ALU.add).then_inc(s_out, 1)
                if kind == "last":
                    for j in range(T):
                        done = v.scalar_tensor_tensor(y[:, j, 0:D], rows[:, j, :], k.res4[:, s, j, AUX:AUX + 1], k.res4[:, s, j, 0:D], ALU.mult, ALU.add)
                    done.then_inc(s_out, 1)

            edge_stages = [(1, edge_scale), (0, edge_stats)] if norm_edges else []
            node_stages = [(1, node_scale)] * norm_nodes + [(sum_lag - 1, select), (sum_lag + 1, finish)] + [(0, node_stats)] * norm_nodes
            every_round(dve, edge_stages, node_stages)

        @block.scalar
        @k.only("sorted")
        def _(act):
            sc = nc.scalar

            def edge_root(e, s):
                act.wait_ge(s_evar, e + 1)
                sc.activation(k.estd[:, s % 2, :], k.emv[:, s % 2, :, 1], ACT.Sqrt, bias=k.eps[:, 0:1]).then_inc(s_estd, 1)

            def edge_relu(e, s):
                o = s % 2
                act.wait_ge(s_escale, e + 1)
                if edge_product and known(e, 2):
                    act.wait_ge(s_eturned, e - 1)
                for q in range(B):
                    message = k.plain[:, o, q, :] if edge_product else k.ring[:, in_ring(e, q, 1)]
                    made = sc.activation(message, k.stage[:, s, q, 0:D], ACT.Relu, bias=k.eshift[:, o, q:q + 1], scale=k.erstd[:, o, q:q + 1])
                made.then_inc(s_relu if edge_product else s_edges, 1)
                sc.activation(k.idle3[:, :], k.eps[:, :], ACT.Copy).then_inc(s_stage, 1)

            def edge_turned(e, s):
                o = s % 2
                act.wait_ge(s_eturned, e + 1)
                if not norm_edges:
                    act.nop().then_inc(s_stage, 1)
                if known(e, 2):
                    act.wait_ge(s_eproduct, e - 1)
                sc.activation(k.plain_t[:, o, :, :], bank(k.ps_b, o)[:, 0:B, :], ACT.Copy).then_inc(s_plain_t, 1)

            def into_ring(e, s):
                o = s % 2
                act.wait_ge(s_eproduct, e + 1)
                if weighted:
                    for q in range(B):
                        made = sc.activation(k.ring[:, in_ring(e, q, 1)], k.ps_sum[:, o, q * D:(q + 1) * D], ACT.Copy,
                                             scale=k.weight_col[:, bass.ds(e * B + q, 1)])
                else:
                    made = sc.activation(k.ring[:, in_ring(e, 0, B)], k.ps_sum[:, o, 0:B * D], ACT.Copy)
                made.then_inc(s_edges, 1)

            def node_root(i, s):
                act.wait_ge(s_nvar, i + 1)
                sc.activation(k.nstd[:, s % 2, :], k.nmv[:, s % 2, :, 1], ACT.Sqrt, bias=k.eps[:, 0:1]).then_inc(s_nstd, 1)

            def node_rows(i, s):
                o = s % 2
                if norm_nodes:
                    act.wait_ge(s_nscale, i + 1)
                else:
                    act.wait_ge(s_x[s], uses_last(i, s))
                if known(i, 2):
                    act.wait_ge(s_turned if two_products else s_product, i - 1)
                for j in range(T):
                    if norm_nodes:
                        made = sc.activation(k.h[:, o, j, :], k.x[:, s, j, 0:D], ACT.Relu, bias=k.nshift[:, o, j:j + 1], scale=k.nrstd[:, o, j:j + 1])
                    else:
                        made = sc.activation(k.h[:, o, j, :], k.x[:, s, j, 0:D], ACT.Copy, scale=k.count[:, bass.ds(i * T + j, 1)])
                made.then_inc(s_h, 1)

            def node_turned(i, s):
                act.wait_ge(s_turned, i + 1)
                if known(i, 2):
                    act.wait_ge(s_product, i - 1)
                sc.activation(k.h_t2[:, s % 2, :, :], bank(k.ps_a, s), ACT.Copy).then_inc(s_h_t, 1)

            def rectify(i, s):
                y = k.y[:, s, :, 0:D]
                act.wait_ge(s_pre, i + 1)
                sc.activation(y, y, ACT.Relu).then_inc(s_out, 1)

            edge_stages = [(4, into_ring), (2, edge_turned)] * edge_product + [(1, edge_relu), (0, edge_root)] * norm_edges
            node_stages = ([(2, node_turned)] * two_products + [(1, node_rows)] * (kind != "linear") + [(5, rectify)] * (kind == "first")
                           + [(0, node_root)] * norm_nodes)
            every_round(act, edge_stages, node_stages)

        @block.tensor
        @k.only("sorted")
        def _(pe):
            t = nc.tensor

            def edge_turn(e, s):
                o = s % 2
                if norm_edges:
                    pe.wait_ge(s_relu, e + 1)
                else:
                    pe.wait_ge(s_got[s], uses(e, s, 4, B))
                if known(e, 2):
                    pe.wait_ge(s_plain_t, e - 1)
                for q in range(B):
                    rows = k.plain[:, o, q, :] if norm_edges else k.stage[:, s, q, 0:D]
                    last = t.transpose(bank(k.ps_b, o)[:, q, :], rows, k.ident[:, :])
                last.then_inc(s_eturned, 1)

            def edge_weigh(e, s):
                o = s % 2
                pe.wait_ge(s_plain_t, e + 1)
                if known(e, 2):
                    pe.wait_ge(s_edges, e - 1)
                for q in range(B):
                    last = t.matmul(k.ps_sum[:, o, q * D:(q + 1) * D], k.plain_t[:, o, q, :], k.W[weight], start=True, stop=True)
                last.then_inc(s_eproduct, 1)

            def node_turn(i, s):
                pe.wait_ge(s_h, i + 1)
                if known(i, 2):
                    pe.wait_ge(s_h_t, i - 1)
                for j in range(T):
                    last = t.transpose(bank(k.ps_a, s)[:, j, :], k.h[:, s % 2, j, :], k.ident[:, :])
                last.then_inc(s_turned, 1)

            def sums(i, s):
                where, o = bank(k.ps_c, s), s % 2
                _, places = nc.values_load_multi_w_load_instructions(
                    k.slots[0:1, bass.ds(i * T * B, T * B)], engines=[mybir.EngineType.PE], min_val=0,
                    max_val=(RING - 1) * D, skip_runtime_bounds_check_because="a remainder by the ring's size, times a row")
                if known(i, 2):
                    pe.wait_ge(s_pre if kind == "first" else s_out, i - 1)
                if kind == "last":
                    pe.wait_ge(s_h, i + 1)
                    t.matmul(where, k.ident[:, :], k.h[:, o, :, :], start=True, stop=False, skip_group_check=True)
                if two_products:
                    pe.wait_ge(s_h_t, i + 1)
                pe.wait_ge(s_select, i + 1)
                pe.wait_ge(s_edges, i + LEAD if not isinstance(i, int) else min(i + LEAD, STEPS))
                for j in range(T):
                    if two_products:
                        t.matmul(where[:, j, :], k.h_t2[:, o, j, :], k.W[own_weight], start=True, stop=False)
                    for q in range(B):
                        last = t.matmul(where[:, j, :], k.select[:, o, j * B + q, :], k.ring[:, bass.ds(places[j * B + q], D)],
                                        start=(kind == "linear" and q == 0),
                                        stop=(q == B - 1 and (kind != "last" or j == T - 1)), skip_group_check=kind == "last")
                last.then_inc(s_product, 1)

            every_round(pe, [(3, edge_weigh), (1, edge_turn)] * edge_product, [(sum_lag, sums)] + [(1, node_turn)] * two_products)


def build(nc, **a):
    with ExitStack() as ctx:
        k = Kernel(nc, ctx)
        tables = [nc.dram_tensor(f"table{n}", [N, w], FP32, kind="Internal").ap() for n, w in enumerate((D, D, W, W))]
        sums = [nc.dram_tensor(f"sums{n}", [N + SPARES, W], FP32, kind="Internal").ap() for n in range(5)]
        k.ps_a, k.ps_b, k.ps_c = (k.ps(f"ps_{c}", [P, 8, P]) for c in "abc")
        k.ps_sum = k.ps("ps_sum", [P, 2, 512])
        x = a["x"]
        k.src_col, k.weight_col = k.sb("src_col", [P, 4 * P], I32), k.sb("weight_col", [P, 4 * P])
        k.dst_col, k.add_col = k.sb("dst_col", [P, 4 * P], I32), k.sb("add_col", [P, 4 * P])
        k.lane_i, k.lane = k.sb("lane_i", [P, P], I32), k.sb("lane", [P, P])
        k.degree, k.count, k.inverse = (k.sb(x, [P, TILES]) for x in ("degree", "count", "inverse"))
        k.slots, k.place = k.sb("slots", [1, TILES * B], I32), k.sb("place", [P, TILES * B])
        k.paths = k.sb("paths", [1, 2], I32)
        with k.one_pass():
            load_constants(k, a)
        with k.one_pass():
            plan_pass(k, a)
        with k.one_pass():
            clear_tables(k, sums[2:3], None)
        with k.one_pass():
            clear_tables(k, sums[:2] + sums[3:], "general")
        with k.one_pass():
            sorted_pass(k, a, "t0", "first", x, tables[0])
        with k.one_pass():
            sorted_pass(k, a, "t1", "mid", tables[0], tables[1])
        with k.one_pass():
            edge_pass(k, a, "e0", "general", "h", x, sums[0], "src", "dst")
        with k.one_pass():
            node_pass(k, a, "n0", "general", "first", x, tables[0], sums[0])
        with k.one_pass():
            edge_pass(k, a, "e1", "general", "plain", tables[0], sums[1], "src", "dst")
        with k.one_pass():
            node_pass(k, a, "n1", "general", "mid", tables[0], tables[1], sums[1], x)
        with k.one_pass():
            filter_edges(k, a, "e2", tables[1], sums[2])
        with k.one_pass():
            filter_nodes(k, a, "n2", tables[1], sums[2], tables[2])
        with k.one_pass():
            sorted_pass(k, a, "t3", "linear", tables[2], tables[3])
        with k.one_pass():
            sorted_pass(k, a, "t4", "last", tables[3], a["out"])
        with k.one_pass():
            edge_pass(k, a, "e3", "general", "weight", tables[2], sums[3], "src", "dst")
        with k.one_pass():
            node_pass(k, a, "n3", "general", "linear", tables[2], tables[3], sums[3])
        with k.one_pass():
            edge_pass(k, a, "e4", "general", "degree", tables[3], sums[4], "src", "dst")
        with k.one_pass():
            node_pass(k, a, "n4", "general", "last", tables[3], a["out"], sums[4])


INPUTS = ["x", "src", "dst", "edge_attr_20", "edge_weight",
          "L0_gnn_W_conv0", "L0_gnn_b_conv0", "L0_gnn_W_lin0", "L0_gnn_b_lin0",
          "L0_gnn_W_conv1", "L0_gnn_b_conv1", "L0_gnn_W_lin1", "L0_gnn_b_lin1",
          "L1_gnn_W_in2f", "L1_gnn_b_in2f", "L1_gnn_W_f1", "L1_gnn_b_f1", "L1_gnn_W_f2", "L1_gnn_b_f2",
          "L1_gnn_W_o1", "L1_gnn_b_o1", "L1_gnn_W_o2", "L1_gnn_b_o2", "L2_gnn_W", "L2_gnn_b"]


def kernel(**inputs):
    import concourse.bacc as bacc
    from concourse.bass_utils import run_bass_kernel_spmd

    nc = bacc.Bacc("TRN2", target_bir_lowering=False, num_devices=1)
    arrays, aps = {}, {}
    for name in INPUTS:
        arrays[name] = np.ascontiguousarray(inputs[name])
        aps[name] = nc.dram_tensor(name, arrays[name].shape, mybir.dt.from_np(arrays[name].dtype),
                                   kind="ExternalInput").ap()
    aps["out"] = nc.dram_tensor("out", [N, D], FP32, kind="ExternalOutput").ap()
    build(nc, **aps)
    return run_bass_kernel_spmd(nc, [arrays], core_ids=[0]).results[0]["out"]
```

```python
from contextlib import ExitStack, contextmanager

import numpy as np

import concourse.bass as bass
from concourse import mybir

FP32, I32, BF16, F16 = mybir.dt.float32, mybir.dt.int32, mybir.dt.bfloat16, mybir.dt.float16
ALU, ACT, AX = mybir.AluOpType, mybir.ActivationFunctionType, mybir.AxisListType

P = 128
N, D = 100000, 128
E, R = 50000, 20
W = D + 4
AUX = D
SPARES = 2 * P
J = 5
G = P * J
NG, NT = divmod(N, G)
EG, ET = divmod(E, G)
NTP, ETP = NT // J, ET // J
EPS = 1e-5
LOG2 = 0.6931471805599453

T = 4
STEPS = -(-N // (T * P))
B = 2
TILES, BLOCKS = STEPS * T, STEPS * B
LEAD = 6
AHEAD = 8
WINDOW = B * LEAD
RING = 64
FULL, LAST = divmod(E, P)
assert STEPS % 4 == 0 and AHEAD % 4 == 0 and AHEAD >= LEAD + 2 and BLOCKS > FULL and RING >= 4 * WINDOW


class Chain:

    def __init__(self, eng, sem, per_round=None):
        self.eng, self.sem, self.per_round, self.base, self.k = eng, sem, per_round, 0, 0

    def round(self, i):
        self.base, self.k = i * self.per_round, 0

    def __call__(self, ins):
        ins.then_inc(self.sem, 1)
        self.k += 1
        self.eng.wait_ge(self.sem, self.base + self.k)

    def end(self):
        assert self.k == self.per_round, (self.k, self.per_round)


def take(eng, sem, n):
    eng.wait_ge(sem, n)
    eng.nop().then_inc(sem, -n)


def moments(v, k, link):
    half = lambda n: k.stats[:, :, n]
    link(v.tensor_tensor(k.mean[:, :], half(1), half(4), ALU.add))
    link(v.tensor_tensor(k.gap[:, :], half(1), half(4), ALU.subtract))
    link(v.tensor_tensor(k.gap[:, :], k.gap[:, :], k.gap[:, :], ALU.mult))
    link(v.tensor_tensor(k.var[:, :], half(2), half(5), ALU.add))


def group_rows(ap, i, parts=P):
    return ap[bass.ds(i * G, parts * J), :].rearrange("(p j) w -> p j w", j=J)


class Kernel:
    def __init__(self, nc, ctx):
        self.nc, self.ctx, self.owned = nc, ctx, 0

    def sb(self, name, shape, dt=FP32):
        return self.ctx.enter_context(self.nc.sbuf_tensor(name, shape, dt))

    def ps(self, name, shape):
        return self.ctx.enter_context(self.nc.psum_tensor(name, shape, FP32))

    def sem(self, name):
        self.sems.append(self.pass_ctx.enter_context(self.nc.semaphore(name)))
        return self.sems[-1]

    def own(self, name, shape, dt=FP32):
        self.owned += 1
        return self.pass_ctx.enter_context(self.nc.sbuf_tensor(f"{name}_{self.owned}", shape, dt))

    def only(self, path):
        def part(program):
            def guarded(eng):
                at = ("sorted", "general").index(path)
                with eng.If(eng.value_load(self.paths[0:1, at:at + 1], min_val=0, max_val=1)):
                    program(eng)
            return guarded
        return part

    def lasting_sem(self, name):
        return self.ctx.enter_context(self.nc.semaphore(name))

    @contextmanager
    def one_pass(self):
        self.sems = []
        with ExitStack() as self.pass_ctx:
            yield
            with self.nc.Block() as block:
                @block.gpsimd
                def _(pool):
                    for s in self.sems:
                        pool.sem_clear(s)


def load_constants(k, a):
    nc = k.nc
    mats = ["L0_gnn_W_conv0", "L0_gnn_W_lin0", "L0_gnn_W_conv1", "L0_gnn_W_lin1", "L1_gnn_W_in2f",
            "L1_gnn_W_f2", "L1_gnn_W_o1", "L1_gnn_W_o2", "L2_gnn_W"]
    rows = ["L0_gnn_b_conv0", "L0_gnn_b_lin0", "L0_gnn_b_conv1", "L0_gnn_b_lin1", "L1_gnn_b_in2f",
            "L1_gnn_b_f2", "L1_gnn_b_o1", "L1_gnn_b_o2", "L2_gnn_b"]
    k.ident, k.tri = k.sb("ident", [P, P]), k.sb("tri", [P, P])
    k.spare_i, k.spare = k.sb("spare_i", [P, 1], I32), k.sb("spare", [P, 1])
    k.eps, k.turn = k.sb("eps", [P, 1]), k.sb("turn", [P, 1])
    k.zeros = k.sb("zeros", [P, J, W])
    k.wt, k.bias = k.sb("wt", [P, len(mats), P]), k.sb("bias", [P, len(rows) + 2, D])
    k.f1, k.f1_t = k.sb("f1", [P, R]), k.sb("f1_t", [R, P])
    k.f1_bias = k.sb("f1_bias", [P, 1])
    k.o1_bias = k.sb("o1_bias", [P, 1])
    k.raw = k.own("raw", [P, len(mats), P])
    s_const, s_load, s_pe, s_sum = k.sem("s_const"), k.sem("s_load"), k.sem("s_pe"), k.sem("s_sum")
    psw = k.ps_a
    k.W = {m: k.wt[:, n, :] for n, m in enumerate(mats)}
    k.B = {m: k.bias[:, n, :] for n, m in enumerate(rows)}
    k.B["L0_0"], k.B["L0_1"] = k.bias[:, len(rows), :], k.bias[:, len(rows) + 1, :]
    n_mats = len(mats)

    with nc.Block() as block:
        @block.sync
        def _(sp):
            for n, m in enumerate(mats):
                sp.dma_start(k.raw[:, n, :], a[m]).then_inc(s_load, 16)
            for n, m in enumerate(rows):
                sp.dma_start(k.bias[:, n, :], a[m].rearrange("(o n) -> o n", o=1).to_broadcast([P, D])).then_inc(s_load, 16)
            sp.dma_start(k.f1[:, :], a["L1_gnn_W_f1"]).then_inc(s_load, 16)
            sp.dma_start(k.f1_bias[:, :], a["L1_gnn_b_f1"].rearrange("(n o) -> n o", o=1)).then_inc(s_load, 16)
            sp.dma_start(k.o1_bias[:, :], a["L1_gnn_b_o1"].rearrange("(n o) -> n o", o=1)).then_inc(s_load, 16)

        @block.gpsimd
        def _(pool):
            pool.memset(k.ident[:, :], 0.0).then_inc(s_const, 1)
            pool.memset(k.tri[:, :], 1.0).then_inc(s_const, 1)
            pool.memset(k.eps[:, :], EPS)
            pool.memset(k.zeros[:, :, :], 0.0)
            pool.iota(k.spare_i[:, :], [[0, 1]], base=N, channel_multiplier=1).then_inc(s_const, 1)
            pool.wait_ge(s_const, 3)
            pool.affine_select(out=k.ident[:, :], in_=k.ident[:, :], compare_op=ALU.not_equal, fill=1.0,
                               base=0, pattern=[[-1, P]], channel_multiplier=1).then_inc(s_const, 1)
            pool.affine_select(out=k.tri[:, :], in_=k.tri[:, :], compare_op=ALU.is_gt, fill=0.0,
                               base=0, pattern=[[-1, P]], channel_multiplier=1).then_inc(s_const, 1)
            pool.tensor_copy(k.spare[:, :], k.spare_i[:, :]).then_inc(s_const, 1)

        @block.tensor
        def _(pe):
            pe.wait_ge(s_const, 6)
            pe.wait_ge(s_load, 16 * (len(mats) + len(rows) + 3))
            for n in range(n_mats):
                if n:
                    pe.wait_ge(s_sum, n)
                nc.tensor.transpose(psw[:, 0, :], k.raw[:, n, :], k.ident[:, :]).then_inc(s_pe, 1)
            pe.wait_ge(s_sum, n_mats)
            nc.tensor.transpose(psw[0:R, 0, :], k.f1[:, :], k.ident[:, :]).then_inc(s_pe, 1)

        @block.vector
        def _(dve):
            for n in range(n_mats):
                dve.wait_ge(s_pe, n + 1)
                nc.vector.tensor_copy(k.wt[:, n, :], psw[:, 0, :]).then_inc(s_sum, 1)
            dve.wait_ge(s_pe, n_mats + 1)
            nc.vector.tensor_copy(k.f1_t[:, :], psw[0:R, 0, :]).then_inc(s_sum, 1)
            dve.wait_ge(s_load, 16 * (len(mats) + len(rows) + 3))
            for n in (0, 1):
                nc.vector.tensor_tensor(k.B[f"L0_{n}"], k.B[f"L0_gnn_b_conv{n}"], k.B[f"L0_gnn_b_lin{n}"],
                                        ALU.add).then_inc(s_sum, 1)
            dve.wait_ge(s_sum, n_mats + 3)


def zero_rows(sp, k, table, sem):
    with sp.Fori(0, NG) as i:
        sp.dma_start(group_rows(table, i), k.zeros[:, :, :]).then_inc(sem, 16)
    rest = N + SPARES - NG * G
    sp.dma_start(table[NG * G:N + SPARES, :].rearrange("(p j) w -> p j w", j=4), k.zeros[0:rest // 4, 0:4, :]).then_inc(sem, 16)


def clear_tables(k, tables):
    s_cleared = k.sem("s_cleared")
    with k.nc.Block() as block:
        @block.sync
        @k.only("general")
        def _(sp):
            for t in tables:
                zero_rows(sp, k, t, s_cleared)
            sp.wait_ge(s_cleared, 16 * len(tables) * (NG + 1))


def general_buffers(k):
    sb = k.own
    k.gidx, k.kidx, k.sidx = (sb(x, [P, J], I32) for x in ("gidx", "kidx", "sidx"))
    k.krow = sb("krow", [P, G], I32)
    k.wcol, k.kcol, k.dup, k.tgt = (sb(x, [P, J]) for x in ("wcol", "kcol", "dup", "tgt"))
    k.mean, k.gap, k.var = (sb(x, [P, J]) for x in ("mean", "gap", "var"))
    k.std, k.rstd = (sb(x, [P, J]) for x in ("std", "rstd"))
    k.stats = sb("stats", [P, J, 6])
    k.same, k.junk = sb("same", [P, J, P]), sb("junk", [P, P])
    k.rows, k.msg, k.summed = (sb(x, [P, J, W]) for x in ("rows", "msg", "summed"))
    k.h_t, k.z, k.az, k.fw, k.res = (sb(x, [P, J, D]) for x in ("h_t", "z", "az", "fw", "res"))


def sorted_buffers(k):
    sb = k.own
    k.numbers = sb("numbers", [P, 4, B], I32)
    k.stage, k.plain = sb("stage", [P, 4, B, W]), sb("plain", [P, 2, B, D])
    k.ring = sb("ring", [P, RING * D])
    k.plain_t = sb("plain_t", [P, 2, B, D])
    k.x, k.res4, k.y = sb("node_x", [P, 4, T, W]), sb("res4", [P, 4, T, W]), sb("y", [P, 4, T, W])
    k.h, k.h_t2 = sb("h", [P, 4, T, D]), sb("h_t2", [P, 2, T, D])
    k.select = sb("select", [P, 4, T * B, P])
    k.estats, k.nstats = sb("estats", [P, 2, B, 6]), sb("nstats", [P, 2, T, 6])
    k.emv, k.nmv = sb("emv", [P, 2, B, 2]), sb("nmv", [P, 2, T, 2])
    k.estd, k.erstd, k.eshift = (sb(x, [P, 2, B]) for x in ("estd", "erstd", "eshift"))
    k.nstd, k.nrstd, k.nshift = (sb(x, [P, 2, T]) for x in ("nstd", "nrstd", "nshift"))
    k.idle, k.idle3 = sb("idle", [P, 4]), sb("idle3", [P, 1])


def edge_pass(k, a, name, mode, table, sums, gather_by, add_by):
    nc = k.nc
    general_buffers(k)
    ln, weighted, from_row = mode in ("h", "weight", "degree"), mode == "weight", mode == "degree"
    width = table.shape[1]
    s_idx, s_gidx, s_key, s_turn = (k.sem(f"{name}_{x}") for x in ("idx", "gidx", "key", "turn"))
    s_got, s_add = k.lasting_sem(f"{name}_got"), k.lasting_sem(f"{name}_add")
    s_chain, s_stat, s_std = k.sem(f"{name}_chain"), k.sem(f"{name}_stat"), k.sem(f"{name}_std")
    s_msg, s_sum, s_out = k.sem(f"{name}_msg"), k.sem(f"{name}_sum"), k.sem(f"{name}_out")
    s_free, s_preset = k.sem(f"{name}_free"), k.sem(f"{name}_preset")
    loads = 2 + weighted
    gather_ap, key_ap = a[gather_by], a[add_by]
    sum_of = lambda j: k.ps_sum[:, j // 3, j % 3 * W:(j % 3 + 1) * W]

    def every_group(eng, body):
        with eng.Fori(0, EG) as i:
            body(i, False)
        body(EG, True)

    with nc.Block() as block:
        @block.sync
        @k.only("general")
        def _(sp):
            def body(i, tail):
                parts = ETP if tail else P
                sp.wait_ge(s_free, i + 1)
                if tail:
                    sp.wait_ge(s_preset, 1)
                col = lambda ap: ap[bass.ds(i * G, parts * J)].rearrange("(p j) -> p j", j=J)
                sp.dma_start(k.gidx[0:parts, :], col(gather_ap)).then_inc(s_gidx, 16)
                sp.dma_start(k.kidx[0:parts, :], col(key_ap)).then_inc(s_idx, 16)
                sp.dma_start(k.krow[:, 0:parts * J], key_ap[bass.ds(i * G, parts * J)].rearrange("(o n) -> o n", o=1)
                             .to_broadcast([P, parts * J])).then_inc(s_idx, 16)
                if weighted:
                    sp.dma_start(k.wcol[0:parts, :], col(a["edge_weight"])).then_inc(s_idx, 16)
            sp.nop().then_inc(s_free, 1)
            every_group(sp, body)

        @block.gpsimd
        @k.only("general")
        def _(pool):
            def body(i, tail):
                take(pool, s_gidx, 16)
                for j in range(J):
                    pool.indirect_dma_start(out=k.rows[:, j, 0:width], out_offset=None, in_=table,
                                            in_offset=bass.IndirectOffsetOnAxis(ap=k.gidx[:, j:j + 1], axis=0)).then_inc(s_got, 16)
                take(pool, s_key, 1)
                for j in range(J):
                    take(pool, s_out, 1)
                    pool.indirect_dma_start(out=sums, out_offset=bass.IndirectOffsetOnAxis(ap=k.sidx[:, j:j + 1], axis=0),
                                            in_=k.summed[:, j, :], in_offset=None, compute_op=ALU.add).then_inc(s_add, 16)
                    pool.wait_ge(s_add, 16 * (i * J + j + 1))
                    pool.tensor_tensor(k.turn[:, :], k.spare[:, :], k.spare[:, :], ALU.add).then_inc(s_turn, 1)
                    take(pool, s_turn, 1)
                pool.nop().then_inc(s_free, 1)
            every_group(pool, body)

        @block.vector
        @k.only("general")
        def _(dve):
            link = Chain(dve, s_chain, 2 * J + 5 + J * (weighted or from_row) + ((2 * J + 7) if ln else 1))
            v = nc.vector

            def body(i, tail):
                link.round(i)
                if tail:
                    dve.wait_ge(s_free, i + 1)
                    v.memset(k.krow[:, :], -1)
                    v.tensor_copy(k.kidx[:, :], k.spare_i[:, :].to_broadcast([P, J])).then_inc(s_preset, 1)
                    dve.wait_ge(s_preset, 1)
                dve.wait_ge(s_idx, 16 * loads * (i + 1))
                link(v.tensor_copy(k.kcol[:, :], k.kidx[:, :]))
                for j in range(J):
                    link(v.tensor_scalar(k.same[:, j, :], k.krow[:, j:G:J], k.kcol[:, j:j + 1], None, ALU.is_equal))
                for j in range(J):
                    link(v.tensor_tensor_reduce(out=k.junk[:, :], in0=k.same[:, j, :], in1=k.tri[:, :], scale=1.0, scalar=0.0,
                                                op0=ALU.mult, op1=ALU.add, accum_out=k.dup[:, j:j + 1]))
                link(v.tensor_scalar(k.dup[:, :], k.dup[:, :], 1.0, None, ALU.min))
                link(v.tensor_scalar(k.tgt[:, :], k.kcol[:, :], -1.0, k.spare[:, 0:1], ALU.mult, ALU.add))
                link(v.tensor_tensor(k.tgt[:, :], k.tgt[:, :], k.dup[:, :], ALU.mult))
                link(v.tensor_tensor(k.tgt[:, :], k.tgt[:, :], k.kcol[:, :], ALU.add))
                v.tensor_copy(k.sidx[:, :], k.tgt[:, :]).then_inc(s_key, 1)
                dve.wait_ge(s_got, 16 * J * (i + 1))
                if from_row:
                    wsrc = k.rows[:, :, AUX]
                elif weighted:
                    wsrc = k.wcol[:, :]
                if weighted or from_row:
                    for j in range(J):
                        link(v.tensor_scalar(k.same[:, j, :], k.same[:, j, :], wsrc[:, j:j + 1], None, ALU.mult))
                if not ln:
                    link(v.memset(k.msg[:, :, D:W], 1.0))
                    v.tensor_copy(k.msg[:, :, 0:D], k.rows[:, :, 0:D]).then_inc(s_msg, 1)
                else:
                    for j in range(J):
                        link(v.bn_stats(k.stats[:, j, :], k.rows[:, j, 0:D]))
                    moments(v, k, link)
                    v.scalar_tensor_tensor(k.var[:, :], k.gap[:, :], D / 4, k.var[:, :], ALU.mult, ALU.add).then_inc(s_stat, 1)
                    dve.wait_ge(s_std, i + 1)
                    link(v.reciprocal(k.rstd[:, :], k.std[:, :]))
                    link(v.scalar_tensor_tensor(k.mean[:, :], k.mean[:, :], -0.5, k.rstd[:, :], ALU.mult, ALU.mult))
                    for j in range(J):
                        link(v.tensor_scalar(k.rows[:, j, 0:D], k.rows[:, j, 0:D], k.rstd[:, j:j + 1], k.mean[:, j:j + 1], ALU.mult, ALU.add))
                if ln:
                    link(v.memset(k.msg[:, :, D:W], 1.0))
                if ln:
                    v.tensor_scalar(k.msg[:, :, 0:D], k.rows[:, :, 0:D], 0.0, None, ALU.max).then_inc(s_msg, 1)
                dve.wait_ge(s_sum, i + 1)
                for j in range(J):
                    v.tensor_copy(k.summed[:, j, :], sum_of(j)).then_inc(s_out, 1)
                link.end()
            every_group(dve, body)

        @block.scalar
        @k.only("general")
        def _(act):
            s = nc.scalar

            def body(i, tail):
                act.wait_ge(s_stat, i + 1)
                s.activation(k.std[:, :], k.var[:, :], ACT.Sqrt, bias=k.eps[:, 0:1], scale=1.0 / D).then_inc(s_std, 1)
            if ln:
                every_group(act, body)

        @block.tensor
        @k.only("general")
        def _(pe):
            t = nc.tensor

            def body(i, tail):
                pe.wait_ge(s_msg, i + 1)
                for j in range(J):
                    last = t.matmul(sum_of(j), k.same[:, j, :], k.msg[:, j, :], start=True, stop=True)
                last.then_inc(s_sum, 1)
            every_group(pe, body)


def node_pass(k, a, name, kind, table, out, sums, residual=None):
    nc = k.nc
    general_buffers(k)
    s_in, s_st = k.sem(f"{name}_in"), k.sem(f"{name}_st")
    s_chain, s_stat, s_std = k.sem(f"{name}_chain"), k.sem(f"{name}_stat"), k.sem(f"{name}_std")
    s_op, s_tp, s_tc, s_mm, s_done = (k.sem(f"{name}_{x}") for x in ("op", "tp", "tc", "mm", "done"))
    ln = kind in ("first", "last")
    width = table.shape[1]
    loads = 2 + (residual is not None)
    out_w = out.shape[1]

    def every_group(eng, body):
        with eng.Fori(0, NG) as i:
            body(i, P)
        body(NG, NTP)

    with nc.Block() as block:
        @block.sync
        @k.only("general")
        def _(sp):
            def body(i, parts):
                sp.wait_ge(s_done, i + 1)
                sp.dma_start(k.rows[0:parts, :, 0:width], group_rows(table, i, parts)).then_inc(s_in, 16)
                sp.dma_start(k.summed[0:parts, :, :], group_rows(sums, i, parts)).then_inc(s_in, 16)
                if residual is not None:
                    sp.dma_start(k.res[0:parts, :, :], group_rows(residual, i, parts)).then_inc(s_in, 16)
                sp.wait_ge(s_done, i + 2)
                sp.dma_start(group_rows(out, i, parts), k.msg[0:parts, :, 0:out_w]).then_inc(s_st, 16)
            sp.nop().then_inc(s_done, 1)
            sp.nop().then_inc(s_st, 16)
            every_group(sp, body)
            sp.wait_ge(s_st, 16 * (NG + 2))

        @block.vector
        @k.only("general")
        def _(dve):
            v = nc.vector
            link = Chain(dve, s_chain, {"first": 2 * J + 5 + 3 + 3, "mid": 4, "linear": 3, "last": 2 * J + 6 + 4}[kind])

            def body(i, parts):
                link.round(i)
                dve.wait_ge(s_in, 16 * loads * (i + 1))
                dve.wait_ge(s_st, 16 * (i + 1))
                x, agg, o = k.rows[:, :, 0:D], k.summed[:, :, 0:D], k.msg[:, :, 0:D]
                each = lambda ap: ap.unsqueeze(2).to_broadcast([P, J, D])
                over = lambda ap: ap.unsqueeze(1).to_broadcast([P, J, D])
                if ln:
                    for j in range(J):
                        link(v.bn_stats(k.stats[:, j, :], k.rows[:, j, 0:D]))
                    moments(v, k, link)
                    v.scalar_tensor_tensor(k.var[:, :], k.gap[:, :], D / 4, k.var[:, :], ALU.mult, ALU.add).then_inc(s_stat, 1)
                    dve.wait_ge(s_std, i + 1)
                    link(v.reciprocal(k.rstd[:, :], k.std[:, :]))
                    link(v.scalar_tensor_tensor(k.mean[:, :], k.mean[:, :], -0.5, k.rstd[:, :], ALU.mult, ALU.mult))
                    for j in range(J):
                        link(v.tensor_scalar(k.z[:, j, :], k.rows[:, j, 0:D], k.rstd[:, j:j + 1], k.mean[:, j:j + 1], ALU.mult, ALU.add))
                    link(v.tensor_scalar(k.z[:, :, :], k.z[:, :, :], 0.0, None, ALU.max))
                if kind in ("first", "mid"):
                    link(v.tensor_scalar(k.dup[:, :], k.summed[:, :, AUX], 1.0, None, ALU.max))
                    link(v.reciprocal(k.dup[:, :], k.dup[:, :]))
                    v.tensor_tensor(k.fw[:, :, :], agg, each(k.dup[:, :]), ALU.mult).then_inc(s_op, 1)
                if kind in ("first", "mid", "linear"):
                    dve.wait_ge(s_tp, i + 1)
                    if kind in ("first", "mid"):
                        link(v.tensor_copy(k.h_t[:, :, :], k.ps_a[:, 0:J, :]))
                    v.tensor_copy(k.az[:, :, :], k.ps_b[:, 0:J, :]).then_inc(s_tc, 1)
                if kind != "last":
                    dve.wait_ge(s_mm, i + 1)
                    bias = {"first": k.B["L0_0"], "mid": k.B["L0_1"], "linear": k.B["L2_gnn_b"]}[kind]
                    link(v.tensor_tensor(o, k.ps_c[:, 0:J, :], over(bias), ALU.add))
                if kind == "first":
                    v.tensor_scalar(o, o, 0.0, None, ALU.max).then_inc(s_done, 1)
                elif kind == "mid":
                    v.tensor_tensor(o, o, k.res[:, :, :], ALU.add).then_inc(s_done, 1)
                elif kind == "linear":
                    link(v.tensor_copy(k.msg[:, :, D:W], k.rows[:, :, D:W]))
                    link(v.tensor_tensor(o, o, x, ALU.add))
                    v.tensor_copy(k.dup[:, :], k.rows[:, :, AUX]).then_inc(s_done, 1)
                else:
                    inv_root = k.rows[:, :, AUX]
                    link(v.tensor_tensor(k.z[:, :, :], k.z[:, :, :], each(inv_root), ALU.mult))
                    link(v.tensor_tensor(k.z[:, :, :], k.z[:, :, :], agg, ALU.add))
                    link(v.tensor_tensor(k.z[:, :, :], k.z[:, :, :], each(inv_root), ALU.mult))
                    v.tensor_tensor(o, k.z[:, :, :], x, ALU.add).then_inc(s_done, 1)
                link.end()
            every_group(dve, body)

        @block.scalar
        @k.only("general")
        def _(act):
            s = nc.scalar

            def body(i, parts):
                act.wait_ge(s_stat, i + 1)
                s.activation(k.std[:, :], k.var[:, :], ACT.Sqrt, bias=k.eps[:, 0:1], scale=1.0 / D).then_inc(s_std, 1)
            if ln:
                every_group(act, body)

        @block.tensor
        @k.only("general")
        def _(pe):
            t = nc.tensor

            def body(i, parts):
                src = k.fw if kind in ("first", "mid") else k.summed
                if kind in ("first", "mid"):
                    pe.wait_ge(s_op, i + 1)
                else:
                    pe.wait_ge(s_in, 16 * loads * (i + 1))
                pe.wait_ge(s_done, i + 1)
                for j in range(J):
                    if kind in ("first", "mid"):
                        t.transpose(k.ps_a[:, j, :], (k.z if kind == "first" else k.rows)[:, j, 0:D], k.ident[:, :])
                    last = t.transpose(k.ps_b[:, j, :], src[:, j, 0:D], k.ident[:, :])
                last.then_inc(s_tp, 1)
                pe.wait_ge(s_tc, i + 1)
                for j in range(J):
                    if kind in ("first", "mid"):
                        n = "01"[kind == "mid"]
                        t.matmul(k.ps_c[:, j, :], k.h_t[:, j, :], k.W[f"L0_gnn_W_lin{n}"], start=True, stop=False)
                        last = t.matmul(k.ps_c[:, j, :], k.az[:, j, :], k.W[f"L0_gnn_W_conv{n}"], start=False, stop=True)
                    else:
                        last = t.matmul(k.ps_c[:, j, :], k.az[:, j, :], k.W["L2_gnn_W"], start=True, stop=True)
                last.then_inc(s_mm, 1)
            if kind != "last":
                every_group(pe, body)


def filter_edges(k, a, name, table, sums):
    nc = k.nc
    PAIR, pairs = 2 * P, -(-E // (2 * P))
    sb = k.own
    sidx = sb("sidx", [P, 4, 2], I32)
    numbers = sb("numbers", [P, 4, 2], I32)
    krow = sb("krow", [P, 2, PAIR], I32)
    rbf = sb("rbf", [P, 2, 2, R])
    rbf_t, h_t = sb("rbf_t", [R, 2, PAIR]), sb("h_t", [P, 2, PAIR])
    rows, hf = sb("rows", [P, 4, 2, D]), sb("hf", [P, 4, 2, D])
    h, z, soft, ssp, fw = (sb(x, [P, 2, 2, D]) for x in ("h", "z", "soft", "ssp", "fw"))
    same = sb("same", [P, 2, 2, PAIR])
    msg, summed = sb("msg", [P, 2, 2, W]), sb("summed", [P, 4, 2, W])
    stats, mv = sb("stats", [P, 2, 2, 6]), sb("mv", [P, 2, 2, 2])
    lnv, rstd, shift = (sb(x, [P, 2, 2]) for x in ("lnv", "rstd", "shift"))
    dup, tgt, spares = (sb(x, [P, 2]) for x in ("dup", "tgt", "spares"))
    junk, idle = sb("junk", [P, PAIR]), sb("idle", [P, 2])
    earlier = sb("earlier", [P, 2, PAIR])
    s_got = [k.lasting_sem(f"{name}_got{s}") for s in range(4)]
    s_add = k.lasting_sem(f"{name}_add")
    s_krow, s_rbf = [k.sem(f"{name}_krow{s}") for s in range(2)], [k.sem(f"{name}_rbf{s}") for s in range(2)]
    (s_free, s_numbers, s_chain, s_var, s_rstd, s_scale, s_h, s_turned, s_turned_sb, s_first, s_z, s_hf, s_lnz, s_act,
     s_ssp, s_second, s_fw, s_keys, s_msg, s_sums, s_summed, s_link, s_preset, s_filled, s_added, s_soft, s_copied) = (
        k.sem(f"{name}_{x}") for x in (
            "free", "numbers", "chain", "var", "rstd", "scale", "h", "turned", "turned_sb", "first", "z", "hf", "lnz", "act",
            "ssp", "second", "fw", "keys", "msg", "sums", "summed", "link", "preset", "filled", "added", "soft", "copied"))

    def pair(tile, s):
        return tile[:, s % 2, :, :]

    def bank(ps, s, at, n=PAIR):
        return ps[:, :, :].rearrange("p a b -> p (a b)")[:, 512 * (s % 2) + at:512 * (s % 2) + at + n]

    def uses(i, s, slots, n):
        return (i - s % slots) * (16 * n // slots) + 16 * n

    def known(i, least):
        return not isinstance(i, int) or i >= least

    def live(i):
        return not isinstance(i, int) or 0 <= i < pairs

    def every_round(eng, stages):
        def one(i, s):
            for n, stage in stages:
                if live(i - n):
                    stage(i - n, (s - n) % 4)
        for i in range(16):
            one(i, i % 4)
        with eng.Fori(4, pairs // 4 - 1) as u:
            for s in range(4):
                one(4 * u + s, s)
        for i in range(pairs - 4, pairs + 12):
            one(i, i % 4)

    with nc.Block() as block:
        @block.sync
        def _(sp):
            def radial(i, s):
                if known(i, 2):
                    sp.wait_ge(s_turned, i - 1)
                if isinstance(i, int) and i == pairs - 1:
                    lo = i * PAIR
                    sp.dma_start(rbf[0:E - lo, s % 2, 0, :], a["edge_attr_20"][lo:E, :]).then_inc(s_rbf[s % 2], 16)
                else:
                    sp.dma_start(pair(rbf, s), a["edge_attr_20"][bass.ds(i * PAIR, PAIR), :].rearrange("(q p) r -> p q r", p=P)).then_inc(s_rbf[s % 2], 16)

            def keys(i, s):
                if known(i, 2):
                    sp.wait_ge(s_keys, i - 1)
                if isinstance(i, int) and i == pairs - 1:
                    sp.wait_ge(s_preset, 1)
                    lo = i * PAIR
                    sp.dma_start(krow[:, s % 2, 0:E - lo], a["src"][lo:E].rearrange("(o n) -> o n", o=1).to_broadcast([P, E - lo])).then_inc(s_krow[s % 2], 16)
                else:
                    sp.dma_start(krow[:, s % 2, :], a["src"][bass.ds(i * PAIR, PAIR)].rearrange("(o n) -> o n", o=1).to_broadcast([P, PAIR])).then_inc(s_krow[s % 2], 16)
            every_round(sp, ((0, radial), (5, keys)))

        @block.gpsimd
        def _(pool):
            pool.nop().then_inc(s_free, 4)

            def gather(i, s):
                take(pool, s_free, 1)
                pool.tensor_copy(numbers[:, s, :], k.dst_col[:, bass.ds(i * 2, 2)]).then_inc(s_numbers, 1)
                take(pool, s_numbers, 1)
                for q in range(2):
                    pool.indirect_dma_start(out=rows[:, s, q, :], out_offset=None, in_=table,
                                            in_offset=bass.IndirectOffsetOnAxis(ap=numbers[:, s, q:q + 1], axis=0)).then_inc(s_got[s], 16)

            def scatter(i, s):
                take(pool, s_summed, 1)
                for q in range(2):
                    pool.indirect_dma_start(out=sums, out_offset=bass.IndirectOffsetOnAxis(ap=sidx[:, s, q:q + 1], axis=0),
                                            in_=summed[:, s, q, :], in_offset=None, compute_op=ALU.add).then_inc(s_add, 16)

            def added(i, s):
                pool.wait_ge(s_add, 32 * (i + 1))
                pool.tensor_tensor(idle[:, 0:1], k.spare[:, :], k.spare[:, :], ALU.add).then_inc(s_added, 1)
                take(pool, s_added, 1)

            every_round(pool, ((11, scatter), (0, gather), (11, added)))

        @block.vector
        def _(dve):
            v = nc.vector
            link = Chain(dve, s_chain, 2)
            klink = Chain(dve, s_link, 8)

            def moments_of(i, s):
                o = s % 2
                link.round(i)
                dve.wait_ge(s_got[s], uses(i, s, 4, 2))
                v.tensor_tensor(idle[:, 1:2], k.spare[:, :], k.spare[:, :], ALU.add)
                for q in range(2):
                    v.bn_stats(stats[:, o, q, :], rows[:, s, q, :]).then_inc(s_chain, 1)
                link.k += 2
                dve.wait_ge(s_chain, link.base + link.k)
                v.tensor_tensor(idle[:, 1:2], k.spare[:, :], k.spare[:, :], ALU.add)
                v.bn_aggr(mv[:, o, 0, :], stats[:, o, 0, :])
                v.bn_aggr(mv[:, o, 1, :], stats[:, o, 1, :]).then_inc(s_var, 1)
                link.end()

            def scale(i, s):
                o = s % 2
                dve.wait_ge(s_rstd, i + 1)
                v.scalar_tensor_tensor(shift[:, o, :], mv[:, o, :, 0], -1.0, rstd[:, o, :], ALU.mult, ALU.mult).then_inc(s_scale, 1)

            def hidden(i, s):
                dve.wait_ge(s_first, i + 1)
                v.tensor_scalar(pair(z, s), bank(k.ps_b, s, 0).rearrange("p (q n) -> p q n", q=2), k.f1_bias[:, 0:1], 0.0, ALU.add, ALU.max).then_inc(s_z, 1)
                v.tensor_tensor(hf[:, s, :, :], bank(k.ps_b, s, PAIR).rearrange("p (q n) -> p q n", q=2),
                                k.B["L1_gnn_b_in2f"].unsqueeze(1).to_broadcast([P, 2, D]), ALU.add).then_inc(s_hf, 1)

            def soften(i, s):
                dve.wait_ge(s_act, i + 1)
                dve.wait_ge(s_z, i + 1)
                if known(i, 2):
                    dve.wait_ge(s_second, i - 1)
                v.scalar_tensor_tensor(pair(ssp, s), pair(z, s), -LOG2, pair(soft, s), ALU.add, ALU.add).then_inc(s_ssp, 1)

            def keys(i, s):
                if isinstance(i, int) and i == pairs - 1:
                    v.memset(krow[:, s % 2, :], -1).then_inc(s_preset, 1)
                klink.round(i)
                dve.wait_ge(s_krow[s % 2], uses(i, s, 2, 1))
                if known(i, 2):
                    dve.wait_ge(s_sums, i - 1)
                for q in range(2):
                    v.tensor_scalar(same[:, s % 2, q, :], krow[:, s % 2, :], k.add_col[:, bass.ds(i * 2 + q, 1)], None, ALU.is_equal).then_inc(s_link, 1)
                klink.k += 2
                dve.wait_ge(s_link, klink.base + klink.k)
                for q in range(2):
                    klink(v.tensor_tensor_reduce(out=junk[:, :], in0=same[:, s % 2, q, :], in1=earlier[:, q, :], scale=1.0, scalar=0.0,
                                                 op0=ALU.mult, op1=ALU.add, accum_out=dup[:, q:q + 1]))
                key = k.add_col[:, bass.ds(i * 2, 2)]
                klink(v.tensor_scalar(dup[:, :], dup[:, :], 1.0, None, ALU.min))
                klink(v.tensor_tensor(tgt[:, :], spares[:, :], key, ALU.subtract))
                klink(v.tensor_tensor(tgt[:, :], tgt[:, :], dup[:, :], ALU.mult))
                klink(v.tensor_tensor(tgt[:, :], tgt[:, :], key, ALU.add))
                if known(i, 4):
                    dve.wait_ge(s_add, 32 * (i - 3))
                v.tensor_copy(sidx[:, s, :], tgt[:, :]).then_inc(s_keys, 1)
                klink.end()

            def messages(i, s):
                dve.wait_ge(s_second, i + 1)
                v.tensor_tensor(pair(fw, s), bank(k.ps_c, s, 0).rearrange("p (q n) -> p q n", q=2),
                                k.B["L1_gnn_b_f2"].unsqueeze(1).to_broadcast([P, 2, D]), ALU.add).then_inc(s_fw, 1)
                dve.wait_ge(s_fw, i + 1)
                for q in range(2):
                    made = v.scalar_tensor_tensor(msg[:, s % 2, q, 0:D], fw[:, s % 2, q, :], k.weight_col[:, bass.ds(i * 2 + q, 1)], hf[:, s, q, :], ALU.mult, ALU.mult)
                made.then_inc(s_msg, 1)

            v.memset(msg[:, :, :, D:W], 1.0)
            v.memset(earlier[:, 0, P:PAIR], 0.0)
            for q in range(2):
                v.tensor_scalar(spares[:, q:q + 1], k.spare[:, :], float(q * P), None, ALU.add)
            v.memset(earlier[:, 1, 0:P], 1.0)
            v.tensor_copy(earlier[:, 0, 0:P], k.tri[:, :]).then_inc(s_filled, 1)
            v.tensor_copy(earlier[:, 1, P:PAIR], k.tri[:, :]).then_inc(s_filled, 1)
            dve.wait_ge(s_filled, 2)

            every_round(dve, ((7, keys), (7, messages), (5, soften), (4, hidden), (1, scale), (0, moments_of)))

        @block.scalar
        def _(act):
            sc = nc.scalar

            def root(i, s):
                act.wait_ge(s_var, i + 1)
                o = s % 2
                sc.activation(lnv[:, o, :], mv[:, o, :, 1], ACT.Ln, bias=k.eps[:, 0:1]).then_inc(s_lnz, 1)
                act.wait_ge(s_lnz, i + 1)
                sc.activation(rstd[:, o, :], lnv[:, o, :], ACT.Exp, scale=-0.5).then_inc(s_rstd, 1)

            def rectify(i, s):
                o = s % 2
                act.wait_ge(s_scale, i + 1)
                act.wait_ge(s_rstd, i + 1)
                if known(i, 2):
                    act.wait_ge(s_turned, i - 1)
                for q in range(2):
                    made = sc.activation(h[:, o, q, :], rows[:, s, q, :], ACT.Relu, bias=shift[:, o, q:q + 1], scale=rstd[:, o, q:q + 1])
                made.then_inc(s_h, 1)

            def turned(i, s):
                act.wait_ge(s_turned, i + 1)
                act.nop().then_inc(s_free, 1)
                if known(i, 2):
                    act.wait_ge(s_first, i - 1)
                sc.activation(rbf_t[:, s % 2, :], bank(k.ps_a, s, PAIR)[0:R, :], ACT.Copy)
                sc.activation(h_t[:, s % 2, :], bank(k.ps_a, s, 0), ACT.Copy).then_inc(s_turned_sb, 1)

            def soften(i, s):
                act.wait_ge(s_first, i + 1)
                act.wait_ge(s_z, i + 1)
                act.wait_ge(s_hf, i + 1)
                if known(i, 2):
                    act.wait_ge(s_ssp, i - 1)
                what = soft[:, s % 2, :, :].rearrange("p q n -> p (q n)")
                sc.activation(what, bank(k.ps_b, s, 0), ACT.Abs, bias=k.f1_bias[:, 0:1]).then_inc(s_soft, 1)
                act.wait_ge(s_soft, 3 * i + 1)
                sc.activation(what, what, ACT.Exp, scale=-1.0).then_inc(s_soft, 1)
                act.wait_ge(s_soft, 3 * i + 2)
                sc.activation(what, what, ACT.Ln, bias=1.0).then_inc(s_act, 1)
                act.nop().then_inc(s_soft, 1)

            def copy_sums(i, s):
                act.wait_ge(s_sums, i + 1)
                act.wait_ge(s_keys, i + 1)
                if known(i, 4):
                    act.wait_ge(s_add, 32 * (i - 3))
                sc.activation(summed[:, s, :, :], k.ps_sum[:, s % 2, 0:2 * W].rearrange("p (q w) -> p q w", q=2), ACT.Copy).then_inc(s_copied, 1)
                act.wait_ge(s_copied, i + 1)
                act.nop().then_inc(s_summed, 1)

            sc.preload_act_table_set("natural_log_exp_and_others")
            every_round(act, ((9, copy_sums), (2, turned), (1, rectify), (4, soften), (0, root)))

        @block.tensor
        def _(pe):
            t = nc.tensor

            def turn(i, s):
                pe.wait_ge(s_h, i + 1)
                pe.wait_ge(s_rbf[s % 2], uses(i, s, 2, 1))
                if known(i, 2):
                    pe.wait_ge(s_turned_sb, i - 1)
                for q in range(2):
                    t.transpose(bank(k.ps_a, s, q * P, P), h[:, s % 2, q, :], k.ident[:, :])
                    last = t.transpose(bank(k.ps_a, s, PAIR + q * P, P)[0:R, :], rbf[:, s % 2, q, :], k.ident[:, :])
                last.then_inc(s_turned, 1)

            def first(i, s):
                pe.wait_ge(s_turned_sb, i + 1)
                if known(i, 2):
                    pe.wait_ge(s_act, i - 1)
                    pe.wait_ge(s_hf, i - 1)
                t.matmul(bank(k.ps_b, s, 0), k.f1_t[:, :], rbf_t[:, s % 2, :], start=True, stop=True)
                for q in range(2):
                    last = t.matmul(bank(k.ps_b, s, PAIR + q * P, P), h_t[:, s % 2, q * P:(q + 1) * P], k.W["L1_gnn_W_in2f"], start=True, stop=True)
                last.then_inc(s_first, 1)

            def second(i, s):
                pe.wait_ge(s_ssp, i + 1)
                if known(i, 2):
                    pe.wait_ge(s_fw, i - 1)
                for q in range(2):
                    last = t.matmul(bank(k.ps_c, s, q * P, P), ssp[:, s % 2, q, :], k.W["L1_gnn_W_f2"], start=True, stop=True)
                last.then_inc(s_second, 1)

            def sum_equal(i, s):
                pe.wait_ge(s_msg, i + 1)
                pe.wait_ge(s_keys, i + 1)
                if known(i, 2):
                    pe.wait_ge(s_copied, i - 1)
                for q in range(2):
                    for c in range(2):
                        last = t.matmul(k.ps_sum[:, s % 2, q * W:(q + 1) * W], same[:, s % 2, c, q * P:(q + 1) * P], msg[:, s % 2, c, :], start=(c == 0), stop=(c == 1))
                last.then_inc(s_sums, 1)

            every_round(pe, ((8, sum_equal), (6, second), (3, first), (1, turn)))


def filter_nodes(k, a, name, table, sums, out):
    nc = k.nc
    sb = k.own
    agg, x, y = sb("agg", [P, 4, T, W]), sb("x", [P, 4, T, D]), sb("y", [P, 4, T, W])
    agg_t, z, soft, ssp = (sb(n, [P, 2, T, P]) for n in ("agg_t", "z", "soft", "ssp"))
    degree, lnd, inv_root = sb("degree", [P, 2, T]), sb("lnd", [P, 2, T]), sb("inv_root", [P, 4, T])
    s_agg, s_x = [k.sem(f"{name}_agg{s}") for s in range(4)], [k.sem(f"{name}_x{s}") for s in range(4)]
    s_stored = [k.sem(f"{name}_stored{s}") for s in range(4)]
    (s_turned, s_agg_t, s_first, s_z, s_soft, s_act, s_ssp, s_second, s_biased, s_out, s_degree, s_lnd, s_root, s_pad) = (
        k.sem(f"{name}_{n}") for n in (
            "turned", "agg_t", "first", "z", "soft", "act", "ssp", "second", "biased", "out", "degree", "lnd", "root", "pad"))
    rest = N - (STEPS - 1) * T * P

    def bank(ps, s):
        return ps[:, T * (s % 2):T * (s % 2) + T, :]

    def flat(tile):
        return tile.rearrange("p t n -> p (t n)")

    def known(i, least):
        return not isinstance(i, int) or i >= least

    def live(i):
        return not isinstance(i, int) or 0 <= i < STEPS

    def uses(i, s, slots):
        return (i - s % slots) * (16 // slots) + 16 + (16 if isinstance(i, int) and i == STEPS - 1 else 0)

    def every_round(eng, stages):
        def one(i, s):
            for n, stage in stages:
                if live(i - n):
                    stage(i - n, (s - n) % 4)
        for i in range(-2, 12):
            one(i, i % 4)
        with eng.Fori(3, STEPS // 4 - 1) as u:
            for s in range(4):
                one(4 * u + s, s)
        for i in range(STEPS - 4, STEPS + 7):
            one(i, i % 4)

    def move(sp, tile, s, rows, i, sem, width, store=False):
        if isinstance(i, int) and i == STEPS - 1:
            lo = i * T * P
            parts = [(tile[:, s, 0, 0:width], rows[lo:lo + P, 0:width]), (tile[0:rest - P, s, 1, 0:width], rows[lo + P:N, 0:width])]
        else:
            parts = [(tile[:, s, :, 0:width], rows[bass.ds(i * T * P, T * P), 0:width].rearrange("(t p) w -> p t w", p=P))]
        for on_chip, dram in parts:
            sp.dma_start(*((dram, on_chip) if store else (on_chip, dram))).then_inc(sem, 16)

    with nc.Block() as block:
        @block.sync
        def _(sp):
            def load_sums(i, s):
                if known(i, 4):
                    sp.wait_ge(s_turned, i - 3)
                    sp.wait_ge(s_degree, i - 3)
                move(sp, agg, s, sums, i, s_agg[s], W)

            def load_x(i, s):
                if known(i, 4):
                    sp.wait_ge(s_out, i - 3)
                move(sp, x, s, table, i, s_x[s], D)

            def store(i, s):
                sp.wait_ge(s_out, i + 1)
                move(sp, y, s, out, i, s_stored[s], W, store=True)

            every_round(sp, ((-2, load_sums), (2, load_x), (6, store)))
            for s in range(4):
                sp.wait_ge(s_stored[s], uses(STEPS - 4 + s, s, 4))

        @block.gpsimd
        def _(pool):
            def add_bias(i, s):
                take(pool, s_x[s], 32 if isinstance(i, int) and i == STEPS - 1 else 16)
                pool.tensor_tensor(x[:, s, :, :], x[:, s, :, :], k.B["L1_gnn_b_o2"].unsqueeze(1).to_broadcast([P, T, D]), ALU.add).then_inc(s_biased, 1)
            every_round(pool, ((0, add_bias),))

        @block.vector
        def _(dve):
            v = nc.vector

            def count(i, s):
                dve.wait_ge(s_agg[s], uses(i, s, 4))
                if known(i, 2):
                    dve.wait_ge(s_lnd, i - 1)
                v.tensor_scalar(degree[:, s % 2, :], agg[:, s, :, AUX], 1.0, 1.0, ALU.add, ALU.max).then_inc(s_degree, 1)

            def positive(i, s):
                dve.wait_ge(s_first, i + 1)
                if known(i, 2):
                    dve.wait_ge(s_ssp, i - 1)
                v.tensor_scalar(flat(z[:, s % 2, :, :]), flat(bank(k.ps_b, s)), k.o1_bias[:, 0:1], 0.0, ALU.add, ALU.max).then_inc(s_z, 1)

            def soften(i, s):
                dve.wait_ge(s_act, i + 1)
                dve.wait_ge(s_z, i + 1)
                if known(i, 2):
                    dve.wait_ge(s_second, i - 1)
                v.scalar_tensor_tensor(ssp[:, s % 2, :, :], z[:, s % 2, :, :], -LOG2, soft[:, s % 2, :, :], ALU.add, ALU.add).then_inc(s_ssp, 1)

            def finish(i, s):
                dve.wait_ge(s_second, i + 1)
                dve.wait_ge(s_biased, i + 1)
                dve.wait_ge(s_root, i + 1)
                if known(i, 4):
                    dve.wait_ge(s_stored[s], uses(i - 4, s, 4))
                v.tensor_copy(y[:, s, :, AUX], inv_root[:, s, :])
                v.tensor_tensor(y[:, s, :, 0:D], bank(k.ps_c, s), x[:, s, :, :], ALU.add).then_inc(s_out, 1)

            v.memset(y[:, :, :, D:W], 0.0).then_inc(s_pad, 1)
            dve.wait_ge(s_pad, 1)
            every_round(dve, ((2, positive), (5, finish), (0, count), (3, soften)))

        @block.scalar
        def _(act):
            sc = nc.scalar

            def copy_sums(i, s):
                act.wait_ge(s_turned, i + 1)
                if known(i, 2):
                    act.wait_ge(s_first, i - 1)
                sc.activation(agg_t[:, s % 2, :, :], bank(k.ps_a, s), ACT.Copy).then_inc(s_agg_t, 1)

            def soften(i, s):
                what = flat(soft[:, s % 2, :, :])
                act.wait_ge(s_first, i + 1)
                act.wait_ge(s_z, i + 1)
                if known(i, 2):
                    act.wait_ge(s_ssp, i - 1)
                sc.activation(what, flat(bank(k.ps_b, s)), ACT.Abs, bias=k.o1_bias[:, 0:1]).then_inc(s_soft, 1)
                act.wait_ge(s_soft, 2 * i + 1)
                sc.activation(what, what, ACT.Exp, scale=-1.0).then_inc(s_soft, 1)
                act.wait_ge(s_soft, 2 * i + 2)
                sc.activation(what, what, ACT.Ln, bias=1.0).then_inc(s_act, 1)

            def log_degree(i, s):
                act.wait_ge(s_degree, i + 1)
                if known(i, 2):
                    act.wait_ge(s_root, i - 1)
                sc.activation(lnd[:, s % 2, :], degree[:, s % 2, :], ACT.Ln).then_inc(s_lnd, 1)

            def root(i, s):
                act.wait_ge(s_lnd, i + 1)
                if known(i, 4):
                    act.wait_ge(s_out, i - 3)
                sc.activation(inv_root[:, s, :], lnd[:, s % 2, :], ACT.Exp, scale=-0.5).then_inc(s_root, 1)
            sc.preload_act_table_set("natural_log_exp_and_others")
            every_round(act, ((1, copy_sums), (2, root), (1, log_degree), (2, soften)))

        @block.tensor
        def _(pe):
            t = nc.tensor

            def turn(i, s):
                pe.wait_ge(s_agg[s], uses(i, s, 4))
                if known(i, 2):
                    pe.wait_ge(s_agg_t, i - 1)
                for j in range(T):
                    last = t.transpose(bank(k.ps_a, s)[:, j, :], agg[:, s, j, 0:D], k.ident[:, :])
                last.then_inc(s_turned, 1)

            def first(i, s):
                pe.wait_ge(s_agg_t, i + 1)
                if known(i, 2):
                    pe.wait_ge(s_act, i - 1)
                t.matmul(flat(bank(k.ps_b, s)), k.W["L1_gnn_W_o1"], flat(agg_t[:, s % 2, :, :]), start=True, stop=True).then_inc(s_first, 1)

            def second(i, s):
                pe.wait_ge(s_ssp, i + 1)
                if known(i, 2):
                    pe.wait_ge(s_out, i - 1)
                for j in range(T):
                    last = t.matmul(bank(k.ps_c, s)[:, j, :], ssp[:, s % 2, j, :], k.W["L1_gnn_W_o2"], start=True, stop=True)
                last.then_inc(s_second, 1)
            every_round(pe, ((4, second), (1, first), (0, turn)))


def plan_pass(k, a, sums):
    nc = k.nc
    s_cleared = k.sem("plan_cleared")
    s_load, s_set, s_rows, s_tp, s_col = (k.sem(f"plan_{x}") for x in ("load", "set", "rows", "tp", "col"))
    s_hot, s_hist, s_link, s_tot, s_first, s_place = (k.sem(f"plan_{x}") for x in ("hot", "hist", "link", "tot", "first", "place"))
    C = -(-BLOCKS // P)
    psa, psb = k.ps_a[:, :, :].rearrange("p a b -> p (a b)"), k.ps_b[:, :, :].rearrange("p a b -> p (a b)")
    halves = [(0, 512), (512, TILES)]
    names = ["dst", "src", "edge_weight"]
    sb = k.own
    raw = sb("key_rows", [P, C, P], I32)
    nxt = sb("next_rows", [P, C, P], I32)
    srow = sb("src_rows", [P, C, P], I32)
    arow, arow_f = sb("add_rows", [P, C, P], I32), sb("arow_f", [P, C, P])
    wrow = sb("weight_rows", [P, C, P])
    rows_f, srow_f, late = sb("rows_f", [P, C, P]), sb("srow_f", [P, C, P]), sb("late", [P, C, P])
    key_col = sb("key_col", [P, C * P], I32)
    hi_i, lo_i = sb("hi_i", [P, C * P], I32), sb("lo_i", [P, C * P], I32)
    hi, lo = sb("hi", [P, C * P]), sb("lo", [P, C * P])
    tile_i, tile_no = sb("tile_i", [P, TILES], I32), sb("tile_no", [P, TILES])
    tile_h, lane_h = sb("tile_h", [P, TILES], F16), sb("lane_h", [P, P], F16)
    hot_hi, hot_lo = sb("hot_hi", [P, 2, TILES], BF16), sb("hot_lo", [P, 2, P], BF16)
    start, b0i, b0, lasti, last = sb("start", [P, TILES + 1]), sb("b0i", [P, TILES], I32), sb("b0", [P, TILES]), sb("lasti", [P, TILES], I32), sb("last", [P, TILES])
    base_i, base, bad = sb("base_i", [P, TILES], I32), sb("base", [P, TILES]), sb("bad", [P, TILES])
    ones, total, junk = sb("ones", [P, P]), sb("total", [P, 4]), sb("plan_junk", [P, TILES])
    part_i, part = sb("part_i", [P, C], I32), sb("part", [P, C])
    at_block = sb("at_block", [P, C, B, TILES])
    slot_i = sb("slot_i", [P, TILES], I32)

    with nc.Block() as block:
        @block.sync
        def _(sp):
            sp.wait_ge(s_set, 5)
            full = FULL // P
            for tile, ap in ((raw, a["dst"]), (srow, a["src"]), (wrow, a["edge_weight"]), (arow, a["src"]), (nxt, a["dst"][1:E])):
                rest = ap.shape[0] - FULL * P
                sp.dma_start(tile[:, 0:full, :], ap[0:full * P * P].rearrange("(c b e) -> b c e", b=P, e=P)).then_inc(s_load, 16)
                sp.dma_start(tile[0:FULL - full * P, full, :], ap[full * P * P:FULL * P].rearrange("(b e) -> b e", e=P)).then_inc(s_load, 16)
                sp.dma_start(tile[FULL - full * P:FULL - full * P + 1, full, 0:rest],
                             ap[FULL * P:FULL * P + rest].rearrange("(o n) -> o n", o=1)).then_inc(s_load, 16)
            zero_rows(sp, k, sums, s_cleared)
            sp.wait_ge(s_cleared, 16 * (NG + 1))

        @block.gpsimd
        def _(pool):
            pool.memset(raw[:, :, :], -1).then_inc(s_set, 1)
            pool.memset(srow[:, :, :], 0).then_inc(s_set, 1)
            pool.memset(wrow[:, :, :], 0.0).then_inc(s_set, 1)
            pool.memset(nxt[:, :, :], N).then_inc(s_set, 1)
            pool.iota(arow[:, :, :], [[0, C], [1, P]], base=N, channel_multiplier=0).then_inc(s_set, 1)
            pool.memset(ones[:, :], 1.0)
            pool.iota(tile_i[:, :], [[1, TILES]], base=0, channel_multiplier=0).then_inc(s_rows, 1)
            pool.iota(k.lane_i[:, :], [[1, P]], base=0, channel_multiplier=0).then_inc(s_rows, 1)
            pool.iota(part_i[:, :], [[P, C]], base=0, channel_multiplier=1).then_inc(s_rows, 1)

        @block.vector
        def _(dve):
            v = nc.vector
            link = Chain(dve, s_link, None)
            dve.wait_ge(s_rows, 3)
            link(v.tensor_copy(tile_no[:, :], tile_i[:, :]))
            link(v.tensor_copy(tile_h[:, :], tile_no[:, :]))
            link(v.tensor_copy(k.lane[:, :], k.lane_i[:, :]))
            link(v.tensor_copy(lane_h[:, :], k.lane[:, :]))
            link(v.tensor_copy(part[:, :], part_i[:, :]))
            link(v.tensor_scalar(base_i[:, :], tile_i[:, :], 2, 1, ALU.logical_shift_right, ALU.logical_shift_left))
            link(v.tensor_copy(base[:, :], base_i[:, :]))
            dve.wait_ge(s_load, 16 * 15)
            link(v.tensor_copy(rows_f[:, :, :], raw[:, :, :]))
            link(v.tensor_copy(srow_f[:, :, :], srow[:, :, :]))
            link(v.tensor_copy(arow_f[:, :, :], arow[:, :, :]))
            link(v.tensor_copy(late[:, :, :], nxt[:, :, :]))
            v.tensor_tensor(late[:, :, :], late[:, :, :], rows_f[:, :, :], ALU.is_lt).then_inc(s_col, 1)
            dve.wait_ge(s_col, 1)
            link(v.tensor_reduce(total[:, 0:1], late[:, :, :].rearrange("p c e -> p (c e)"), op=ALU.add, axis=AX.X))
            for n, tile in enumerate((key_col, k.src_col, k.weight_col, k.add_col)):
                dve.wait_ge(s_tp, n + 1)
                v.tensor_copy(tile[:, :], psa[:, 0:C * P]).then_inc(s_col, 1)
                dve.wait_ge(s_col, n + 2)
            link(v.tensor_scalar(k.add_col[:, BLOCKS - 1:BLOCKS], k.spare[:, :], float(P), None, ALU.add))
            link(v.tensor_scalar(k.dst_col[:, :], key_col[:, :], 0, None, ALU.max))
            link(v.tensor_scalar(hi_i[:, :], key_col[:, :], 7, None, ALU.arith_shift_right))
            link(v.tensor_scalar(lo_i[:, :], key_col[:, :], P - 1, None, ALU.bitwise_and))
            link(v.tensor_copy(hi[:, :], hi_i[:, :]))
            link(v.tensor_copy(lo[:, :], lo_i[:, :]))

            def hot(b, s):
                v.tensor_scalar(hot_hi[:, s, :], tile_h[:, :], hi[:, bass.ds(b, 1)], None, ALU.is_equal)
                v.tensor_scalar(hot_lo[:, s, :], lane_h[:, :], lo[:, bass.ds(b, 1)], None, ALU.is_equal).then_inc(s_hot, 1)
            hot(0, 0)
            hot(1, 1)
            with dve.Fori(1, BLOCKS // 2) as u:
                for s in range(2):
                    dve.wait_ge(s_hist, 2 * u + s - 1)
                    hot(2 * u + s, s)
            dve.wait_ge(s_hist, BLOCKS)
            link(v.tensor_copy(k.degree[:, :], psb[:, 0:TILES]))
            link(v.tensor_scalar(k.count[:, :], k.degree[:, :], 1.0, None, ALU.max))
            v.reciprocal(k.inverse[:, :], k.count[:, :]).then_inc(s_tot, 1)
            dve.wait_ge(s_first, 1)
            link(v.memset(start[:, 0:1], 0.0))
            link(v.memset(junk[:, :], 0.0))
            link(v.tensor_tensor_scan(start[:, 1:TILES + 1], psa[:, 0:TILES], junk[:, :], 0.0, ALU.add, ALU.add))
            link(v.tensor_copy(b0i[:, :], start[:, 0:TILES]))
            link(v.tensor_scalar(b0i[:, :], b0i[:, :], 7, None, ALU.arith_shift_right))
            link(v.tensor_copy(b0[:, :], b0i[:, :]))
            link(v.tensor_scalar(last[:, :], start[:, 1:TILES + 1], -1.0, None, ALU.add))
            link(v.tensor_copy(lasti[:, :], last[:, :]))
            link(v.tensor_scalar(lasti[:, :], lasti[:, :], 7, None, ALU.arith_shift_right))
            link(v.tensor_copy(last[:, :], lasti[:, :]))
            link(v.tensor_tensor(last[:, :], last[:, :], b0[:, :], ALU.subtract))
            link(v.tensor_scalar(bad[:, :], last[:, :], 1.0, None, ALU.is_gt))
            link(v.tensor_reduce(total[:, 1:2], bad[:, :], op=ALU.add, axis=AX.X))
            link(v.tensor_tensor(last[:, :], b0[:, :], base[:, :], ALU.subtract))
            link(v.tensor_scalar(bad[:, :], last[:, :], float(-WINDOW), None, ALU.is_lt))
            link(v.tensor_reduce(total[:, 2:3], bad[:, :], op=ALU.add, axis=AX.X))
            link(v.tensor_scalar(bad[:, :], last[:, :], float(WINDOW - 2), None, ALU.is_gt))
            link(v.tensor_reduce(total[:, 3:4], bad[:, :], op=ALU.add, axis=AX.X))
            for q in range(B):
                link(v.tensor_scalar(last[:, :], b0[:, :], float(q), None, ALU.add))
                link(v.tensor_copy(slot_i[:, :], last[:, :]))
                link(v.tensor_scalar(slot_i[:, :], slot_i[:, :], RING - 1, 7, ALU.bitwise_and, ALU.logical_shift_left))
                link(v.tensor_copy(k.slots[:, :].rearrange("o (t q) -> o t q", q=B)[:, :, q], slot_i[0:1, :]))
            for c in range(C):
                for q in range(B):
                    link(v.tensor_scalar(at_block[:, c, q, :], b0[:, :], part[:, c:c + 1], float(q), ALU.subtract, ALU.add))
                    link(v.tensor_scalar(at_block[:, c, q, :], at_block[:, c, q, :], 0.0, None, ALU.is_equal))
            link(v.tensor_scalar(base[:, :], tile_no[:, :], float(P), None, ALU.mult))
            v.memset(junk[:, 0:1], 0.0).then_inc(s_tot, 1)
            for q, ps in enumerate((psa, psb)):
                dve.wait_ge(s_place, q + 1)
                link(v.tensor_tensor(k.place[:, :].rearrange("p (t q) -> p t q", q=B)[:, :, q], ps[:, 0:TILES], base[:, :], ALU.subtract))
            dve.wait_ge(s_place, 3)
            link(v.tensor_reduce(total[:, 0:1], k.ps_c[:, 0, 0:4], op=ALU.add, axis=AX.X))
            link(v.tensor_scalar(total[:, 0:1], total[:, 0:1], 0.0, None, ALU.is_gt))
            link(v.tensor_copy(k.paths[:, 1:2], total[0:1, 0:1]))
            link(v.tensor_scalar(total[:, 0:1], total[:, 0:1], -1.0, 1.0, ALU.mult, ALU.add))
            link(v.tensor_copy(k.paths[:, 0:1], total[0:1, 0:1]))

        @block.tensor
        def _(pe):
            t = nc.tensor
            pe.wait_ge(s_set, 4)
            for n, tile in enumerate((rows_f, srow_f, wrow, arow_f)):
                pe.wait_ge(s_col, n + 1)
                for c in range(C):
                    turned = t.transpose(psa[:, c * P:(c + 1) * P], tile[:, c, :], k.ident[:, :])
                turned.then_inc(s_tp, 1)

            def count(b, s, start=False, stop=False):
                pe.wait_ge(s_hot, b + 1)
                for m, n in halves:
                    counted = t.matmul(psb[:, m:n], hot_lo[:, s, :], hot_hi[:, s, m:n], start=start, stop=stop)
                counted.then_inc(s_hist, 1)
            count(0, 0, True)
            count(1, 1)
            with pe.Fori(1, BLOCKS // 2 - 1) as u:
                for s in range(2):
                    count(2 * u + s, s)
            count(BLOCKS - 2, 0)
            count(BLOCKS - 1, 1, stop=True)
            pe.wait_ge(s_tot, 1)
            for m, n in halves:
                summed = t.matmul(psa[:, m:n], ones[:, :], k.degree[:, m:n], start=True, stop=True)
            summed.then_inc(s_first, 1)
            pe.wait_ge(s_tot, 2)
            for q, ps in enumerate((psa, psb)):
                for m, n in halves:
                    for c in range(C):
                        placed = t.matmul(ps[:, m:n], rows_f[:, c, :], at_block[:, c, q, m:n], start=(c == 0), stop=(c == C - 1))
                placed.then_inc(s_place, 1)
            t.matmul(k.ps_c[:, 0, 0:4], ones[:, :], total[:, :], start=True, stop=True).then_inc(s_place, 1)


def sorted_pass(k, a, name, kind, table, out):
    nc = k.nc
    sorted_buffers(k)
    ring_w = B * D
    sum_lag = {"first": 4, "mid": 4, "linear": 2, "last": 3}[kind]
    norm_edges, norm_nodes, weighted = kind != "mid", kind in ("first", "last"), kind == "linear"
    two_products, edge_product = kind in ("first", "mid"), kind != "last"
    residual = {"mid": a["x"], "last": table}.get(kind)
    in_w, out_w = table.shape[1], out.shape[1]
    s_x = [k.sem(f"{name}_x{s}") for s in range(4)]
    s_res = [k.sem(f"{name}_res{s}") for s in range(4)]
    s_got = [k.lasting_sem(f"{name}_got{s}") for s in range(4)]
    s_stored = [k.sem(f"{name}_stored{s}") for s in range(4)]
    (s_stage, s_numbers, s_elink, s_evar, s_estd, s_escale, s_relu, s_eturned, s_plain_t, s_eproduct, s_edges,
     s_nlink, s_nvar, s_nstd, s_nscale, s_h, s_select, s_turned, s_h_t, s_product, s_pre, s_out, s_elink2, s_nlink2) = (
        k.sem(f"{name}_{x}") for x in (
            "stage", "numbers", "edge_link", "edge_var", "edge_std", "edge_scale", "relu", "edge_turned", "plain_t",
            "edge_product", "edges", "node_link", "node_var", "node_std", "node_scale", "h", "select", "turned", "h_t",
            "product", "pre", "out", "edge_link2", "node_link2"))
    weight = {"first": "L0_gnn_W_conv0", "mid": "L0_gnn_W_conv1", "linear": "L2_gnn_W", "last": None}[kind]
    own_weight = {"first": "L0_gnn_W_lin0", "mid": "L0_gnn_W_lin1"}.get(kind)
    bias = {"first": k.B["L0_0"], "mid": k.B["L0_1"], "linear": k.B["L2_gnn_b"], "last": None}[kind]
    rest = N - (STEPS - 1) * T * P

    def bank(ps, s):
        return ps[:, T * (s % 2):T * (s % 2) + T, :]

    def in_ring(e, q, n):
        return bass.ds(e % (RING // B) * ring_w + q * D, n * D)

    def uses(i, s, slots, n):
        return (i - s % slots) * (16 * n // slots) + 16 * n

    def uses_last(i, s):
        return uses(i, s, 4, 1) + (16 if isinstance(i, int) and i == STEPS - 1 else 0)

    def known(i, least):
        return not isinstance(i, int) or i >= least

    def live(e):
        return not isinstance(e, int) or 0 <= e < STEPS

    EDGES, NODES = 0, AHEAD

    def every_round(eng, stages):
        def one(r, s):
            for n, stage, behind in stages:
                if live(r - behind - n):
                    stage(r - behind - n, (s - n) % 4)
        for r in range(20):
            one(r, r % 4)
        with eng.Fori(5, STEPS // 4) as u:
            for s in range(4):
                one(4 * u + s, s)
        for r in range(STEPS, STEPS + AHEAD + 8):
            one(r, r % 4)

    with nc.Block() as block:
        @block.sync
        @k.only("sorted")
        def _(sp):
            def move(tile, s, rows, i, sem, width, store=False):
                if isinstance(i, int) and i == STEPS - 1:
                    lo = i * T * P
                    parts = [(tile[:, s, 0, 0:width], rows[lo:lo + P, 0:width]), (tile[0:rest - P, s, 1, 0:width], rows[lo + P:N, 0:width])]
                else:
                    parts = [(tile[:, s, :, 0:width], rows[bass.ds(i * T * P, T * P), 0:width].rearrange("(t p) w -> p t w", p=P))]
                for on_chip, dram in parts:
                    sp.dma_start(*((dram, on_chip) if store else (on_chip, dram))).then_inc(sem, 16)

            def load_x(i, s):
                if known(i, 4):
                    sp.wait_ge(s_out if kind == "linear" else s_h, i - 3)
                move(k.x, s, table, i, s_x[s], in_w)

            def load_residual(i, s):
                if known(i, 4):
                    sp.wait_ge(s_out, i - 3)
                move(k.res4, s, residual, i, s_res[s], residual.shape[1])

            def store(i, s):
                sp.wait_ge(s_out, i + 1)
                move(k.y, s, out, i, s_stored[s], out_w, store=True)

            stages = [(sum_lag + 2, store, NODES), (0 if kind == "linear" else -3, load_x, NODES)]
            if residual is not None:
                stages.append((1, load_residual, NODES))
            every_round(sp, stages)
            for s in range(4):
                sp.wait_ge(s_stored[s], uses((STEPS - 4) + s, s, 4, 1) + 16 * (s == 3))

        @block.gpsimd
        @k.only("sorted")
        def _(pool):
            pool.nop().then_inc(s_stage, 4)

            def gather(e, s):
                take(pool, s_stage, 1)
                pool.tensor_copy(k.numbers[:, s, :], k.src_col[:, bass.ds(e * B, B)]).then_inc(s_numbers, 1)
                take(pool, s_numbers, 1)
                for q in range(B):
                    pool.indirect_dma_start(out=k.stage[:, s, q, 0:in_w], out_offset=None, in_=table,
                                            in_offset=bass.IndirectOffsetOnAxis(ap=k.numbers[:, s, q:q + 1], axis=0)).then_inc(s_got[s], 16)
            with pool.Fori(0, STEPS // 4) as u:
                for s in range(4):
                    gather(4 * u + s, s)

        @block.vector
        @k.only("sorted")
        def _(dve):
            v = nc.vector
            edge_links = 1 + (kind == "last")

            def spread(sem, i, n, stats, mv, done, column):
                dve.wait_ge(sem, n * i + n)
                v.tensor_tensor(k.idle[:, column:column + 1], k.lane[:, 0:1], k.lane[:, 0:1], ALU.add)
                for j in range(n):
                    aggregated = v.bn_aggr(mv[:, j, :], stats[:, j, :])
                aggregated.then_inc(done, 1)

            def edge_stats(e, s):
                dve.wait_ge(s_got[s], uses(e, s, 4, B))
                v.tensor_tensor(k.idle[:, 0:1], k.lane[:, 0:1], k.lane[:, 0:1], ALU.add)
                for q in range(B):
                    v.bn_stats(k.estats[:, s % 2, q, :], k.stage[:, s, q, 0:D]).then_inc(s_elink, 1)

            def edge_spread(e, s):
                spread(s_elink, e, B, k.estats[:, s % 2, :, :], k.emv[:, s % 2, :, :], s_evar, 1)

            def edge_inverse(e, s):
                dve.wait_ge(s_estd, e + 1)
                v.reciprocal(k.erstd[:, s % 2, :], k.estd[:, s % 2, :]).then_inc(s_elink2, 1)

            def edge_factor(e, s):
                o = s % 2
                dve.wait_ge(s_elink2, edge_links * e + 1)
                v.tensor_tensor(k.erstd[:, o, :], k.erstd[:, o, :], k.stage[:, s, :, AUX], ALU.mult).then_inc(s_elink2, 1)

            def edge_offset(e, s):
                o = s % 2
                dve.wait_ge(s_elink2, edge_links * e + edge_links)
                v.scalar_tensor_tensor(k.eshift[:, o, :], k.emv[:, o, :, 0], -1.0, k.erstd[:, o, :], ALU.mult, ALU.mult).then_inc(s_escale, 1)

            def select(i, s):
                if known(i, 4):
                    dve.wait_ge(s_product, i - 3)
                v.tensor_tensor(k.select[:, s, :, :], k.lane[:, :].unsqueeze(1).to_broadcast([P, T * B, P]),
                                k.place[:, bass.ds(i * T * B, T * B)].unsqueeze(2).to_broadcast([P, T * B, P]),
                                ALU.is_equal).then_inc(s_select, 1)

            def node_stats(i, s):
                dve.wait_ge(s_x[s], uses_last(i, s))
                v.tensor_tensor(k.idle[:, 2:3], k.lane[:, 0:1], k.lane[:, 0:1], ALU.add)
                for j in range(T):
                    v.bn_stats(k.nstats[:, s % 2, j, :], k.x[:, s, j, 0:D]).then_inc(s_nlink, 1)

            def node_spread(i, s):
                spread(s_nlink, i, T, k.nstats[:, s % 2, :, :], k.nmv[:, s % 2, :, :], s_nvar, 3)

            def node_inverse(i, s):
                dve.wait_ge(s_nstd, i + 1)
                v.reciprocal(k.nrstd[:, s % 2, :], k.nstd[:, s % 2, :]).then_inc(s_nlink2, 1)

            def node_factor(i, s):
                o = s % 2
                dve.wait_ge(s_nlink2, 2 * i + 1)
                factor = k.x[:, s, :, AUX] if kind == "last" else k.count[:, bass.ds(i * T, T)]
                v.tensor_tensor(k.nrstd[:, o, :], k.nrstd[:, o, :], factor, ALU.mult).then_inc(s_nlink2, 1)

            def node_offset(i, s):
                o = s % 2
                dve.wait_ge(s_nlink2, 2 * i + 2)
                v.scalar_tensor_tensor(k.nshift[:, o, :], k.nmv[:, o, :, 0], -1.0, k.nrstd[:, o, :], ALU.mult, ALU.mult).then_inc(s_nscale, 1)

            def finish(i, s):
                y, rows = k.y[:, s, :, :], bank(k.ps_c, s)
                dve.wait_ge(s_product, i + 1)
                if known(i, 4):
                    dve.wait_ge(s_stored[s], uses(i - 4, s, 4, 1))
                if two_products:
                    for j in range(T):
                        pre = v.scalar_tensor_tensor(y[:, j, 0:D], rows[:, j, :], k.inverse[:, bass.ds(i * T + j, 1)], bias, ALU.mult, ALU.add)
                    pre.then_inc(s_pre, 1)
                if residual is not None:
                    dve.wait_ge(s_res[s], uses_last(i, s))
                if kind == "mid":
                    dve.wait_ge(s_pre, i + 1)
                    v.tensor_tensor(y[:, :, 0:D], y[:, :, 0:D], k.res4[:, s, :, 0:D], ALU.add).then_inc(s_out, 1)
                if kind == "linear":
                    dve.wait_ge(s_x[s], uses_last(i, s))
                    v.tensor_copy(y[:, :, D:W], k.x[:, s, :, D:W])
                    v.tensor_tensor(y[:, :, 0:D], rows, bias.unsqueeze(1).to_broadcast([P, T, D]), ALU.add).then_inc(s_pre, 1)
                    dve.wait_ge(s_pre, i + 1)
                    v.tensor_tensor(y[:, :, 0:D], y[:, :, 0:D], k.x[:, s, :, 0:D], ALU.add).then_inc(s_out, 1)
                if kind == "last":
                    for j in range(T):
                        done = v.scalar_tensor_tensor(y[:, j, 0:D], rows[:, j, :], k.res4[:, s, j, AUX:AUX + 1], k.res4[:, s, j, 0:D], ALU.mult, ALU.add)
                    done.then_inc(s_out, 1)

            stages = [(1, node_inverse, NODES), (1, edge_inverse, EDGES), (0, edge_stats, EDGES), (1, node_factor, NODES)]
            stages += [(1, edge_factor, EDGES)] * (kind == "last") + [(0, node_stats, NODES), (1, node_offset, NODES)]
            stages += [(1, edge_offset, EDGES), (0, edge_spread, EDGES), (0, node_spread, NODES)]
            stages = [x for x in stages if (norm_nodes if x[2] == NODES else norm_edges)]
            every_round(dve, stages + [(sum_lag - 1, select, NODES), (sum_lag + 1, finish, NODES)])

        @block.scalar
        @k.only("sorted")
        def _(act):
            sc = nc.scalar

            def edge_root(e, s):
                act.wait_ge(s_evar, e + 1)
                sc.activation(k.estd[:, s % 2, :], k.emv[:, s % 2, :, 1], ACT.Sqrt, bias=k.eps[:, 0:1]).then_inc(s_estd, 1)

            def edge_relu(e, s):
                o = s % 2
                act.wait_ge(s_escale, e + 1)
                if edge_product and known(e, 2):
                    act.wait_ge(s_eturned, e - 1)
                for q in range(B):
                    message = k.plain[:, o, q, :] if edge_product else k.ring[:, in_ring(e, q, 1)]
                    made = sc.activation(message, k.stage[:, s, q, 0:D], ACT.Relu, bias=k.eshift[:, o, q:q + 1], scale=k.erstd[:, o, q:q + 1])
                made.then_inc(s_relu if edge_product else s_edges, 1)
                sc.activation(k.idle3[:, :], k.eps[:, :], ACT.Copy).then_inc(s_stage, 1)

            def edge_turned(e, s):
                o = s % 2
                act.wait_ge(s_eturned, e + 1)
                if not norm_edges:
                    act.nop().then_inc(s_stage, 1)
                if known(e, 2):
                    act.wait_ge(s_eproduct, e - 1)
                sc.activation(k.plain_t[:, o, :, :], bank(k.ps_b, o)[:, 0:B, :], ACT.Copy).then_inc(s_plain_t, 1)

            def into_ring(e, s):
                o = s % 2
                act.wait_ge(s_eproduct, e + 1)
                if weighted:
                    for q in range(B):
                        made = sc.activation(k.ring[:, in_ring(e, q, 1)], k.ps_sum[:, o, q * D:(q + 1) * D], ACT.Copy,
                                             scale=k.weight_col[:, bass.ds(e * B + q, 1)])
                else:
                    made = sc.activation(k.ring[:, in_ring(e, 0, B)], k.ps_sum[:, o, 0:B * D], ACT.Copy)
                made.then_inc(s_edges, 1)

            def node_root(i, s):
                act.wait_ge(s_nvar, i + 1)
                sc.activation(k.nstd[:, s % 2, :], k.nmv[:, s % 2, :, 1], ACT.Sqrt, bias=k.eps[:, 0:1]).then_inc(s_nstd, 1)

            def node_rows(i, s):
                o = s % 2
                if norm_nodes:
                    act.wait_ge(s_nscale, i + 1)
                else:
                    act.wait_ge(s_x[s], uses_last(i, s))
                if known(i, 4):
                    act.wait_ge(s_turned if two_products else s_product, i - 3)
                for j in range(T):
                    if norm_nodes:
                        made = sc.activation(k.h[:, s, j, :], k.x[:, s, j, 0:D], ACT.Relu, bias=k.nshift[:, o, j:j + 1], scale=k.nrstd[:, o, j:j + 1])
                    else:
                        made = sc.activation(k.h[:, s, j, :], k.x[:, s, j, 0:D], ACT.Copy, scale=k.count[:, bass.ds(i * T + j, 1)])
                made.then_inc(s_h, 1)

            def node_turned(i, s):
                act.wait_ge(s_turned, i + 1)
                if known(i, 2):
                    act.wait_ge(s_product, i - 1)
                sc.activation(k.h_t2[:, s % 2, :, :], bank(k.ps_a, s), ACT.Copy).then_inc(s_h_t, 1)

            def rectify(i, s):
                y = k.y[:, s, :, 0:D]
                act.wait_ge(s_pre, i + 1)
                sc.activation(y, y, ACT.Relu).then_inc(s_out, 1)

            stages = [(3, node_turned, NODES)] * two_products + [(1, node_rows, NODES)] * (kind != "linear")
            stages += [(1, edge_relu, EDGES)] * norm_edges + [(5, into_ring, EDGES), (3, edge_turned, EDGES)] * edge_product
            stages += [(6, rectify, NODES)] * (kind == "first") + [(0, edge_root, EDGES)] * norm_edges + [(0, node_root, NODES)] * norm_nodes
            every_round(act, stages)

        @block.tensor
        @k.only("sorted")
        def _(pe):
            t = nc.tensor

            def edge_turn(e, s):
                o = s % 2
                if norm_edges:
                    pe.wait_ge(s_relu, e + 1)
                else:
                    pe.wait_ge(s_got[s], uses(e, s, 4, B))
                if known(e, 2):
                    pe.wait_ge(s_plain_t, e - 1)
                for q in range(B):
                    rows = k.plain[:, o, q, :] if norm_edges else k.stage[:, s, q, 0:D]
                    last = t.transpose(bank(k.ps_b, o)[:, q, :], rows, k.ident[:, :])
                last.then_inc(s_eturned, 1)

            def edge_weigh(e, s):
                o = s % 2
                pe.wait_ge(s_plain_t, e + 1)
                if known(e, 2):
                    pe.wait_ge(s_edges, e - 1)
                for q in range(B):
                    last = t.matmul(k.ps_sum[:, o, q * D:(q + 1) * D], k.plain_t[:, o, q, :], k.W[weight], start=True, stop=True)
                last.then_inc(s_eproduct, 1)

            def node_turn(i, s):
                pe.wait_ge(s_h, i + 1)
                if known(i, 2):
                    pe.wait_ge(s_h_t, i - 1)
                for j in range(T):
                    last = t.transpose(bank(k.ps_a, s)[:, j, :], k.h[:, s, j, :], k.ident[:, :])
                last.then_inc(s_turned, 1)

            def sums(i, s):
                where, o = bank(k.ps_c, s), s % 2
                _, places = nc.values_load_multi_w_load_instructions(
                    k.slots[0:1, bass.ds(i * T * B, T * B)], engines=[mybir.EngineType.PE], min_val=0,
                    max_val=(RING - 1) * D, skip_runtime_bounds_check_because="a remainder by the ring's size, times a row")
                if known(i, 2):
                    pe.wait_ge(s_pre if kind == "first" else s_out, i - 1)
                if kind == "last":
                    pe.wait_ge(s_h, i + 1)
                    t.matmul(where, k.ident[:, :], k.h[:, s, :, :], start=True, stop=False, skip_group_check=True)
                if two_products:
                    pe.wait_ge(s_h_t, i + 1)
                pe.wait_ge(s_select, i + 1)
                pe.wait_ge(s_edges, i + LEAD if not isinstance(i, int) else min(i + LEAD, STEPS))
                for j in range(T):
                    if two_products:
                        t.matmul(where[:, j, :], k.h_t2[:, o, j, :], k.W[own_weight], start=True, stop=False)
                    for q in range(B):
                        last = t.matmul(where[:, j, :], k.select[:, s, j * B + q, :], k.ring[:, bass.ds(places[j * B + q], D)],
                                        start=(kind == "linear" and q == 0),
                                        stop=(q == B - 1 and (kind != "last" or j == T - 1)), skip_group_check=kind == "last")
                last.then_inc(s_product, 1)

            stages = [(sum_lag, sums, NODES)] + [(2, node_turn, NODES)] * two_products
            every_round(pe, stages + [(4, edge_weigh, EDGES), (2, edge_turn, EDGES)] * edge_product)


def build(nc, **a):
    with ExitStack() as ctx:
        k = Kernel(nc, ctx)
        tables = [nc.dram_tensor(f"table{n}", [N, w], FP32, kind="Internal").ap() for n, w in enumerate((D, D, W, W))]
        sums = [nc.dram_tensor(f"sums{n}", [N + SPARES, W], FP32, kind="Internal").ap() for n in range(5)]
        k.ps_a, k.ps_b, k.ps_c = (k.ps(f"ps_{c}", [P, 8, P]) for c in "abc")
        k.ps_sum = k.ps("ps_sum", [P, 2, 512])
        x = a["x"]
        k.src_col, k.weight_col = k.sb("src_col", [P, 4 * P], I32), k.sb("weight_col", [P, 4 * P])
        k.dst_col, k.add_col = k.sb("dst_col", [P, 4 * P], I32), k.sb("add_col", [P, 4 * P])
        k.lane_i, k.lane = k.sb("lane_i", [P, P], I32), k.sb("lane", [P, P])
        k.degree, k.count, k.inverse = (k.sb(x, [P, TILES]) for x in ("degree", "count", "inverse"))
        k.slots, k.place = k.sb("slots", [1, TILES * B], I32), k.sb("place", [P, TILES * B])
        k.paths = k.sb("paths", [1, 2], I32)
        with k.one_pass():
            load_constants(k, a)
        with k.one_pass():
            plan_pass(k, a, sums[2])
        with k.one_pass():
            clear_tables(k, sums[:2] + sums[3:])
        with k.one_pass():
            sorted_pass(k, a, "t0", "first", x, tables[0])
        with k.one_pass():
            sorted_pass(k, a, "t1", "mid", tables[0], tables[1])
        with k.one_pass():
            edge_pass(k, a, "e0", "h", x, sums[0], "src", "dst")
        with k.one_pass():
            node_pass(k, a, "n0", "first", x, tables[0], sums[0])
        with k.one_pass():
            edge_pass(k, a, "e1", "plain", tables[0], sums[1], "src", "dst")
        with k.one_pass():
            node_pass(k, a, "n1", "mid", tables[0], tables[1], sums[1], x)
        with k.one_pass():
            filter_edges(k, a, "e2", tables[1], sums[2])
        with k.one_pass():
            filter_nodes(k, a, "n2", tables[1], sums[2], tables[2])
        with k.one_pass():
            sorted_pass(k, a, "t3", "linear", tables[2], tables[3])
        with k.one_pass():
            sorted_pass(k, a, "t4", "last", tables[3], a["out"])
        with k.one_pass():
            edge_pass(k, a, "e3", "weight", tables[2], sums[3], "src", "dst")
        with k.one_pass():
            node_pass(k, a, "n3", "linear", tables[2], tables[3], sums[3])
        with k.one_pass():
            edge_pass(k, a, "e4", "degree", tables[3], sums[4], "src", "dst")
        with k.one_pass():
            node_pass(k, a, "n4", "last", tables[3], a["out"], sums[4])


INPUTS = ["x", "src", "dst", "edge_attr_20", "edge_weight",
          "L0_gnn_W_conv0", "L0_gnn_b_conv0", "L0_gnn_W_lin0", "L0_gnn_b_lin0",
          "L0_gnn_W_conv1", "L0_gnn_b_conv1", "L0_gnn_W_lin1", "L0_gnn_b_lin1",
          "L1_gnn_W_in2f", "L1_gnn_b_in2f", "L1_gnn_W_f1", "L1_gnn_b_f1", "L1_gnn_W_f2", "L1_gnn_b_f2",
          "L1_gnn_W_o1", "L1_gnn_b_o1", "L1_gnn_W_o2", "L1_gnn_b_o2", "L2_gnn_W", "L2_gnn_b"]


def kernel(**inputs):
    import concourse.bacc as bacc
    from concourse.bass_utils import run_bass_kernel_spmd

    nc = bacc.Bacc("TRN2", target_bir_lowering=False, num_devices=1)
    arrays, aps = {}, {}
    for name in INPUTS:
        arrays[name] = np.ascontiguousarray(inputs[name])
        aps[name] = nc.dram_tensor(name, arrays[name].shape, mybir.dt.from_np(arrays[name].dtype),
                                   kind="ExternalInput").ap()
    aps["out"] = nc.dram_tensor("out", [N, D], FP32, kind="ExternalOutput").ap()
    build(nc, **aps)
    return run_bass_kernel_spmd(nc, [arrays], core_ids=[0]).results[0]["out"]
```
